# Optimizing a Trainium2 kernel written in Bass

```python
import numpy as np
import jax
import jax.numpy as jnp

def _softmax(x, axis=-1):
    return jax.nn.softmax(x, axis=axis)

def _gelu(x):
    return jax.nn.gelu(x, approximate=True)

def _silu(x):
    return jax.nn.silu(x)

def _sigmoid(x):
    return jax.nn.sigmoid(x)

def _layernorm(x, axis=-1, eps=1e-05):
    m = jnp.mean(x, axis=axis, keepdims=True)
    v = jnp.var(x, axis=axis, keepdims=True)
    return (x - m) / jnp.sqrt(v + eps)

def _scatter_add(tgt, idx, src, axis=0):
    return tgt.at[idx].add(src)

def _segment_sum(src, seg, n):
    return jax.ops.segment_sum(src, seg, n)
kernel_name = 'mk_xattn_ffn_d1_seqx_r4_12dc73'

def setup_inputs(seed: int=0):
    np.random.seed(seed)
    _w = jnp.asarray

    def _rec_inputs():
        import jax
        import jax.numpy as jnp
        _rk = jax.random.key(seed)
        x = 7.22e-05 + 1 * jax.random.normal(jax.random.fold_in(_rk, 1), (32, 128, 256), jnp.float32)
        _lenS = 128 - jax.random.randint(jax.random.fold_in(_rk, 7), (32,), 0, max(1, 128 // 4) + 1, jnp.int32)
        _lenS2 = 128 - jax.random.randint(jax.random.fold_in(_rk, 8), (32,), 0, max(1, 128 // 4) + 1, jnp.int32)
        _ctx_768P = jax.random.normal(jax.random.fold_in(_rk, 11), (32, 16, 192), jnp.float32)
        _ctx_768c = jax.random.dirichlet(jax.random.fold_in(_rk, 511), 0.3 * jnp.ones((16,), jnp.float32), (32, 128))
        _ctx_768t = jnp.einsum('bsk,bkd->bsd', _ctx_768c, _ctx_768P)
        _ctx_768t = _ctx_768t * jax.lax.rsqrt(jnp.mean(jnp.square(_ctx_768t)) + 1e-12) * 0.953939
        ctx_768 = 2.09791e-05 + 1.00001 * (_ctx_768t + 0.3 * jax.random.normal(jax.random.fold_in(_rk, 611), (32, 128, 192), jnp.float32))
        return (x, ctx_768)
    x, ctx_768 = _rec_inputs()

    def _L0_xattn_setup():
        import jax, jax.numpy as jnp
        import numpy as np
        HEADS = 16
        DIM_HEAD = 64
        key = jax.random.key(seed)
        ks = jax.random.split(key, 7)
        B, Nq, Dq = (4, 512, 256)
        Nk, Dc = (256, 192)
        inner = HEADS * DIM_HEAD
        sq = 1.0 / np.sqrt(Dq)
        sc = 1.0 / np.sqrt(Dc)
        si = 1.0 / np.sqrt(inner)
        return {'x': jax.random.normal(ks[0], (B, Nq, Dq), dtype=jnp.float32), 'context': jax.random.normal(ks[1], (B, Nk, Dc), dtype=jnp.float32), 'Wq': jax.random.normal(ks[2], (Dq, inner), dtype=jnp.float32) * sq, 'Wk': jax.random.normal(ks[3], (Dc, inner), dtype=jnp.float32) * sc, 'Wv': jax.random.normal(ks[4], (Dc, inner), dtype=jnp.float32) * sc, 'Wo': jax.random.normal(ks[5], (inner, Dq), dtype=jnp.float32) * si, 'bo': jax.random.normal(ks[6], (Dq,), dtype=jnp.float32) * 0.01}
    _L0_xattn_all = _L0_xattn_setup()
    _L0_xattn_in = {k: v for k, v in _L0_xattn_all.items() if k in ('Wq', 'Wk', 'Wv', 'Wo', 'bo')}
    del _L0_xattn_all

    def _L0_ffn_setup():
        import jax, jax.numpy as jnp
        import numpy as np
        D = 256
        H = 1024
        E = 8
        B = 2
        T = 512
        LN_EPS = 1e-05

        def _layer_norm(r, gamma, beta):
            mu = jnp.mean(r, axis=-1, keepdims=True)
            var = jnp.mean(jnp.square(r - mu), axis=-1, keepdims=True)
            return (r - mu) * jax.lax.rsqrt(var + LN_EPS) * gamma + beta
        key = jax.random.key(seed)
        ks = jax.random.split(key, 9)
        s_in = 1.0 / np.sqrt(D)
        s_hid = 1.0 / np.sqrt(H)
        x = jax.random.normal(ks[0], (B, T, D), dtype=jnp.float32)
        Wg = jax.random.uniform(ks[1], (D, E), jnp.float32, -s_in, s_in)
        bg = jax.random.uniform(ks[2], (E,), jnp.float32, -s_in, s_in)
        W1 = jax.random.uniform(ks[3], (E, D, H), jnp.float32, -s_in, s_in)
        b1 = jax.random.uniform(ks[4], (E, H), jnp.float32, -s_in, s_in)
        W2 = jax.random.uniform(ks[5], (E, H, D), jnp.float32, -s_hid, s_hid)
        b2 = jax.random.uniform(ks[6], (E, D), jnp.float32, -s_hid, s_hid)
        gamma = jnp.ones((D,), jnp.float32)
        beta = jnp.zeros((D,), jnp.float32)
        return {'x': x, 'Wg': Wg, 'bg': bg, 'W1': W1, 'b1': b1, 'W2': W2, 'b2': b2, 'gamma': gamma, 'beta': beta}
    _L0_ffn_all = _L0_ffn_setup()
    _L0_ffn_in = {k: v for k, v in _L0_ffn_all.items() if k in ('Wg', 'bg', 'W1', 'b1', 'W2', 'b2', 'gamma', 'beta')}
    del _L0_ffn_all
    return {'x': x, 'ctx_768': ctx_768, 'L0_xattn_Wq': _L0_xattn_in['Wq'], 'L0_xattn_Wk': _L0_xattn_in['Wk'], 'L0_xattn_Wv': _L0_xattn_in['Wv'], 'L0_xattn_Wo': _L0_xattn_in['Wo'], 'L0_xattn_bo': _L0_xattn_in['bo'], 'L0_ffn_Wg': _L0_ffn_in['Wg'], 'L0_ffn_bg': _L0_ffn_in['bg'], 'L0_ffn_W1': _L0_ffn_in['W1'], 'L0_ffn_b1': _L0_ffn_in['b1'], 'L0_ffn_W2': _L0_ffn_in['W2'], 'L0_ffn_b2': _L0_ffn_in['b2'], 'L0_ffn_gamma': _L0_ffn_in['gamma'], 'L0_ffn_beta': _L0_ffn_in['beta']}

def reference(x, ctx_768, L0_xattn_Wq, L0_xattn_Wk, L0_xattn_Wv, L0_xattn_Wo, L0_xattn_bo, L0_ffn_Wg, L0_ffn_bg, L0_ffn_W1, L0_ffn_b1, L0_ffn_W2, L0_ffn_b2, L0_ffn_gamma, L0_ffn_beta):
    import jax
    import jax.numpy as jnp

    def _L0_xattn_ref(x, context, Wq, Wk, Wv, Wo, bo):
        import jax, jax.numpy as jnp
        import numpy as np
        HEADS = 16
        DIM_HEAD = 64
        B, Nq, _ = x.shape
        Nk = context.shape[1]
        h, dh = (HEADS, DIM_HEAD)
        q = (x @ Wq).reshape(B, Nq, h, dh)
        k = (context @ Wk).reshape(B, Nk, h, dh)
        v = (context @ Wv).reshape(B, Nk, h, dh)
        scale = 1.0 / jnp.sqrt(jnp.asarray(dh, dtype=x.dtype))
        scores = jnp.einsum('bqhd,bkhd->bhqk', q, k) * scale
        attn = jax.nn.softmax(scores, axis=-1)
        out = jnp.einsum('bhqk,bkhd->bqhd', attn, v).reshape(B, Nq, h * dh)
        return out @ Wo + bo

    def _L0_ffn_ref(x, Wg, bg, W1, b1, W2, b2, gamma, beta):
        import jax, jax.numpy as jnp
        import numpy as np
        D = 256
        H = 1024
        E = 8
        B = 2
        T = 512
        LN_EPS = 1e-05

        def _layer_norm(r, gamma, beta):
            mu = jnp.mean(r, axis=-1, keepdims=True)
            var = jnp.mean(jnp.square(r - mu), axis=-1, keepdims=True)
            return (r - mu) * jax.lax.rsqrt(var + LN_EPS) * gamma + beta
        logits = jnp.einsum('btd,de->bte', x, Wg) + bg
        top2_vals, top2_idx = jax.lax.top_k(logits, 2)
        scores = jax.nn.softmax(top2_vals, axis=-1)
        onehot = jax.nn.one_hot(top2_idx, E, dtype=x.dtype)
        combine = jnp.einsum('btk,btke->bte', scores, onehot)
        h = jnp.einsum('btd,edh->bteh', x, W1) + b1[None, None]
        h = jax.nn.gelu(h, approximate=False)
        y = jnp.einsum('bteh,ehd->bted', h, W2) + b2[None, None]
        out = jnp.einsum('bted,bte->btd', y, combine)
        return _layer_norm(x + out, gamma, beta)
    x = x + _L0_xattn_ref(_layernorm(x, axis=-1), ctx_768, L0_xattn_Wq, L0_xattn_Wk, L0_xattn_Wv, L0_xattn_Wo, L0_xattn_bo)
    x = x + _L0_ffn_ref(_layernorm(x, axis=-1), L0_ffn_Wg, L0_ffn_bg, L0_ffn_W1, L0_ffn_b1, L0_ffn_W2, L0_ffn_b2, L0_ffn_gamma, L0_ffn_beta)
    return x

_drawn_inputs = setup_inputs


def setup_inputs(seed=0):
    import zlib

    import numpy as np

    out = dict(_drawn_inputs(seed))
    spreads = {'L0_ffn_gamma': (1.0, 0.2), 'L0_ffn_beta': (0.0, 0.1)}
    factors = {'L0_xattn_bo': 5.381, 'L0_ffn_bg': 4.153, 'L0_ffn_b1': 8.0, 'L0_ffn_b2': 8.0}
    for name, (base, spread) in spreads.items():
        noise = np.random.default_rng([zlib.crc32(name.encode()), seed]).standard_normal(out[name].shape)
        drawn = base * np.exp(spread * noise) if base else spread * noise
        out[name] = jnp.asarray(drawn.astype(out[name].dtype))
    for name, factor in factors.items():
        out[name] = (out[name] * factor).astype(out[name].dtype)
    return out
```

```python
from contextlib import ExitStack

import concourse.bass as bass
from concourse import mybir

F32 = mybir.dt.float32
F32R = mybir.dt.float32r
BF16 = mybir.dt.bfloat16
I32 = mybir.dt.int32
U32 = mybir.dt.uint32
ALU = mybir.AluOpType
ACT = mybir.ActivationFunctionType
AX_X = mybir.AxisListType.X

P = 128
B, D, DC = 32, 256, 192
HEADS, DH = 16, 64
INNER = HEADS * DH
GB = 4
GT = GB * P
NG = B // GB
NM = INNER // P
KD = D // P
E, H = 8, 1024
KH = H // P
REGION = B * P + P
SLOTS = (2 * B * P + E * (P - 1)) // P + 1
RING = 2
WIDE = KD * H
TILE_BITS = 7
assert KD * H == KH * D and 1 << TILE_BITS == P
EPS = 1e-5
CELLS = 16
RSQRT_SEED = 0x5F3759DF


def pair_bank_order(gate):
    order = ["c0", "c1"] + [f"v{j}" for j in range(2 * GB)] + ["x0", "x1", "q0", "k0", "q1", "k1"]
    for m in range(NM):
        if m >= 2:
            order.append(f"o{m - 2}")
        if 1 <= m < NM - 1:
            order += [f"q{m + 1}", f"k{m + 1}"]
        if gate:
            order += ROUTING_STEPS.get(m, [])
    return order + [f"o{NM - 2}", f"o{NM - 1}"]


ROUTING_STEPS = {0: ["z0", "z1"], 2: ["logits"], 4: ["rank"]}
FIRST, LATER, LAST = pair_bank_order(False), pair_bank_order(True), ["z0", "z1", "logits", "rank"]
assert len(FIRST) % 2 == 0 and len(LATER) % 2 == 0


def pair_bank(name, g):
    if isinstance(g, int) and g == 0:
        at, before = FIRST.index(name), 0
    elif isinstance(g, int) and g == NG:
        at, before = LAST.index(name), len(FIRST) // 2 + (NG - 1) * (len(LATER) // 2)
    else:
        at, before = LATER.index(name), g * (len(LATER) // 2) + (len(FIRST) - len(LATER)) // 2
    return at % 2, before + at // 2


def is_first(g):
    return isinstance(g, int) and g == 0


def build(nc, x, ctx_in, Wq, Wk, Wv, Wo, bo, Wg, bg, W1, b1, W2, b2, gamma, beta, out):
    x2_dram = nc.dram_tensor("x2_dram", (B * P, D), F32).ap()
    z_dram = nc.dram_tensor("z_dram", (B * P, D), F32).ap()
    routed_in = nc.dram_tensor("routed_in", (E * REGION + P, D), F32).ap()
    routed_out = nc.dram_tensor("routed_out", (SLOTS * P, D), F32).ap()

    with ExitStack() as whole:
        def keep(name, shape, dt):
            return whole.enter_context(nc.sbuf_tensor(name, shape, dt))

        ident = keep("ident", [P, P], F32)
        places_all = keep("places_all", [P, NG, GB, 2], U32)
        cells = keep("cells", [P, CELLS, 2], F32)
        weights_all = keep("weights_all", [P, NG, GB, 2], F32)
        chosen_sum = keep("chosen_sum", [P, E], BF16)
        ones_b = keep("ones_b", [P, P], BF16)

        attention(nc, x, ctx_in, Wq, Wk, Wv, Wo, bo, Wg, bg, x2_dram, z_dram, routed_in,
                  ident, places_all, weights_all, chosen_sum, ones_b, cells)
        experts(nc, W1, b1, W2, b2, routed_in, routed_out, ident, places_all, chosen_sum, ones_b, cells)
        combine(nc, x2_dram, z_dram, routed_out, gamma, beta, places_all, weights_all, cells, out)


def carry(eng, cell):
    return eng.tensor_tensor(cell[:, 0:1], cell[:, 1:2], cell[:, 1:2], ALU.add)


class Links:

    def __init__(self, eng, sem, before=0):
        self.eng, self.sem, self.before, self.n = eng, sem, before, 0

    def __call__(self, ins):
        self.n += 1
        ins.then_inc(self.sem, 1)
        self.eng.wait_ge(self.sem, self.before + self.n)


def rsqrt_and_shift(nc, link, mv, t, rstd, shift):
    v, a = t[:, 0:GB], t[:, GB:2 * GB]
    link(nc.vector.tensor_scalar(v, mv[:, :, 1], EPS, None, ALU.add))
    link(nc.vector.tensor_scalar(a.bitcast(I32), v.bitcast(I32), 1, None, ALU.logical_shift_right))
    link(nc.vector.tensor_scalar(rstd.bitcast(I32), a.bitcast(I32), -1.0, float(RSQRT_SEED),
                                 ALU.mult, ALU.add))
    for _ in range(3):
        link(nc.vector.scalar_tensor_tensor(out=a, in0=rstd, scalar=-0.5, in1=rstd,
                                            op0=ALU.mult, op1=ALU.mult))
        link(nc.vector.tensor_tensor(a, a, v, ALU.mult))
        link(nc.vector.scalar_tensor_tensor(out=rstd, in0=a, scalar=1.5, in1=rstd,
                                            op0=ALU.add, op1=ALU.mult))
    return nc.vector.scalar_tensor_tensor(out=shift, in0=mv[:, :, 0], scalar=-1.0, in1=rstd,
                                          op0=ALU.mult, op1=ALU.mult)


def attention(nc, x, ctx_in, Wq, Wk, Wv, Wo, bo, Wg, bg, x2_dram, z_dram, routed_in,
              ident, places_all, weights_all, chosen_sum, ones_b, cells):
    with ExitStack() as ctx:
        def sb(name, shape, dt=F32):
            return ctx.enter_context(nc.sbuf_tensor(name, shape, dt))

        def psum(name, shape):
            return ctx.enter_context(nc.psum_tensor(name, shape, F32))

        def sem(name):
            return ctx.enter_context(nc.semaphore(name))

        stage = sb("stage", [P, 2, 2048])
        wq_hi, wq_lo = sb("wq_hi", [P, KD, INNER], F32R), sb("wq_lo", [P, KD, INNER], F32R)
        wk_hi, wk_lo = sb("wk_hi", [P, INNER], F32R), sb("wk_lo", [P, INNER], F32R)
        wv_hi, wv_lo = sb("wv_hi", [P, INNER], F32R), sb("wv_lo", [P, INNER], F32R)
        wk_end, wv_end = sb("wk_end", [P, INNER], F32R), sb("wv_end", [P, INNER], F32R)
        wo_hi, wo_lo = sb("wo_hi", [P, NM, D], F32R), sb("wo_lo", [P, NM, D], F32R)
        wg = sb("wg", [P, KD, E])
        bo_all, bg_all = sb("bo_all", [P, D]), sb("bg_all", [P, E])
        before = sb("before", [P, P], BF16)
        expert_no = sb("expert_no", [P, E])
        region_at = sb("region_at", [P, E])

        xin, xn = sb("xin", [P, GB, D]), sb("xn", [P, GB, D])
        x_bo = sb("x_bo", [P, GB, D])
        cin = sb("cin", [P, GB, 2 * P])
        xT_hi, xT_lo = sb("xT_hi", [P, KD, GT], F32R), sb("xT_lo", [P, KD, GT], F32R)
        cT_hi, cT_lo = sb("cT_hi", [P, GT], F32R), sb("cT_lo", [P, GT], F32R)
        cT_end_hi, cT_end_lo = sb("cT_end_hi", [P, GT], F32R), sb("cT_end_lo", [P, GT], F32R)
        qT, kT = sb("qT", [P, 2, GT]), sb("kT", [P, 2, GT])
        v = sb("v", [P, GB, INNER])
        probs = sb("probs", [P, 2, 2, GB, P])
        probsT = sb("probsT", [P, 2, 2, GB, P])
        oT_hi, oT_lo = sb("oT_hi", [P, NM, GT], F32R), sb("oT_lo", [P, NM, GT], F32R)
        x2, z, zT = sb("x2", [P, GB, D]), sb("z", [P, GB, D]), sb("zT", [P, KD, GT])

        stats, mv = sb("stats", [P, GB, 6]), sb("mv", [P, GB, 2])
        tmp = sb("tmp", [P, 2 * GB])
        rstd1, shift1 = sb("rstd1", [P, GB]), sb("shift1", [P, GB])
        rstd2, shift2 = sb("rstd2", [P, GB]), sb("shift2", [P, GB])
        row_max = sb("row_max", [P, 2, GB])
        row_sum, row_rec = sb("row_sum", [P, 2, GB]), sb("row_rec", [P, 2, GB])
        logits = sb("logits", [P, GB, E])
        best, best_at = sb("best", [P, GB, 8]), sb("best_at", [P, GB, 8], U32)
        best_f = sb("best_f", [P, GB, 2])
        picks = sb("picks", [P, GB, 2, E])
        chosen = sb("chosen", [P, GB, E], BF16)
        sums = sb("sums", [P, GB, E], BF16)
        place = sb("place", [P, GB, E])
        place2 = sb("place2", [P, GB, 2, E])
        place_f = sb("place_f", [P, GB, 2])
        places = sb("places", [P, GB, 2], U32)
        gap, odds, p_best = sb("gap", [P, GB]), sb("odds", [P, GB]), sb("p_best", [P, GB, 2])

        s_ps = psum("s_ps", [P, 2, 2, GB, P])
        t_ps = psum("t_ps", [P, 2, GB, P])
        pair = psum("pair", [P, 2, 512])
        y_ps = s_ps[:, :, :, :, :].rearrange("p u a b k -> p (u a) (b k)")

        w_in = [sem(f"w_in{n}") for n in range(4)]
        w_hi, w_ready = sem("w_hi"), sem("w_ready")
        small_in = sem("small_in")
        x_in, c_in, x_used = sem("x_in"), sem("c_in"), sem("x_used")
        const_step, const_ready = sem("const_step"), sem("const_ready")
        chain = sem("chain")
        norm1_ready, xn_ready, norm2_ready, z_ready = sem("norm1_ready"), sem("xn_ready"), sem("norm2_ready"), sem("z_ready")
        full = [sem("pair0_full"), sem("pair1_full")]
        free = [sem("pair0_free"), sem("pair1_free")]
        cT_hi_ready, xT_hi_ready, oT_hi_ready = sem("cT_hi_ready"), sem("xT_hi_ready"), sem("oT_hi_ready")
        s_full, shifted, p_ready = sem("s_full"), sem("shifted"), sem("p_ready")
        expd, rec_ready, t_full, pT_ready = sem("expd"), sem("rec_ready"), sem("t_full"), sem("pT_ready")
        y_full, x2_ready = sem("y_full"), sem("x2_ready")
        x2_stored, z_stored, scattered = sem("x2_stored"), sem("z_stored"), sem("scattered")
        chosen_ready, places_ready, gap_ready, odds_ready = sem("chosen_ready"), sem("places_ready"), sem("gap_ready"), sem("odds_ready")

        block = ctx.enter_context(nc.Block())

        def take(eng, name, g):
            b, n = pair_bank(name, g)
            if not (isinstance(n, int) and n == 0):
                eng.wait_ge(free[b], n)
            return b

        def filled(eng, name, g):
            b, n = pair_bank(name, g)
            eng.wait_ge(full[b], n + 1)
            return b

        def drained(eng, name, g, taken=None):
            b, n = pair_bank(name, g)
            if b != taken:
                eng.wait_ge(free[b], n + 1)

        @block.sync
        def _(sp):
            def load_x(g):
                sp.dma_start(xin[:, :, :], x[bass.ds(g * GB, GB), :, :].rearrange("b p d -> p b d")).then_inc(x_in, 16)

            def load_c(g):
                src = ctx_in[bass.ds(g * GB, GB), :, :]
                sp.dma_start(cin[:, :, 0:DC], src.rearrange("b p d -> p b d")).then_inc(c_in, 16)
                sp.dma_start(cin[:, :, DC:2 * P], src[:, :, P:DC].rearrange("b p d -> p b d")).then_inc(c_in, 16)

            load_c(0)
            load_x(0)
            with sp.Fori(1, NG) as g:
                row = sp.snap(g * (GB * P) - GB * P)
                sp.wait_ge(cT_hi_ready, 2 * g)
                load_c(g)
                sp.wait_ge(x_used, g)
                load_x(g)
                sp.wait_ge(x2_ready, GB * g)
                sp.dma_start(x2_dram[bass.ds(row, GT), :].rearrange("(b p) d -> p b d", p=P), x2[:, :, :]).then_inc(x2_stored, 16)
                sp.wait_ge(z_ready, g)
                sp.dma_start(z_dram[bass.ds(row, GT), :].rearrange("(b p) d -> p b d", p=P), z[:, :, :]).then_inc(z_stored, 16)
            sp.wait_ge(x2_ready, GB * NG)
            last = (NG - 1) * GT
            sp.dma_start(x2_dram[last:last + GT, :].rearrange("(b p) d -> p b d", p=P), x2[:, :, :]).then_inc(x2_stored, 16)
            sp.wait_ge(z_ready, NG)
            sp.dma_start(z_dram[last:last + GT, :].rearrange("(b p) d -> p b d", p=P), z[:, :, :]).then_inc(z_stored, 16)
            sp.wait_ge(x2_stored, 16 * NG)
            sp.wait_ge(z_stored, 16 * NG)

        @block.gpsimd
        def _(pool):
            pool.memset(ident[:, :], 0.0).then_inc(const_step, 1)
            pool.memset(before[:, :], 1.0).then_inc(const_step, 1)
            pool.memset(cells[:, :, :], 0.0).then_inc(const_ready, 1)
            pool.memset(ones_b[:, :], 1.0).then_inc(const_ready, 1)
            pool.iota(expert_no[:, :], [[1, E]], base=0, channel_multiplier=0,
                      allow_small_or_imprecise_dtypes=True).then_inc(const_ready, 1)
            pool.iota(region_at[:, :], [[REGION, E]], base=0, channel_multiplier=0,
                      allow_small_or_imprecise_dtypes=True).then_inc(const_ready, 1)
            pool.memset(chosen_sum[:, :], 0.0).then_inc(const_ready, 1)
            pool.wait_ge(const_step, 2)
            pool.affine_select(out=ident[:, :], in_=ident[:, :], compare_op=ALU.not_equal, fill=1.0,
                               base=0, pattern=[[-1, P]], channel_multiplier=1).then_inc(const_ready, 1)
            pool.affine_select(out=before[:, :], in_=before[:, :], compare_op=ALU.is_gt, fill=0.0,
                               base=0, pattern=[[1, P]], channel_multiplier=-1).then_inc(const_ready, 1)
            pool.wait_ge(small_in, 16 * 3)
            pool.wait_ge(const_ready, 7)

            def group(g):
                pool.wait_ge(norm1_ready, g + 1)
                if not is_first(g):
                    pool.wait_ge(xT_hi_ready, g * 2)
                    pool.wait_ge(x2_ready, GB * g)
                    carry(pool, cells[:, 0, :])
                for b in range(GB):
                    last = pool.tensor_scalar(xn[:, b, :], xin[:, b, :], rstd1[:, b:b + 1], shift1[:, b:b + 1], ALU.mult, ALU.add)
                last.then_inc(xn_ready, 1)
                pool.tensor_tensor(x_bo[:, :, :], xin[:, :, :], bo_all[:, :].unsqueeze(1).to_broadcast([P, GB, D]),
                                   ALU.add).then_inc(x_used, 1)

            def normalise_out(g):
                pool.wait_ge(norm2_ready, g)
                if not (isinstance(g, int) and g == 1):
                    pool.wait_ge(z_stored, 16 * g - 16)
                    pool.wait_ge(scattered, (16 * 2 * GB) * g - 16 * 2 * GB)
                    carry(pool, cells[:, 1, :])
                for b in range(GB):
                    last = pool.tensor_scalar(z[:, b, :], x2[:, b, :], rstd2[:, b:b + 1], shift2[:, b:b + 1], ALU.mult, ALU.add)
                last.then_inc(z_ready, 1)

            def scatter(g, picks):
                if picks[0][0] == 0:
                    pool.wait_ge(places_ready, g)
                    carry(pool, cells[:, 2, :])
                for b, k in picks:
                    pool.indirect_dma_start(
                        out=routed_in, out_offset=bass.IndirectOffsetOnAxis(ap=places[:, b, k:k + 1], axis=0),
                        in_=z[:, b, :], in_offset=None).then_inc(scattered, 16)

            def steps(g):
                for m in range(NM):
                    for a in range(2):
                        pool.wait_ge(rec_ready, g * (2 * NM) + 2 * m + a + 1)
                        pool.tensor_tensor(probs[:, m % 2, a, :, :], probs[:, m % 2, a, :, :],
                                           row_rec[:, a, :].unsqueeze(2).to_broadcast([P, GB, P]), ALU.mult).then_inc(p_ready, 1)
                    if m >= NM - GB and not is_first(g):
                        scatter(g, [(m - (NM - GB), k) for k in range(2)])

            group(0)
            steps(0)
            group(1)
            normalise_out(1)
            steps(1)
            with pool.Fori(2, NG) as g:
                group(g)
                normalise_out(g)
                steps(g)
            normalise_out(NG)
            scatter(NG, [(b, k) for b in range(GB) for k in range(2)])
            pool.wait_ge(scattered, 16 * 2 * GB * NG)

        @block.scalar
        def _(act):
            def halves(n):
                return stage[:, n % 2, 0:INNER], stage[:, n % 2, INNER:2 * INNER]

            act.dma_start(stage[:, 0, 0:INNER], Wv[0:P, :]).then_inc(w_in[0], 16)
            act.dma_start(stage[0:DH, 0, INNER:], Wv[P:DC, :]).then_inc(w_in[0], 16)
            act.dma_start(stage[DH:P, 0, INNER:], Wv[P:DC, :]).then_inc(w_in[0], 16)
            act.dma_start(stage[:, 1, 0:INNER], Wk[0:P, :]).then_inc(w_in[1], 16)
            act.dma_start(stage[0:DH, 1, INNER:], Wk[P:DC, :]).then_inc(w_in[1], 16)
            act.dma_start(stage[DH:P, 1, INNER:], Wk[P:DC, :]).then_inc(w_in[1], 16)
            act.dma_start(bo_all[:, :], bo.rearrange("(a n) -> a n", a=1).to_broadcast([P, D])).then_inc(small_in, 16)
            act.dma_start(bg_all[:, :], bg.rearrange("(a n) -> a n", a=1).to_broadcast([P, E])).then_inc(small_in, 16)
            act.dma_start(wg[:, :, :], Wg.rearrange("(k p) e -> p k e", p=P)).then_inc(small_in, 16)
            for n, (hi, end) in enumerate(((wv_hi, wv_end), (wk_hi, wk_end))):
                act.wait_ge(w_in[n], 48)
                nc.scalar.activation(hi[:, :], halves(n)[0], ACT.Copy).then_inc(w_hi, 1)
                nc.scalar.activation(end[:, :], halves(n)[1], ACT.Copy).then_inc(w_hi, 1)
            act.wait_ge(w_ready, 1)
            act.dma_start(stage[:, 0, :].rearrange("p (k n) -> p k n", k=KD), Wq.rearrange("(k p) n -> p k n", p=P)).then_inc(w_in[2], 16)
            act.wait_ge(w_ready, 2)
            act.dma_start(stage[:, 1, :].rearrange("p (k n) -> p k n", k=NM), Wo.rearrange("(k p) n -> p k n", p=P)).then_inc(w_in[3], 16)
            act.wait_ge(w_in[2], 16)
            nc.scalar.activation(wq_hi[:, :, :].rearrange("p k n -> p (k n)"), stage[:, 0, :], ACT.Copy).then_inc(w_hi, 1)
            act.wait_ge(w_in[3], 16)
            nc.scalar.activation(wo_hi[:, :, :].rearrange("p k n -> p (k n)"), stage[:, 1, :], ACT.Copy).then_inc(w_hi, 1)

            def queries_keys(g, m):
                if not (is_first(g) and m < 2):
                    act.wait_ge(s_full, g * NM + m - 1)
                b = filled(act, f"q{m}", g)
                nc.scalar.activation(qT[:, m % 2, :], pair[:, b, :], ACT.Copy, scale=DH ** -0.5).then_inc(free[b], 1)
                b = filled(act, f"k{m}", g)
                nc.scalar.activation(kT[:, m % 2, :], pair[:, b, :], ACT.Copy).then_inc(free[b], 1)

            def group(g):
                gate = not is_first(g)
                for k, hi in enumerate((cT_hi, cT_end_hi)):
                    b = filled(act, f"c{k}", g)
                    nc.scalar.activation(hi[:, :], pair[:, b, :], ACT.Copy).then_inc(cT_hi_ready, 1)
                for j in range(2 * GB):
                    b = filled(act, f"v{j}", g)
                    nc.scalar.activation(v[:, j // 2, 512 * (j % 2):512 * (j % 2) + 512], pair[:, b, :], ACT.Copy).then_inc(free[b], 1)
                for k in range(KD):
                    b = filled(act, f"x{k}", g)
                    nc.scalar.activation(xT_hi[:, k, :], pair[:, b, :], ACT.Copy).then_inc(xT_hi_ready, 1)
                queries_keys(g, 0)
                queries_keys(g, 1)
                for m in range(NM):
                    if m >= 2:
                        outputs_hi(g, m - 2)
                    for a in range(2):
                        act.wait_ge(shifted, g * (2 * NM) + 2 * m + a + 1)
                        nc.scalar.activation(probs[:, m % 2, a, :, :], probs[:, m % 2, a, :, :], ACT.Exp).then_inc(expd, 1)
                    if 1 <= m < NM - 1:
                        queries_keys(g, m + 1)
                    if gate:
                        routing(g, m)
                    if m >= 1:
                        probs_out(g, m - 1)
                outputs_hi(g, NM - 2)
                probs_out(g, NM - 1)
                outputs_hi(g, NM - 1)

            def probs_out(g, m):
                for a in range(2):
                    act.wait_ge(t_full, g * (2 * NM) + 2 * m + a + 1)
                    nc.scalar.activation(probsT[:, m % 2, a, :, :], t_ps[:, a, :, :], ACT.Copy).then_inc(pT_ready, 1)

            def outputs_hi(g, m):
                b = filled(act, f"o{m}", g)
                if not is_first(g):
                    act.wait_ge(x2_ready, GB * g)
                nc.scalar.activation(oT_hi[:, m, :], pair[:, b, :], ACT.Copy).then_inc(oT_hi_ready, 1)

            def routing(g, m):
                if m == 0:
                    for k in range(KD):
                        b = filled(act, f"z{k}", g)
                        nc.scalar.activation(zT[:, k, :], pair[:, b, :], ACT.Copy).then_inc(free[b], 1)
                if m == 3:
                    act.wait_ge(gap_ready, g)
                    nc.scalar.activation(odds[:, :], gap[:, :], ACT.Exp).then_inc(odds_ready, 1)

            group(0)
            with act.Fori(1, NG) as g:
                group(g)
            routing(NG, 0)
            routing(NG, 3)

        @block.vector
        def _(dve):
            for n, (lo, hi, end) in enumerate(((wv_lo, wv_hi, wv_end), (wk_lo, wk_hi, wk_end))):
                dve.wait_ge(w_hi, 2 * n + 2)
                nc.vector.tensor_tensor(lo[:, :], stage[:, n, 0:INNER], hi[:, :].bitcast(F32), ALU.subtract)
                nc.vector.tensor_tensor(end[DH:P, :], stage[DH:P, n, INNER:], end[DH:P, :].bitcast(F32), ALU.subtract).then_inc(w_ready, 1)

            def late_weights():
                dve.wait_ge(w_hi, 5)
                nc.vector.tensor_tensor(wq_lo[:, :, :].rearrange("p k n -> p (k n)"), stage[:, 0, :],
                                        wq_hi[:, :, :].rearrange("p k n -> p (k n)").bitcast(F32), ALU.subtract).then_inc(w_ready, 1)
                dve.wait_ge(w_hi, 6)
                nc.vector.tensor_tensor(wo_lo[:, :, :].rearrange("p k n -> p (k n)"), stage[:, 1, :],
                                        wo_hi[:, :, :].rearrange("p k n -> p (k n)").bitcast(F32), ALU.subtract).then_inc(w_ready, 1)

            def statistics(link, src):
                for b in range(GB):
                    i = nc.vector.bn_stats(stats[:, b, :], src[:, b, :])
                link(i)
                carry(nc.vector, cells[:, 3, :])
                for b in range(GB):
                    i = nc.vector.bn_aggr(mv[:, b, :], stats[:, b, :])
                link(i)

            def norm1(g, link):
                dve.wait_ge(x_in, g * 16 + 16)
                if not is_first(g):
                    dve.wait_ge(x_used, g)
                statistics(link, xin)
                rsqrt_and_shift(nc, link, mv, tmp, rstd1[:, :], shift1[:, :]).then_inc(norm1_ready, 1)

            def norm2(g, link):
                dve.wait_ge(x2_ready, GB * g)
                if not (isinstance(g, int) and g == 1):
                    dve.wait_ge(z_ready, g - 1)
                statistics(link, x2)
                rsqrt_and_shift(nc, link, mv, tmp, rstd2[:, :], shift2[:, :]).then_inc(norm2_ready, 1)

            def outputs_lo(g, m):
                b = pair_bank(f"o{m}", g)[0]
                dve.wait_ge(oT_hi_ready, g * NM + m + 1)
                i = nc.vector.tensor_tensor(oT_lo[:, m, :], pair[:, b, :], oT_hi[:, m, :].bitcast(F32), ALU.subtract)
                i.then_inc(free[b], 1)

            def group(g, link):
                gate = not is_first(g)
                b = pair_bank("c0", g)[0]
                dve.wait_ge(cT_hi_ready, 2 * g + 1)
                i = nc.vector.tensor_tensor(cT_lo[:, :], pair[:, b, :], cT_hi[:, :].bitcast(F32), ALU.subtract)
                i.then_inc(free[b], 1)
                b = pair_bank("c1", g)[0]
                dve.wait_ge(cT_hi_ready, 2 * g + 2)
                i = nc.vector.tensor_tensor(cT_end_lo[0:DH, :], pair[0:DH, b, :], cT_end_hi[0:DH, :].bitcast(F32), ALU.subtract)
                i.then_inc(free[b], 1)
                norm1(g, link)
                if gate:
                    norm2(g, link)
                else:
                    late_weights()
                for k in range(KD):
                    b = pair_bank(f"x{k}", g)[0]
                    dve.wait_ge(xT_hi_ready, KD * g + k + 1)
                    i = nc.vector.tensor_tensor(xT_lo[:, k, :], pair[:, b, :], xT_hi[:, k, :].bitcast(F32), ALU.subtract)
                    i.then_inc(free[b], 1)
                for m in range(NM):
                    n = g * (2 * NM) + 2 * m
                    dve.wait_ge(s_full, g * NM + m + 1)
                    if not (is_first(g) and m < 2):
                        dve.wait_ge(t_full, n - 2)
                    for a in range(2):
                        link(nc.vector.tensor_reduce(row_max[:, a, :], s_ps[:, m % 2, a, :, :], AX_X, ALU.max))
                        nc.vector.tensor_tensor(probs[:, m % 2, a, :, :], s_ps[:, m % 2, a, :, :],
                                                row_max[:, a, :].unsqueeze(2).to_broadcast([P, GB, P]), ALU.subtract).then_inc(shifted, 1)
                        if a == 0 and m >= 2:
                            outputs_lo(g, m - 2)
                    for a in range(2):
                        dve.wait_ge(expd, n + a + 1)
                        if not (is_first(g) and m == 0):
                            dve.wait_ge(p_ready, n + a - 1)
                        link(nc.vector.tensor_reduce(row_sum[:, a, :], probs[:, m % 2, a, :, :], AX_X, ALU.add))
                        nc.vector.reciprocal(row_rec[:, a, :], row_sum[:, a, :]).then_inc(rec_ready, 1)
                    if gate:
                        routing(g, m, link)
                outputs_lo(g, NM - 2)
                outputs_lo(g, NM - 1)
                if gate:
                    dve.wait_ge(x2_stored, 16 * g)
                dve.wait_ge(x_used, g + 1)
                for b in range(GB):
                    dve.wait_ge(y_full, GB * g + b + 1)
                    nc.vector.tensor_tensor(x2[:, b, :], y_ps[:, b, 0:D], x_bo[:, b, :], ALU.add).then_inc(x2_ready, 1)

            def routing(g, m, link):
                if m == 2:
                    b = filled(dve, "logits", g)
                    i = nc.vector.tensor_tensor(logits[:, :, :], pair[:, b, 0:GB * E].rearrange("p (t e) -> p t e", e=E),
                                                bg_all[:, :].unsqueeze(1).to_broadcast([P, GB, E]), ALU.add)
                    i.then_inc(free[b], 1)
                    drained(dve, "logits", g)
                    carry(nc.vector, cells[:, 4, :])
                    for t in range(GB):
                        i = nc.vector.max(best[:, t, :], logits[:, t, :])
                    link(i)
                    nc.vector.tensor_tensor(gap[:, :], best[:, :, 1], best[:, :, 0], ALU.subtract).then_inc(gap_ready, 1)
                    for t in range(GB):
                        i = nc.vector.max_index(best_at[:, t, :], best[:, t, :], logits[:, t, :])
                    link(i)
                    link(nc.vector.tensor_copy(best_f[:, :, :], best_at[:, :, 0:2]))
                    link(nc.vector.tensor_tensor(picks[:, :, :, :], expert_no[:, :].unsqueeze(1).unsqueeze(1).to_broadcast([P, GB, 2, E]),
                                                 best_f[:, :, :].unsqueeze(3).to_broadcast([P, GB, 2, E]), ALU.is_equal))
                    link(nc.vector.tensor_tensor(chosen[:, :, :], picks[:, :, 0, :], picks[:, :, 1, :], ALU.add))
                    link(nc.vector.tensor_copy(sums[:, 0, :], chosen_sum[:, :]))
                    for t in range(1, GB):
                        link(nc.vector.tensor_tensor(sums[:, t, :], sums[:, t - 1, :], chosen[:, t - 1, :], ALU.add))
                    i = nc.vector.tensor_tensor(chosen_sum[:, :], sums[:, GB - 1, :], chosen[:, GB - 1, :], ALU.add)
                    i.then_inc(chosen_ready, 1)
                if m == 4:
                    b = filled(dve, "rank", g)
                    i = nc.vector.tensor_tensor(place[:, :, :], pair[:, b, 0:GB * E].rearrange("p (t e) -> p t e", e=E),
                                                region_at[:, :].unsqueeze(1).to_broadcast([P, GB, E]), ALU.add)
                    i.then_inc(free[b], 1)
                    drained(dve, "rank", g)
                    link(nc.vector.tensor_tensor(place2[:, :, :, :], picks[:, :, :, :],
                                                 place[:, :, :].unsqueeze(2).to_broadcast([P, GB, 2, E]), ALU.mult))
                    link(nc.vector.tensor_reduce(place_f[:, :, :], place2[:, :, :, :], AX_X, ALU.add))
                    if not (isinstance(g, int) and g == 1):
                        dve.wait_ge(scattered, (16 * 2 * GB) * g - 16 * 2 * GB)
                    i = nc.vector.tensor_copy(places[:, :, :], place_f[:, :, :])
                    i.then_inc(places_ready, 1)
                    nc.vector.tensor_copy(places_all[:, bass.ds(g - 1, 1), :, :].rearrange("p g t k -> p (g t) k"), place_f[:, :, :])
                    dve.wait_ge(odds_ready, g)
                    link(nc.vector.tensor_scalar(gap[:, :], odds[:, :], 1.0, None, ALU.add))
                    link(nc.vector.reciprocal(p_best[:, :, 0], gap[:, :]))
                    link(nc.vector.tensor_tensor(p_best[:, :, 1], p_best[:, :, 0], odds[:, :], ALU.mult))
                    link(nc.vector.tensor_copy(weights_all[:, bass.ds(g - 1, 1), :, :].rearrange("p g t k -> p (g t) k"), p_best[:, :, :]))

            link = Links(dve, chain)
            group(0, link)
            first_links = link.n
            with dve.Fori(1, NG) as g:
                link = Links(dve, chain, g * LINKS_PER_GROUP + (first_links - LINKS_PER_GROUP))
                group(g, link)
                assert link.n == LINKS_PER_GROUP, link.n
            link = Links(dve, chain, first_links + (NG - 1) * LINKS_PER_GROUP)
            norm2(NG, link)
            routing(NG, 2, link)
            routing(NG, 4, link)

        @block.tensor
        def _(pe):
            mm, tr = nc.tensor.matmul, nc.tensor.transpose

            def three(out, a_hi, a_lo, b_hi, b_lo, start, stop):
                mm(out, a_hi, b_hi, start=start, stop=False)
                mm(out, a_hi, b_lo, start=False, stop=False)
                return mm(out, a_lo, b_hi, start=False, stop=stop)

            def project_queries_keys(g, m):
                cols = slice(m * P, m * P + P)
                b = take(pe, f"q{m}", g)
                if m == 0:
                    drained(pe, "x0", g, b)
                    drained(pe, "x1", g, b)
                for k in range(KD):
                    i = three(pair[:, b, :], wq_hi[:, k, cols], wq_lo[:, k, cols], xT_hi[:, k, :], xT_lo[:, k, :], k == 0, k == KD - 1)
                i.then_inc(full[b], 1)
                b = take(pe, f"k{m}", g)
                three(pair[:, b, :], wk_hi[:, cols], wk_lo[:, cols], cT_hi[:, :], cT_lo[:, :], True, False)
                mm(pair[:, b, :], wk_end[:, cols], cT_end_hi[:, :], start=False, stop=False)
                i = mm(pair[:, b, :], wk_end[0:DH, cols], cT_end_lo[0:DH, :], start=False, stop=True)
                i.then_inc(full[b], 1)

            def scores(g, m):
                n = g * NM + m
                drained(pe, f"q{m}", g)
                drained(pe, f"k{m}", g)
                if not (is_first(g) and m < 2):
                    pe.wait_ge(shifted, 2 * n - 2)
                if m < 2 and not is_first(g):
                    pe.wait_ge(x2_ready, GB * g - GB + 2 * m + 2)
                for b in range(GB):
                    for a in range(2):
                        rows, cols = slice(DH * a, DH * a + DH), slice(b * P, b * P + P)
                        i = mm(s_ps[:, m % 2, a, b, :], qT[rows, m % 2, cols], kT[rows, m % 2, cols], start=True, stop=True)
                i.then_inc(s_full, 1)

            def transpose_probs(g, m):
                n = g * (2 * NM) + 2 * m
                for a in range(2):
                    pe.wait_ge(p_ready, n + a + 1)
                    if not (is_first(g) and m == 0):
                        pe.wait_ge(pT_ready, n + a - 1)
                    for b in range(GB):
                        i = tr(t_ps[:, a, b, :], probs[:, m % 2, a, b, :], ident[:, :])
                    i.then_inc(t_full, 1)

            def weigh_values(g, m):
                pe.wait_ge(pT_ready, g * (2 * NM) + 2 * m + 2)
                bank = take(pe, f"o{m}", g)
                for b in range(GB):
                    for a in range(2):
                        cols = slice((2 * m + a) * DH, (2 * m + a + 1) * DH)
                        i = mm(pair[DH * a:DH * a + DH, bank, b * P:b * P + P], v[:, b, cols], probsT[:, m % 2, a, b, :],
                               start=True, stop=True)
                i.then_inc(full[bank], 1)

            def project_out(g, t, ms):
                rows = slice(t * P, t * P + P)
                if 0 in ms:
                    pe.wait_ge(shifted, g * (2 * NM) + (2 * NM - 2 if t < 2 else 2 * NM))
                for m in ms:
                    if (t, m) in ((0, NM - 4), (0, NM - 3), (2, NM - 2), (0, NM - 1)):
                        drained(pe, f"o{m}", g)
                    i = three(y_ps[:, t, 0:D], oT_hi[:, m, rows], oT_lo[:, m, rows], wo_hi[:, m, :], wo_lo[:, m, :],
                              m == 0, m == NM - 1)
                if NM - 1 in ms:
                    i.then_inc(y_full, 1)

            def group(g):
                gate = not is_first(g)
                pe.wait_ge(c_in, g * 32 + 32)
                for k in range(2):
                    b = take(pe, f"c{k}", g)
                    for t in range(GB):
                        i = tr(pair[:, b, t * P:t * P + P], cin[:, t, k * P:k * P + P], ident[:, :])
                    i.then_inc(full[b], 1)
                for j in range(2 * GB):
                    if j == 0 and not gate:
                        pe.wait_ge(w_ready, 2)
                    b = take(pe, f"v{j}", g)
                    if j == 0:
                        drained(pe, "c0", g, b)
                        drained(pe, "c1", g, b)
                    t, cols = slice(j // 2 * P, j // 2 * P + P), slice(j % 2 * 512, j % 2 * 512 + 512)
                    three(pair[:, b, :], cT_hi[:, t], cT_lo[:, t], wv_hi[:, cols], wv_lo[:, cols], True, False)
                    mm(pair[:, b, :], cT_end_hi[:, t], wv_end[:, cols], start=False, stop=False)
                    mm(pair[:, b, :], cT_end_lo[0:DH, t], wv_end[0:DH, cols], start=False, stop=True).then_inc(full[b], 1)
                pe.wait_ge(xn_ready, g + 1)
                for k in range(KD):
                    b = take(pe, f"x{k}", g)
                    for t in range(GB):
                        i = tr(pair[:, b, t * P:t * P + P], xn[:, t, k * P:k * P + P], ident[:, :])
                    i.then_inc(full[b], 1)
                if not gate:
                    pe.wait_ge(w_ready, 3)
                project_queries_keys(g, 0)
                drained(pe, f"v{2 * GB - 2}", g)
                drained(pe, f"v{2 * GB - 1}", g)
                project_queries_keys(g, 1)
                for m in range(NM):
                    scores(g, m)
                    if m >= 2:
                        weigh_values(g, m - 2)
                    if 1 <= m < NM - 1:
                        project_queries_keys(g, m + 1)
                    if gate:
                        routing(g, m)
                    if m >= 1:
                        transpose_probs(g, m - 1)
                if not gate:
                    pe.wait_ge(w_ready, 4)
                project_out(g, 0, range(NM - 3))
                weigh_values(g, NM - 2)
                project_out(g, 1, range(NM - 3))
                transpose_probs(g, NM - 1)
                for t in range(2):
                    project_out(g, t, [NM - 3])
                weigh_values(g, NM - 1)
                for t in (2, 3):
                    project_out(g, t, range(NM - 1))
                for t in range(2):
                    project_out(g, t, [NM - 2, NM - 1])
                for t in (2, 3):
                    project_out(g, t, [NM - 1])

            def routing(g, m):
                if m == 0:
                    pe.wait_ge(z_ready, g)
                    for k in range(KD):
                        b = take(pe, f"z{k}", g)
                        for t in range(GB):
                            i = tr(pair[:, b, t * P:t * P + P], z[:, t, k * P:k * P + P], ident[:, :])
                        i.then_inc(full[b], 1)
                if m == 2:
                    b = take(pe, "logits", g)
                    drained(pe, "z0", g, b)
                    drained(pe, "z1", g, b)
                    for t in range(GB):
                        for k in range(KD):
                            i = mm(pair[:, b, t * E:t * E + E], zT[:, k, t * P:t * P + P], wg[:, k, :], start=(k == 0), stop=(k == KD - 1))
                    i.then_inc(full[b], 1)
                if m == 4:
                    pe.wait_ge(chosen_ready, g)
                    b = take(pe, "rank", g)
                    for t in range(GB):
                        mm(pair[:, b, t * E:t * E + E], before[:, :], chosen[:, t, :], start=True, stop=False)
                        i = mm(pair[:, b, t * E:t * E + E], ones_b[:, :], sums[:, t, :], start=False, stop=True)
                    i.then_inc(full[b], 1)

            pe.wait_ge(const_ready, 7)
            pe.wait_ge(small_in, 48)
            group(0)
            with pe.Fori(1, NG) as g:
                group(g)
            routing(NG, 0)
            routing(NG, 2)
            routing(NG, 4)


LINKS_PER_GROUP = 75


def experts(nc, W1, b1, W2, b2, routed_in, routed_out, ident, places_all, chosen_sum, ones_b, cells):
    with ExitStack() as ctx:
        def sb(name, shape, dt=F32):
            return ctx.enter_context(nc.sbuf_tensor(name, shape, dt))

        def psum(name, shape):
            return ctx.enter_context(nc.psum_tensor(name, shape, F32))

        def sem(name):
            return ctx.enter_context(nc.semaphore(name))

        w1_hi, w1_lo = sb("w1_hi", [P, RING * WIDE], F32R), sb("w1_lo", [P, RING * WIDE], F32R)
        w2_hi, w2_lo = sb("w2_hi", [P, RING * WIDE], F32R), sb("w2_lo", [P, RING * WIDE], F32R)
        w1_stage, w2_stage = sb("w1_stage", [P, WIDE]), sb("w2_stage", [P, WIDE])
        w1_first, w2_first = sb("w1_first", [P, WIDE]), sb("w2_first", [P, WIDE])
        b1_all, b2_all = sb("b1_all", [P, RING * H]), sb("b2_all", [P, RING * D])
        zeros = sb("zeros", [P, D])

        counts, tiles, ends = sb("counts", [P, E]), sb("tiles", [P, E]), sb("ends", [P, E])
        tiles_i = sb("tiles_i", [P, E], I32)
        slot_no, regions = sb("slot_no", [P, SLOTS]), sb("regions", [P, E])
        passed, passed_tiles = sb("passed", [P, SLOTS, E]), sb("passed_tiles", [P, SLOTS, E])
        slot_expert, tile_no = sb("slot_expert", [P, SLOTS]), sb("tile_no", [P, SLOTS])
        move, move_step = sb("move", [P, E]), sb("move_step", [P, E])
        place_in, moved, beyond = sb("place_in", [P, 2 * B]), sb("moved", [P, 2 * B]), sb("beyond", [P, 2 * B, E])
        slot_row, half = sb("slot_row", [P, SLOTS]), sb("half", [P, SLOTS], I32)
        x_row = sb("x_row", [P, SLOTS], I32)
        owner = sb("owner", [P, SLOTS], I32)
        need = sb("need", [P, SLOTS], I32)
        w_at = sb("w_at", [P, SLOTS], I32)
        b1_at, b2_at = sb("b1_at", [P, SLOTS], I32), sb("b2_at", [P, SLOTS], I32)
        end_slot = sb("end_slot", [P, E], I32)
        pad_row = sb("pad_row", [P, E], I32)

        tile = sb("tile", [P, 2, D])
        rT_hi, rT_lo = sb("rT_hi", [P, KD, P], F32R), sb("rT_lo", [P, KD, P], F32R)
        hid = sb("hid", [P, H])
        hT_hi, hT_lo = sb("hT_hi", [P, KH, P], F32R), sb("hT_lo", [P, KH, P], F32R)
        y = sb("y", [P, 2, D])

        h_ps, ht_ps = psum("h_ps", [P, 2, 512]), psum("ht_ps", [P, 2, 4, P])
        rt_ps, yo_ps, n_ps = psum("rt_ps", [P, 4, P]), psum("yo_ps", [P, 512]), psum("n_ps", [P, 512])

        no_ready, counted, chain = sem("no_ready"), sem("counted"), sem("table_chain")
        pads_ready, slots_ready = sem("pads_ready"), sem("slots_ready")
        padded, zeros_ready = sem("padded"), sem("zeros_ready")
        first_in, first_hi = [sem("first1_in"), sem("first2_in")], sem("first_hi")
        w1_in, w2_in, b_in, w_hi_done = sem("w1_in"), sem("w2_in"), sem("b_in"), sem("w_hi_done")
        w1_ready, w2_ready = sem("w1_ready"), sem("w2_ready")
        tile_in = [sem("tile0_in"), sem("tile1_in")]
        rt_full, rT_hi_ready, rT_ready = sem("rt_full"), sem("rT_hi_ready"), sem("rT_ready")
        h_full, h_biased, h_ready = sem("h_full"), sem("h_biased"), sem("h_ready")
        ht_full, hT_hi_ready, hT_ready = sem("ht_full"), sem("hT_hi_ready"), sem("hT_ready")
        yo_full, y_ready = sem("yo_full"), sem("y_ready")
        y_stored = [sem("y0_stored"), sem("y1_stored")]

        block = ctx.enter_context(nc.Block())

        def from_table(eng, table, s, top, least=0):
            return eng.value_load(table[0:1, bass.ds(s, 1)], min_val=least, max_val=top)

        @block.sync
        def _(sp):
            sp.dma_start(w1_first[:, :].rearrange("p (k h) -> p k h", k=KD), W1[0].rearrange("(k p) h -> p k h", p=P)).then_inc(first_in[0], 16)
            sp.dma_start(w2_first[:, :].rearrange("p (k d) -> p k d", k=KH), W2[0].rearrange("(k p) d -> p k d", p=P)).then_inc(first_in[1], 16)
            sp.wait_ge(zeros_ready, 1)
            sp.dma_start(routed_in[E * REGION:E * REGION + P, :], zeros[:, :]).then_inc(padded, 16)
            sp.wait_ge(pads_ready, 1)
            with sp.Fori(0, E) as e:
                row = from_table(sp, pad_row, e, E * REGION - P)
                sp.dma_start(routed_in[bass.ds(row, P), :], zeros[:, :]).then_inc(padded, 16)
            sp.wait_ge(slots_ready, 1)
            sp.wait_ge(padded, 16 * (E + 1))
            for s in range(2):
                row = from_table(sp, x_row, s, E * REGION)
                sp.dma_start(tile[:, s, :], routed_in[bass.ds(row, P), :]).then_inc(tile_in[s], 16)

            def load(s, j):
                row = from_table(sp, x_row, sp.snap(s + 2), E * REGION)
                sp.wait_ge(rt_full, s + 1)
                sp.dma_start(tile[:, j, :], routed_in[bass.ds(row, P), :]).then_inc(tile_in[j], 16)

            def store(s, j):
                row = s * P if isinstance(s, int) else sp.snap(s * P)
                sp.wait_ge(y_ready, s + 2)
                sp.dma_start(routed_out[bass.ds(row, P), :], y[:, j, :]).then_inc(y_stored[j], 16)

            load(0, 0)
            load(1, 1)
            with sp.Fori(0, SLOTS // 2 - 2) as i:
                for j in range(2):
                    s = sp.snap(i * 2 + j)
                    load(sp.snap(s + 2), j)
                    store(s, j)
            for s in range(SLOTS - 4, SLOTS):
                store(s, s % 2)
            sp.wait_ge(y_stored[0], 16 * (SLOTS // 2))
            sp.wait_ge(y_stored[1], 16 * (SLOTS // 2))

        @block.gpsimd
        def _(pool):
            def load_weights(e):
                one = bass.ds(e, 1)
                pool.dma_start(w1_stage[:, :].rearrange("p (k h) -> p k h", k=KD), W1[one, :, :].rearrange("a (k p) h -> p (a k) h", p=P)).then_inc(w1_in, 16)
                pool.dma_start(w2_stage[:, :].rearrange("p (k d) -> p k d", k=KH), W2[one, :, :].rearrange("a (k p) d -> p (a k) d", p=P)).then_inc(w2_in, 16)

            def load_biases(e, r):
                one = bass.ds(e, 1)
                pool.dma_start(b1_all[:, r * H:r * H + H], b1[one, :].to_broadcast([P, H])).then_inc(b_in, 16)
                pool.dma_start(b2_all[:, r * D:r * D + D], b2[one, :].to_broadcast([P, D])).then_inc(b_in, 16)

            load_weights(1)
            pool.memset(zeros[:, :], 0.0).then_inc(zeros_ready, 1)
            pool.iota(slot_no[:, :], [[1, SLOTS]], base=0, channel_multiplier=0,
                      allow_small_or_imprecise_dtypes=True).then_inc(no_ready, 1)
            pool.iota(regions[:, :], [[REGION, E]], base=0, channel_multiplier=0,
                      allow_small_or_imprecise_dtypes=True).then_inc(no_ready, 1)
            load_biases(0, 0)
            pool.wait_ge(b_in, 32)
            load_biases(1, 1)

            def split(e, r):
                at = slice(r * WIDE, r * WIDE + WIDE)
                for n, (hi, lo, stage, came, ready) in enumerate(((w1_hi, w1_lo, w1_stage, w1_in, w1_ready),
                                                                  (w2_hi, w2_lo, w2_stage, w2_in, w2_ready))):
                    pool.wait_ge(came, 16 * e)
                    carry(pool, cells[:, 5 + n, :])
                    pool.tensor_scalar(hi[:, at], stage[:, :], 1.0, 0.0, ALU.mult, ALU.add).then_inc(w_hi_done, 1)
                    pool.wait_ge(b_in, 32 * e + 32)
                    if isinstance(e, int) and e == 1:
                        pool.wait_ge(ready, 1)
                    pool.wait_ge(w_hi_done, 2 * e - 1 + n)
                    pool.tensor_tensor(lo[:, at], stage[:, :], hi[:, at].bitcast(F32), ALU.subtract).then_inc(ready, 1)

            def weights(e, r, more):
                done = from_table(pool, end_slot, pool.snap(e - RING) if not isinstance(e, int) else e - RING, SLOTS + 1, 1)
                pool.wait_ge(y_ready, done)
                carry(pool, cells[:, 7, :])
                load_biases(e, r)
                split(e, r)
                if more:
                    after(e)

            def after(e):
                pool.wait_ge(w1_ready, e + 1)
                pool.wait_ge(w2_ready, e + 1)
                load_weights(e + 1 if isinstance(e, int) else pool.snap(e + 1))

            split(1, 1)
            after(1)
            pool.wait_ge(slots_ready, 1)
            with pool.Fori(1, E // 2 - 1) as i:
                weights(pool.snap(i * 2), 0, True)
                weights(pool.snap(i * 2 + 1), 1, True)
            weights(E - 2, 0, True)
            weights(E - 1, 1, False)

        @block.scalar
        def _(act):
            for n, (hi, stage) in enumerate(((w1_hi, w1_first), (w2_hi, w2_first))):
                act.wait_ge(first_in[n], 16)
                nc.scalar.activation(hi[:, 0:WIDE], stage[:, :], ACT.Identity).then_inc(first_hi, 1)

            def high_inputs(s):
                act.wait_ge(rt_full, s + 1)
                nc.scalar.activation(rT_hi[:, :, :], rt_ps[:, 0:KD, :], ACT.Identity).then_inc(rT_hi_ready, 1)

            def high_hidden(s):
                for a in range(2):
                    act.wait_ge(ht_full, 2 * s + a + 1)
                    nc.scalar.activation(hT_hi[:, 4 * a:4 * a + 4, :], ht_ps[:, a, :, :], ACT.Identity).then_inc(hT_hi_ready, 1)

            def gelu(s):
                for a in range(2):
                    act.wait_ge(h_biased, 2 * s + a + 1)
                    nc.scalar.activation(hid[:, 512 * a:512 * a + 512], hid[:, 512 * a:512 * a + 512], ACT.Gelu).then_inc(h_ready, 1)

            high_inputs(0)
            gelu(0)
            high_inputs(1)
            high_hidden(0)
            with act.Fori(1, SLOTS - 1) as s:
                gelu(s)
                high_inputs(act.snap(s + 1))
                high_hidden(s)
            gelu(SLOTS - 1)
            high_hidden(SLOTS - 1)

        @block.vector
        def _(dve):
            link = Links(dve, chain)
            dve.wait_ge(counted, 1)
            link(nc.vector.tensor_copy(counts[:, :], n_ps[:, 0:E]))
            dve.wait_ge(no_ready, 2)
            nc.vector.tensor_tensor(pad_row[:, :], counts[:, :], regions[:, :], ALU.add).then_inc(pads_ready, 1)
            link(nc.vector.tensor_scalar(tiles_i[:, :], counts[:, :], float(P - 1), None, ALU.add))
            link(nc.vector.tensor_scalar(tiles_i[:, :], tiles_i[:, :], TILE_BITS, None, ALU.logical_shift_right))
            link(nc.vector.tensor_copy(tiles[:, :], tiles_i[:, :]))
            link(nc.vector.tensor_copy(ends[:, 0:1], tiles[:, 0:1]))
            for e in range(1, E):
                link(nc.vector.tensor_tensor(ends[:, e:e + 1], ends[:, e - 1:e], tiles[:, e:e + 1], ALU.add))
            nc.vector.tensor_scalar(end_slot[:, :], ends[:, :], 1.0, None, ALU.add).then_inc(y_ready, 1)
            link(nc.vector.tensor_tensor(passed[:, :, :], slot_no[:, :].unsqueeze(2).to_broadcast([P, SLOTS, E]),
                                         ends[:, :].unsqueeze(1).to_broadcast([P, SLOTS, E]), ALU.is_ge))
            nc.vector.tensor_reduce(slot_expert[:, :], passed[:, :, :], AX_X, ALU.add)
            link(nc.vector.tensor_tensor(passed_tiles[:, :, :], passed[:, :, :],
                                         tiles[:, :].unsqueeze(1).to_broadcast([P, SLOTS, E]), ALU.mult))
            link(nc.vector.tensor_reduce(tile_no[:, :], passed_tiles[:, :, :], AX_X, ALU.add))
            link(nc.vector.tensor_tensor(tile_no[:, :], slot_no[:, :], tile_no[:, :], ALU.subtract))
            link(nc.vector.tensor_scalar(tile_no[:, :], tile_no[:, :], float(P), None, ALU.mult))
            link(nc.vector.scalar_tensor_tensor(out=slot_row[:, :], in0=slot_expert[:, :], scalar=float(REGION),
                                                in1=tile_no[:, :], op0=ALU.mult, op1=ALU.add))
            nc.vector.tensor_scalar(x_row[:, :], slot_row[:, :], float(E * REGION), None, ALU.min)
            link(nc.vector.tensor_scalar(owner[:, :], slot_expert[:, :], float(E - 1), None, ALU.min))
            nc.vector.tensor_scalar(need[:, :], owner[:, :], 1.0, None, ALU.add)
            link(nc.vector.tensor_scalar(half[:, :], owner[:, :], RING - 1, None, ALU.bitwise_and))
            nc.vector.tensor_scalar(w_at[:, :], half[:, :], float(WIDE), None, ALU.mult)
            nc.vector.tensor_scalar(b1_at[:, :], half[:, :], float(H), None, ALU.mult)
            nc.vector.tensor_scalar(b2_at[:, :], half[:, :], float(D), None, ALU.mult).then_inc(slots_ready, 1)
            for n, (lo, hi, stage) in enumerate(((w1_lo, w1_hi, w1_first), (w2_lo, w2_hi, w2_first))):
                dve.wait_ge(first_hi, n + 1)
                nc.vector.tensor_tensor(lo[:, 0:WIDE], stage[:, :], hi[:, 0:WIDE].bitcast(F32), ALU.subtract).then_inc((w1_ready, w2_ready)[n], 1)
            dve.wait_ge(b_in, 64)
            dve.wait_ge(slots_ready, 1)

            def low_inputs(s):
                dve.wait_ge(rT_hi_ready, s + 1)
                nc.vector.tensor_tensor(rT_lo[:, :, :], rt_ps[:, 0:KD, :], rT_hi[:, :, :].bitcast(F32), ALU.subtract).then_inc(rT_ready, 1)

            def low_hidden(s):
                for a in range(2):
                    dve.wait_ge(hT_hi_ready, 2 * s + a + 1)
                    nc.vector.tensor_tensor(hT_lo[:, 4 * a:4 * a + 4, :], ht_ps[:, a, :, :],
                                            hT_hi[:, 4 * a:4 * a + 4, :].bitcast(F32), ALU.subtract).then_inc(hT_ready, 1)

            def bias_hidden(s):
                at = from_table(dve, b1_at, s, (RING - 1) * H)
                ats = [dve.snap(at + 512 * a) for a in range(2)]
                for a in range(2):
                    dve.wait_ge(h_full, 2 * s + a + 1)
                    nc.vector.tensor_tensor(hid[:, 512 * a:512 * a + 512], h_ps[:, a, :], b1_all[:, bass.ds(ats[a], 512)], ALU.add).then_inc(h_biased, 1)

            def outputs(s, j):
                at = from_table(dve, b2_at, s, (RING - 1) * D)
                if not (isinstance(s, int) and s < 2):
                    dve.wait_ge(y_stored[j], (s // 2) * 16 if isinstance(s, int) else s * 8 - 8 * j)
                dve.wait_ge(yo_full, s + 1)
                nc.vector.tensor_tensor(y[:, j, :], yo_ps[:, 0:D], b2_all[:, bass.ds(at, D)], ALU.add).then_inc(y_ready, 1)

            def step(s, j, more=True):
                bias_hidden(s)
                if more:
                    low_inputs(s + 1 if isinstance(s, int) else dve.snap(s + 1))
                if not (isinstance(s, int) and s == 0):
                    outputs(s - 1 if isinstance(s, int) else dve.snap(s - 1), 1 - j)
                low_hidden(s)

            def places_out():
                link(nc.vector.tensor_tensor(move[:, :], ends[:, :], tiles[:, :], ALU.subtract))
                link(nc.vector.scalar_tensor_tensor(out=move[:, :], in0=move[:, :], scalar=float(P), in1=regions[:, :],
                                                    op0=ALU.mult, op1=ALU.subtract))
                link(nc.vector.tensor_copy(move_step[:, 0:1], move[:, 0:1]))
                link(nc.vector.tensor_tensor(move_step[:, 1:E], move[:, 1:E], move[:, 0:E - 1], ALU.subtract))
                flat = places_all[:, :, :, :].rearrange("p g t k -> p (g t k)")
                link(nc.vector.tensor_copy(place_in[:, :], flat))
                link(nc.vector.tensor_tensor(beyond[:, :, :], place_in[:, :].unsqueeze(2).to_broadcast([P, 2 * B, E]),
                                             regions[:, :].unsqueeze(1).to_broadcast([P, 2 * B, E]), ALU.is_ge))
                link(nc.vector.tensor_tensor(beyond[:, :, :], beyond[:, :, :],
                                             move_step[:, :].unsqueeze(1).to_broadcast([P, 2 * B, E]), ALU.mult))
                link(nc.vector.tensor_reduce(moved[:, :], beyond[:, :, :], AX_X, ALU.add))
                nc.vector.tensor_tensor(flat, place_in[:, :], moved[:, :], ALU.add)

            low_inputs(0)
            step(0, 0)
            step(1, 1)
            places_out()
            step(2, 0)
            with dve.Fori(1, SLOTS // 2 - 1) as i:
                step(dve.snap(i * 2 + 1), 1)
                step(dve.snap(i * 2 + 2), 0)
            step(SLOTS - 1, 1, False)
            outputs(SLOTS - 1, 1)

        @block.tensor
        def _(pe):
            mm, tr = nc.tensor.matmul, nc.tensor.transpose
            mm(n_ps[:, 0:E], ones_b[:, :], chosen_sum[:, :], start=True, stop=True).then_inc(counted, 1)

            def three(out, a_hi, a_lo, b_hi, b_lo, start, stop):
                mm(out, a_hi, b_hi, start=start, stop=False)
                mm(out, a_hi, b_lo, start=False, stop=False)
                return mm(out, a_lo, b_hi, start=False, stop=stop)

            def transpose_inputs(s, j):
                pe.wait_ge(tile_in[j], (s // 2 + 1) * 16 if isinstance(s, int) else s * 8 + (16 - 8 * j))
                for k in range(KD):
                    i = tr(rt_ps[:, k, :], tile[:, j, k * P:k * P + P], ident[:, :])
                i.then_inc(rt_full, 1)

            def hidden(s):
                at = from_table(pe, w_at, s, (RING - 1) * WIDE)
                needed = from_table(pe, need, s, E, 1)
                ats = [pe.snap(at + 512 * n) for n in range(4)]
                pe.wait_ge(w1_ready, needed)
                pe.wait_ge(rT_ready, s + 1)
                for a in range(2):
                    if not (isinstance(s, int) and s == 0):
                        pe.wait_ge(h_biased, 2 * s + a - 1)
                    for k in range(KD):
                        cols = bass.ds(ats[2 * k + a], 512)
                        i = three(h_ps[:, a, :], rT_hi[:, k, :], rT_lo[:, k, :], w1_hi[:, cols], w1_lo[:, cols], k == 0, k == KD - 1)
                    i.then_inc(h_full, 1)

            def transpose_hidden(s):
                for a in range(2):
                    pe.wait_ge(h_ready, 2 * s + a + 1)
                    for k in range(4):
                        i = tr(ht_ps[:, a, k, :], hid[:, (4 * a + k) * P:(4 * a + k) * P + P], ident[:, :])
                    i.then_inc(ht_full, 1)

            def outputs(s):
                at = from_table(pe, w_at, s, (RING - 1) * WIDE)
                needed = from_table(pe, need, s, E, 1)
                ats = [pe.snap(at + D * k) for k in range(KH)]
                pe.wait_ge(w2_ready, needed)
                if not (isinstance(s, int) and s == 0):
                    pe.wait_ge(y_ready, s + 1)
                for k in range(KH):
                    if k % 4 == 0:
                        pe.wait_ge(hT_ready, 2 * s + 1 + k // 4)
                    cols = bass.ds(ats[k], D)
                    i = three(yo_ps[:, 0:D], hT_hi[:, k, :], hT_lo[:, k, :], w2_hi[:, cols], w2_lo[:, cols], k == 0, k == KH - 1)
                i.then_inc(yo_full, 1)

            def step(s, j):
                hidden(s)
                if not (isinstance(s, int) and s == SLOTS - 1):
                    transpose_inputs(s + 1 if isinstance(s, int) else pe.snap(s + 1), 1 - j)
                if not (isinstance(s, int) and s == 0):
                    outputs(s - 1 if isinstance(s, int) else pe.snap(s - 1))
                transpose_hidden(s)

            transpose_inputs(0, 0)
            pe.wait_ge(slots_ready, 1)
            step(0, 0)
            with pe.Fori(0, SLOTS // 2 - 1) as i:
                step(pe.snap(i * 2 + 1), 1)
                step(pe.snap(i * 2 + 2), 0)
            step(SLOTS - 1, 1)
            outputs(SLOTS - 1)


def combine(nc, x2_dram, z_dram, routed_out, gamma, beta, places_all, weights_all, cells, out):
    with ExitStack() as ctx:
        def sb(name, shape, dt=F32):
            return ctx.enter_context(nc.sbuf_tensor(name, shape, dt))

        def sem(name):
            return ctx.enter_context(nc.semaphore(name))

        gamma_all, beta_all = sb("gamma_all", [P, D]), sb("beta_all", [P, D])
        rows = sb("rows", [P, 2, GB, 2], U32)
        y = sb("y_rows", [P, 2, GB, 2, D])
        z, x2 = sb("z_rows", [P, 2, GB, D]), sb("x2_rows", [P, 2, GB, D])
        r = sb("r", [P, 2, GB, D])
        normed, result = sb("normed", [P, 2, GB, D]), sb("result", [P, 2, GB, D])
        stats, mv = sb("stats2", [P, GB, 6]), sb("mv2", [P, GB, 2])
        tmp = sb("tmp2", [P, 2 * GB])
        rstd, shift = sb("rstd", [P, 2, GB]), sb("shift", [P, 2, GB])

        params_in, chain = sem("params_in"), sem("combine_chain")
        z_in, x2_in, y_in = [sem("z0_in"), sem("z1_in")], [sem("x20_in"), sem("x21_in")], [sem("y0_in"), sem("y1_in")]
        rows_ready, summed = sem("rows_ready"), sem("summed")
        norm_ready, normed_ready, result_ready = sem("norm_ready"), sem("normed_ready"), sem("result_ready")
        x2_beta_ready = sem("x2_beta_ready")
        out_stored = [sem("out0_stored"), sem("out1_stored")]

        block = ctx.enter_context(nc.Block())

        @block.sync
        def _(sp):
            sp.dma_start(gamma_all[:, :], gamma.rearrange("(a n) -> a n", a=1).to_broadcast([P, D])).then_inc(params_in, 16)
            sp.dma_start(beta_all[:, :], beta.rearrange("(a n) -> a n", a=1).to_broadcast([P, D])).then_inc(params_in, 16)

            def load(g, j):
                row = g * GT if isinstance(g, int) else sp.snap(g * GT)
                if not isinstance(g, int):
                    sp.wait_ge(result_ready, g - 1)
                sp.dma_start(z[:, j, :, :], z_dram[bass.ds(row, GT), :].rearrange("(b p) d -> p b d", p=P)).then_inc(z_in[j], 16)
                sp.dma_start(x2[:, j, :, :], x2_dram[bass.ds(row, GT), :].rearrange("(b p) d -> p b d", p=P)).then_inc(x2_in[j], 16)

            def store(g, j):
                at = g * GB if isinstance(g, int) else sp.snap(g * GB)
                sp.wait_ge(result_ready, g + 1)
                sp.dma_start(out[bass.ds(at, GB), :, :].rearrange("b p d -> p b d"), result[:, j, :, :]).then_inc(out_stored[j], 16)

            load(0, 0)
            load(1, 1)
            with sp.Fori(1, NG // 2) as i:
                for j in range(2):
                    g = sp.snap(i * 2 + j)
                    before = sp.snap(g - 2)
                    load(g, j)
                    store(before, j)
            store(NG - 2, 0)
            store(NG - 1, 1)
            sp.wait_ge(out_stored[0], 16 * (NG // 2))
            sp.wait_ge(out_stored[1], 16 * (NG // 2))

        @block.gpsimd
        def _(pool):
            def gather(g, j):
                pool.wait_ge(rows_ready, g + 1)
                if not isinstance(g, int):
                    pool.wait_ge(summed, g - 1)
                    carry(pool, cells[:, 8 + j, :])
                for b in range(GB):
                    for k in range(2):
                        pool.indirect_dma_start(
                            out=y[:, j, b, k, :], out_offset=None, in_=routed_out,
                            in_offset=bass.IndirectOffsetOnAxis(ap=rows[:, j, b, k:k + 1], axis=0)).then_inc(y_in[j], 16)

            def add_beta(g, j):
                pool.wait_ge(params_in, 32)
                pool.wait_ge(x2_in[j], (g // 2 + 1) * 16 if isinstance(g, int) else g * 8 + (16 - 8 * j))
                pool.tensor_tensor(x2[:, j, :, :], x2[:, j, :, :], beta_all[:, :].unsqueeze(1).to_broadcast([P, GB, D]), ALU.add).then_inc(x2_beta_ready, 1)

            gather(0, 0)
            gather(1, 1)
            with pool.Fori(1, NG // 2) as i:
                gather(pool.snap(i * 2), 0)
                add_beta(pool.snap(i * 2 - 2), 0)
                gather(pool.snap(i * 2 + 1), 1)
                add_beta(pool.snap(i * 2 - 1), 1)
            add_beta(NG - 2, 0)
            add_beta(NG - 1, 1)

        @block.scalar
        def _(act):
            def group(g, j):
                act.wait_ge(norm_ready, g + 1)
                if not (isinstance(g, int) and g < 2):
                    act.wait_ge(result_ready, g - 1)
                for b in range(GB):
                    i = nc.scalar.activation(normed[:, j, b, :], r[:, j, b, :], ACT.Identity, scale=rstd[:, j, b:b + 1], bias=shift[:, j, b:b + 1])
                i.then_inc(normed_ready, 1)

            group(0, 0)
            group(1, 1)
            with act.Fori(1, NG // 2) as i:
                group(act.snap(i * 2), 0)
                group(act.snap(i * 2 + 1), 1)

        @block.vector
        def _(dve):
            def take_rows(g, j):
                at = g if isinstance(g, int) else dve.snap(g)
                nc.vector.tensor_copy(rows[:, j, :, :], places_all[:, bass.ds(at, 1), :, :].rearrange("p g t k -> p (g t) k")).then_inc(rows_ready, 1)

            def add_up(g, j, link):
                fixed = isinstance(g, int)
                if not (fixed and g < 2):
                    dve.wait_ge(normed_ready, g - 1)
                dve.wait_ge(z_in[j], (g // 2 + 1) * 16 if fixed else g * 8 + (16 - 8 * j))
                dve.wait_ge(y_in[j], (g // 2 + 1) * (32 * GB) if fixed else g * (16 * GB) + (32 - 16 * j) * GB)
                for k in range(2):
                    for b in range(GB):
                        w = weights_all[:, bass.ds(g, 1), b:b + 1, k:k + 1].rearrange("p g t k -> p (g t k)")
                        i = nc.vector.scalar_tensor_tensor(out=r[:, j, b, :], in0=y[:, j, b, k, :], scalar=w,
                                                           in1=(z if k == 0 else r)[:, j, b, :], op0=ALU.mult, op1=ALU.add)
                    link(i)
                for b in range(GB):
                    i = nc.vector.bn_stats(stats[:, b, :], r[:, j, b, :])
                i.then_inc(summed, 1)
                dve.wait_ge(summed, g + 1)
                carry(nc.vector, cells[:, 10, :])
                for b in range(GB):
                    i = nc.vector.bn_aggr(mv[:, b, :], stats[:, b, :])
                link(i)

            def scale(g, j, link):
                rsqrt_and_shift(nc, link, mv, tmp, rstd[:, j, :], shift[:, j, :]).then_inc(norm_ready, 1)

            def finish(g, j, link):
                if not (isinstance(g, int) and g < 2):
                    dve.wait_ge(out_stored[j], g * 8 - 8 * j)
                dve.wait_ge(x2_beta_ready, g + 1)
                dve.wait_ge(normed_ready, g + 1)
                link(nc.vector.tensor_tensor(normed[:, j, :, :], normed[:, j, :, :], gamma_all[:, :].unsqueeze(1).to_broadcast([P, GB, D]), ALU.mult))
                nc.vector.tensor_tensor(result[:, j, :, :], normed[:, j, :, :], x2[:, j, :, :], ALU.add).then_inc(result_ready, 1)

            def step(g, j, link, ahead=True):
                add_up(g, j, link)
                if ahead:
                    take_rows(g + 2, j)
                if not (isinstance(g, int) and g == 0):
                    finish(g - 1 if isinstance(g, int) else dve.snap(g - 1), 1 - j, link)
                scale(g, j, link)

            take_rows(0, 0)
            take_rows(1, 1)
            dve.wait_ge(params_in, 32)
            link = Links(dve, chain)
            step(0, 0, link)
            step(1, 1, link)
            step(2, 0, link)
            with dve.Fori(1, NG // 2 - 2) as i:
                link = Links(dve, chain, i * (2 * STEP_LINKS) + (STEP_LINKS - 1))
                step(dve.snap(i * 2 + 1), 1, link)
                step(dve.snap(i * 2 + 2), 0, link)
                assert link.n == 2 * STEP_LINKS
            link = Links(dve, chain, (NG - 3) * STEP_LINKS - 1)
            step(NG - 3, 1, link)
            step(NG - 2, 0, link, False)
            step(NG - 1, 1, link, False)
            finish(NG - 1, 1, link)


STEP_LINKS = 16


_INS = ["x", "ctx_768", "L0_xattn_Wq", "L0_xattn_Wk", "L0_xattn_Wv", "L0_xattn_Wo", "L0_xattn_bo", "L0_ffn_Wg",
        "L0_ffn_bg", "L0_ffn_W1", "L0_ffn_b1", "L0_ffn_W2", "L0_ffn_b2", "L0_ffn_gamma", "L0_ffn_beta"]


def kernel(**inputs):
    import numpy as _np
    import concourse.bacc as _bacc
    from concourse.bass_utils import run_bass_kernel_spmd as _run

    nc = _bacc.Bacc("TRN2", target_bir_lowering=False, num_devices=1)
    arrays, args = {}, []
    for name in _INS:
        a = _np.ascontiguousarray(inputs[name])
        arrays[f"in_{name}"] = a
        args.append(nc.dram_tensor(f"in_{name}", a.shape, mybir.dt.from_np(a.dtype), kind="ExternalInput").ap())
    args.append(nc.dram_tensor("out_0", (B, P, D), F32, kind="ExternalOutput").ap())
    build(nc, *args)
    r = _run(nc, [arrays], core_ids=[0])
    return r.results[0]["out_0"]
```

```python
from contextlib import ExitStack

import concourse.bass as bass
from concourse import mybir

F32 = mybir.dt.float32
F32R = mybir.dt.float32r
BF16 = mybir.dt.bfloat16
I32 = mybir.dt.int32
U32 = mybir.dt.uint32
ALU = mybir.AluOpType
ACT = mybir.ActivationFunctionType
AX_X = mybir.AxisListType.X

P = 128
B, D, DC = 32, 256, 192
HEADS, DH = 16, 64
INNER = HEADS * DH
GB = 4
GT = GB * P
NG = B // GB
NM = INNER // P
KD = D // P
E, H = 8, 1024
KH = H // P
REGION = B * P + P
SLOTS = (2 * B * P + E * (P - 1)) // P + 1
RING = 2
WIDE = KD * H
TILE_BITS = 7
assert KD * H == KH * D and 1 << TILE_BITS == P
EPS = 1e-5
CELLS = 16
RSQRT_SEED = 0x5F3759DF


def pair_bank_order(gate):
    order = [f"v{j}" for j in range(2 * GB)] + ["q0", "k0", "q1", "k1"]
    for m in range(NM):
        if gate and m != RANK_STEP:
            order += ROUTING_STEPS.get(m, [])
        if m >= 2:
            order.append(f"o{m - 2}")
        if gate and m == RANK_STEP:
            order += ROUTING_STEPS[m]
        if m < NM - 2:
            order += [f"q{m + 2}", f"k{m + 2}"]
    return order + [f"o{NM - 2}", f"o{NM - 1}"]


Z_STEP, LOGITS_STEP, RANK_STEP = 1, 3, 5
ROUTING_STEPS = {Z_STEP: ["z0", "z1"], LOGITS_STEP: ["logits"], RANK_STEP: ["rank"]}
EARLY = range(6)
LATE = range(6, NM)
X_AT = 6
SCATTER_STEPS = {5: [(0, 0), (0, 1)], 6: [(1, 0), (1, 1), (2, 0)], 7: [(2, 1), (3, 0), (3, 1)]}
FIRST, LATER, LAST = pair_bank_order(False), pair_bank_order(True), ["z0", "z1", "logits", "rank"]
assert len(FIRST) % 2 == 0 and len(LATER) % 2 == 0


def pair_bank(name, g):
    if isinstance(g, int) and g == 0:
        at, before = FIRST.index(name), 0
    elif isinstance(g, int) and g == NG:
        at, before = LAST.index(name), len(FIRST) // 2 + (NG - 1) * (len(LATER) // 2)
    else:
        at, before = LATER.index(name), g * (len(LATER) // 2) + (len(FIRST) - len(LATER)) // 2
    return at % 2, before + at // 2


def is_first(g):
    return isinstance(g, int) and g == 0


def build(nc, x, ctx_in, Wq, Wk, Wv, Wo, bo, Wg, bg, W1, b1, W2, b2, gamma, beta, out):
    x2_dram = nc.dram_tensor("x2_dram", (B * P, D), F32).ap()
    z_dram = nc.dram_tensor("z_dram", (B * P, D), F32).ap()
    routed_in = nc.dram_tensor("routed_in", (E * REGION + P, D), F32).ap()
    routed_out = nc.dram_tensor("routed_out", (SLOTS * P, D), F32).ap()

    with ExitStack() as whole:
        def keep(name, shape, dt):
            return whole.enter_context(nc.sbuf_tensor(name, shape, dt))

        ident = keep("ident", [P, P], F32)
        places_all = keep("places_all", [P, NG, GB, 2], U32)
        cells = keep("cells", [P, CELLS, 2], F32)
        weights_all = keep("weights_all", [P, NG, GB, 2], F32)
        chosen_sum = keep("chosen_sum", [P, E], BF16)
        ones_b = keep("ones_b", [P, P], BF16)

        attention(nc, x, ctx_in, Wq, Wk, Wv, Wo, bo, Wg, bg, x2_dram, z_dram, routed_in,
                  ident, places_all, weights_all, chosen_sum, ones_b, cells)
        experts(nc, W1, b1, W2, b2, routed_in, routed_out, ident, places_all, chosen_sum, ones_b, cells)
        combine(nc, x2_dram, z_dram, routed_out, gamma, beta, places_all, weights_all, cells, out)


def carry(eng, cell):
    return eng.tensor_tensor(cell[:, 0:1], cell[:, 1:2], cell[:, 1:2], ALU.add)


class Links:

    def __init__(self, eng, sem, before=0):
        self.eng, self.sem, self.before, self.n = eng, sem, before, 0

    def __call__(self, ins):
        self.n += 1
        ins.then_inc(self.sem, 1)
        self.eng.wait_ge(self.sem, self.before + self.n)


def rsqrt_and_shift(nc, link, mv, t, rstd, shift):
    v, a = t[:, 0:GB], t[:, GB:2 * GB]
    link(nc.vector.tensor_scalar(v, mv[:, :, 1], EPS, None, ALU.add))
    link(nc.vector.tensor_scalar(a.bitcast(I32), v.bitcast(I32), 1, None, ALU.logical_shift_right))
    link(nc.vector.tensor_scalar(rstd.bitcast(I32), a.bitcast(I32), -1.0, float(RSQRT_SEED),
                                 ALU.mult, ALU.add))
    for _ in range(3):
        link(nc.vector.scalar_tensor_tensor(out=a, in0=rstd, scalar=-0.5, in1=rstd,
                                            op0=ALU.mult, op1=ALU.mult))
        link(nc.vector.tensor_tensor(a, a, v, ALU.mult))
        link(nc.vector.scalar_tensor_tensor(out=rstd, in0=a, scalar=1.5, in1=rstd,
                                            op0=ALU.add, op1=ALU.mult))
    return nc.vector.scalar_tensor_tensor(out=shift, in0=mv[:, :, 0], scalar=-1.0, in1=rstd,
                                          op0=ALU.mult, op1=ALU.mult)


def attention(nc, x, ctx_in, Wq, Wk, Wv, Wo, bo, Wg, bg, x2_dram, z_dram, routed_in,
              ident, places_all, weights_all, chosen_sum, ones_b, cells):
    with ExitStack() as ctx:
        def sb(name, shape, dt=F32):
            return ctx.enter_context(nc.sbuf_tensor(name, shape, dt))

        def psum(name, shape):
            return ctx.enter_context(nc.psum_tensor(name, shape, F32))

        def sem(name):
            return ctx.enter_context(nc.semaphore(name))

        stage = sb("stage", [P, 2, 2048])
        wq_hi, wq_lo = sb("wq_hi", [P, KD, INNER], F32R), sb("wq_lo", [P, KD, INNER], F32R)
        wk_hi, wk_lo = sb("wk_hi", [P, INNER], F32R), sb("wk_lo", [P, INNER], F32R)
        wv_hi, wv_lo = sb("wv_hi", [P, INNER], F32R), sb("wv_lo", [P, INNER], F32R)
        wk_end, wv_end = sb("wk_end", [P, INNER], F32R), sb("wv_end", [P, INNER], F32R)
        wo_hi, wo_lo = sb("wo_hi", [P, NM, D], F32R), sb("wo_lo", [P, NM, D], F32R)
        wg = sb("wg", [P, KD, E])
        bo_all, bg_all = sb("bo_all", [P, D]), sb("bg_all", [P, E])
        before = sb("before", [P, P], BF16)
        expert_no = sb("expert_no", [P, E])
        region_at = sb("region_at", [P, E])

        xin, xn = sb("xin", [P, GB, D]), sb("xn", [P, GB, D])
        x_bo = sb("x_bo", [P, GB, D])
        cin = sb("cin", [P, GB, 2 * P])
        xT_hi, xT_lo = sb("xT_hi", [P, KD, GT], F32R), sb("xT_lo", [P, KD, GT], F32R)
        cT_hi, cT_lo = sb("cT_hi", [P, GT], F32R), sb("cT_lo", [P, GT], F32R)
        cT_end_hi, cT_end_lo = sb("cT_end_hi", [P, GT], F32R), sb("cT_end_lo", [P, GT], F32R)
        qT, kT = sb("qT", [P, 2, GT]), sb("kT", [P, 2, GT])
        v = sb("v", [P, GB, INNER])
        probs = sb("probs", [P, 2, 2, GB, P])
        probsT = sb("probsT", [P, 2, 2, GB, P])
        oT_hi, oT_lo = sb("oT_hi", [P, NM, GT], F32R), sb("oT_lo", [P, NM, GT], F32R)
        x2, z, zT = sb("x2", [P, GB, D]), sb("z", [P, GB, D]), sb("zT", [P, KD, GT])

        stats, mv = sb("stats", [P, GB, 6]), sb("mv", [P, GB, 2])
        tmp = sb("tmp", [P, 2 * GB])
        rstd1, shift1 = sb("rstd1", [P, GB]), sb("shift1", [P, GB])
        rstd2, shift2 = sb("rstd2", [P, GB]), sb("shift2", [P, GB])
        row_max = sb("row_max", [P, 2, GB])
        row_sum, row_rec = sb("row_sum", [P, 2, GB]), sb("row_rec", [P, 2, GB])
        logits = sb("logits", [P, GB, E])
        best, best_at = sb("best", [P, GB, 8]), sb("best_at", [P, GB, 8], U32)
        best_f = sb("best_f", [P, GB, 2])
        picks = sb("picks", [P, GB, 2, E])
        chosen = sb("chosen", [P, GB, E], BF16)
        sums = sb("sums", [P, GB, E], BF16)
        place = sb("place", [P, GB, E])
        place2 = sb("place2", [P, GB, 2, E])
        place_f = sb("place_f", [P, GB, 2])
        places = sb("places", [P, GB, 2], U32)
        gap, odds, p_best = sb("gap", [P, GB]), sb("odds", [P, GB]), sb("p_best", [P, GB, 2])

        s_ps = psum("s_ps", [P, 2, 2, GB, P])
        t_ps = psum("t_ps", [P, 2, GB, P])
        t_flat = t_ps[:, :, :, :].rearrange("p a b k -> p a (b k)")
        pair = psum("pair", [P, 2, 512])
        y_ps = s_ps[:, :, :, :, :].rearrange("p u a b k -> p (u a) (b k)")

        w_in = [sem(f"w_in{n}") for n in range(4)]
        w_hi, w_ready = sem("w_hi"), sem("w_ready")
        small_in = sem("small_in")
        x_in, c_in, x_used = sem("x_in"), sem("c_in"), sem("x_used")
        const_step, const_ready = sem("const_step"), sem("const_ready")
        chain = sem("chain")
        norm1_ready, xn_ready, norm2_ready, z_ready = sem("norm1_ready"), sem("xn_ready"), sem("norm2_ready"), sem("z_ready")
        full = [sem("pair0_full"), sem("pair1_full")]
        free = [sem("pair0_free"), sem("pair1_free")]
        c_full, x_full, cT_ready, xT_ready = sem("c_full"), sem("x_full"), sem("cT_ready"), sem("xT_ready")
        cT_hi_ready, xT_hi_ready, oT_hi_ready = sem("cT_hi_ready"), sem("xT_hi_ready"), sem("oT_hi_ready")
        s_full, shifted, p_ready = sem("s_full"), sem("shifted"), sem("p_ready")
        expd, rec_ready, t_full, pT_ready = sem("expd"), sem("rec_ready"), sem("t_full"), sem("pT_ready")
        y_full, x2_ready = sem("y_full"), sem("x2_ready")
        x2_stored, z_stored, scattered = sem("x2_stored"), sem("z_stored"), sem("scattered")
        chosen_ready, places_ready, gap_ready, odds_ready = sem("chosen_ready"), sem("places_ready"), sem("gap_ready"), sem("odds_ready")

        block = ctx.enter_context(nc.Block())

        def take(eng, name, g):
            b, n = pair_bank(name, g)
            if not (isinstance(n, int) and n == 0):
                eng.wait_ge(free[b], n)
            return b

        def filled(eng, name, g):
            b, n = pair_bank(name, g)
            eng.wait_ge(full[b], n + 1)
            return b

        def drained(eng, name, g, taken=None):
            b, n = pair_bank(name, g)
            if b != taken:
                eng.wait_ge(free[b], n + 1)

        @block.sync
        def _(sp):
            def load_x(g):
                sp.dma_start(xin[:, :, :], x[bass.ds(g * GB, GB), :, :].rearrange("b p d -> p b d")).then_inc(x_in, 16)

            def load_c(g):
                src = ctx_in[bass.ds(g * GB, GB), :, :]
                sp.dma_start(cin[:, :, 0:DC], src.rearrange("b p d -> p b d")).then_inc(c_in, 16)
                sp.dma_start(cin[:, :, DC:2 * P], src[:, :, P:DC].rearrange("b p d -> p b d")).then_inc(c_in, 16)

            load_c(0)
            load_x(0)
            with sp.Fori(1, NG) as g:
                row = sp.snap(g * (GB * P) - GB * P)
                sp.wait_ge(cT_hi_ready, 2 * g)
                load_c(g)
                sp.wait_ge(x_used, g)
                load_x(g)
                sp.wait_ge(x2_ready, GB * g)
                sp.dma_start(x2_dram[bass.ds(row, GT), :].rearrange("(b p) d -> p b d", p=P), x2[:, :, :]).then_inc(x2_stored, 16)
                sp.wait_ge(z_ready, g)
                sp.dma_start(z_dram[bass.ds(row, GT), :].rearrange("(b p) d -> p b d", p=P), z[:, :, :]).then_inc(z_stored, 16)
            sp.wait_ge(x2_ready, GB * NG)
            last = (NG - 1) * GT
            sp.dma_start(x2_dram[last:last + GT, :].rearrange("(b p) d -> p b d", p=P), x2[:, :, :]).then_inc(x2_stored, 16)
            sp.wait_ge(z_ready, NG)
            sp.dma_start(z_dram[last:last + GT, :].rearrange("(b p) d -> p b d", p=P), z[:, :, :]).then_inc(z_stored, 16)
            sp.wait_ge(x2_stored, 16 * NG)
            sp.wait_ge(z_stored, 16 * NG)

        @block.gpsimd
        def _(pool):
            pool.memset(ident[:, :], 0.0).then_inc(const_step, 1)
            pool.memset(before[:, :], 1.0).then_inc(const_step, 1)
            pool.memset(cells[:, :, :], 0.0).then_inc(const_ready, 1)
            pool.memset(ones_b[:, :], 1.0).then_inc(const_ready, 1)
            pool.iota(expert_no[:, :], [[1, E]], base=0, channel_multiplier=0,
                      allow_small_or_imprecise_dtypes=True).then_inc(const_ready, 1)
            pool.iota(region_at[:, :], [[REGION, E]], base=0, channel_multiplier=0,
                      allow_small_or_imprecise_dtypes=True).then_inc(const_ready, 1)
            pool.memset(chosen_sum[:, :], 0.0).then_inc(const_ready, 1)
            pool.wait_ge(const_step, 2)
            pool.affine_select(out=ident[:, :], in_=ident[:, :], compare_op=ALU.not_equal, fill=1.0,
                               base=0, pattern=[[-1, P]], channel_multiplier=1).then_inc(const_ready, 1)
            pool.affine_select(out=before[:, :], in_=before[:, :], compare_op=ALU.is_gt, fill=0.0,
                               base=0, pattern=[[1, P]], channel_multiplier=-1).then_inc(const_ready, 1)
            pool.wait_ge(small_in, 16 * 3)
            pool.wait_ge(const_ready, 7)

            def group(g):
                pool.wait_ge(norm1_ready, g + 1)
                if not is_first(g):
                    pool.wait_ge(xT_hi_ready, g * 2)
                    carry(pool, cells[:, 0, :])
                for b in range(GB):
                    last = pool.tensor_scalar(xn[:, b, :], xin[:, b, :], rstd1[:, b:b + 1], shift1[:, b:b + 1], ALU.mult, ALU.add)
                last.then_inc(xn_ready, 1)

            def residual(g):
                if not is_first(g):
                    pool.wait_ge(x2_ready, GB * g)
                pool.tensor_tensor(x_bo[:, :, :], xin[:, :, :], bo_all[:, :].unsqueeze(1).to_broadcast([P, GB, D]),
                                   ALU.add).then_inc(x_used, 1)

            def normalise_out(g):
                pool.wait_ge(norm2_ready, g)
                if not (isinstance(g, int) and g == 1):
                    pool.wait_ge(z_stored, 16 * g - 16)
                    pool.wait_ge(scattered, (16 * 2 * GB) * g - 16 * 2 * GB)
                    carry(pool, cells[:, 1, :])
                for b in range(GB):
                    last = pool.tensor_scalar(z[:, b, :], x2[:, b, :], rstd2[:, b:b + 1], shift2[:, b:b + 1], ALU.mult, ALU.add)
                last.then_inc(z_ready, 1)

            def scatter(g, picks):
                if picks[0] == (0, 0):
                    pool.wait_ge(places_ready, g)
                    carry(pool, cells[:, 2, :])
                for b, k in picks:
                    pool.indirect_dma_start(
                        out=routed_in, out_offset=bass.IndirectOffsetOnAxis(ap=places[:, b, k:k + 1], axis=0),
                        in_=z[:, b, :], in_offset=None).then_inc(scattered, 16)

            def steps(g, ms):
                for m in ms:
                    for a in range(2):
                        pool.wait_ge(rec_ready, g * (2 * NM) + 2 * m + a + 1)
                        pool.tensor_tensor(probs[:, m % 2, a, :, :], probs[:, m % 2, a, :, :],
                                           row_rec[:, a, :].unsqueeze(2).to_broadcast([P, GB, P]), ALU.mult).then_inc(p_ready, 1)
                    if m in SCATTER_STEPS and not is_first(g):
                        scatter(g, SCATTER_STEPS[m])

            def turn(g):
                steps(g - 1 if isinstance(g, int) else pool.snap(g - 1), LATE)
                group(g)
                normalise_out(g)
                residual(g)
                steps(g, EARLY)

            group(0)
            residual(0)
            steps(0, EARLY)
            turn(1)
            with pool.Fori(2, NG) as g:
                turn(g)
            steps(NG - 1, LATE)
            normalise_out(NG)
            scatter(NG, [(b, k) for b in range(GB) for k in range(2)])
            pool.wait_ge(scattered, 16 * 2 * GB * NG)

        @block.scalar
        def _(act):
            def halves(n):
                return stage[:, n % 2, 0:INNER], stage[:, n % 2, INNER:2 * INNER]

            act.dma_start(stage[:, 0, 0:INNER], Wv[0:P, :]).then_inc(w_in[0], 16)
            act.dma_start(stage[0:DH, 0, INNER:], Wv[P:DC, :]).then_inc(w_in[0], 16)
            act.dma_start(stage[DH:P, 0, INNER:], Wv[P:DC, :]).then_inc(w_in[0], 16)
            act.dma_start(stage[:, 1, 0:INNER], Wk[0:P, :]).then_inc(w_in[1], 16)
            act.dma_start(stage[0:DH, 1, INNER:], Wk[P:DC, :]).then_inc(w_in[1], 16)
            act.dma_start(stage[DH:P, 1, INNER:], Wk[P:DC, :]).then_inc(w_in[1], 16)
            act.dma_start(bo_all[:, :], bo.rearrange("(a n) -> a n", a=1).to_broadcast([P, D])).then_inc(small_in, 16)
            act.dma_start(bg_all[:, :], bg.rearrange("(a n) -> a n", a=1).to_broadcast([P, E])).then_inc(small_in, 16)
            act.dma_start(wg[:, :, :], Wg.rearrange("(k p) e -> p k e", p=P)).then_inc(small_in, 16)
            for n, (hi, end) in enumerate(((wv_hi, wv_end), (wk_hi, wk_end))):
                act.wait_ge(w_in[n], 48)
                nc.scalar.activation(hi[:, :], halves(n)[0], ACT.Copy).then_inc(w_hi, 1)
                nc.scalar.activation(end[:, :], halves(n)[1], ACT.Copy).then_inc(w_hi, 1)
            act.wait_ge(w_ready, 1)
            act.dma_start(stage[:, 0, :].rearrange("p (k n) -> p k n", k=KD), Wq.rearrange("(k p) n -> p k n", p=P)).then_inc(w_in[2], 16)
            act.wait_ge(w_ready, 2)
            act.dma_start(stage[:, 1, :].rearrange("p (k n) -> p k n", k=NM), Wo.rearrange("(k p) n -> p k n", p=P)).then_inc(w_in[3], 16)
            act.wait_ge(w_in[2], 16)
            nc.scalar.activation(wq_hi[:, :, :].rearrange("p k n -> p (k n)"), stage[:, 0, :], ACT.Copy).then_inc(w_hi, 1)
            act.wait_ge(w_in[3], 16)
            nc.scalar.activation(wo_hi[:, :, :].rearrange("p k n -> p (k n)"), stage[:, 1, :], ACT.Copy).then_inc(w_hi, 1)

            def queries_keys(g, m):
                if not (is_first(g) and m < 2):
                    act.wait_ge(s_full, g * NM + m - 1)
                b = filled(act, f"q{m}", g)
                nc.scalar.activation(qT[:, m % 2, :], pair[:, b, :], ACT.Copy, scale=DH ** -0.5).then_inc(free[b], 1)
                b = filled(act, f"k{m}", g)
                nc.scalar.activation(kT[:, m % 2, :], pair[:, b, :], ACT.Copy).then_inc(free[b], 1)

            def group(g):
                for j in range(2 * GB):
                    if j == X_AT:
                        tokens_hi(g)
                    b = filled(act, f"v{j}", g)
                    nc.scalar.activation(v[:, j // 2, 512 * (j % 2):512 * (j % 2) + 512], pair[:, b, :], ACT.Copy).then_inc(free[b], 1)
                queries_keys(g, 0)
                queries_keys(g, 1)

            def inputs_hi(g):
                for k, hi in enumerate((cT_hi, cT_end_hi)):
                    act.wait_ge(c_full, 2 * g + k + 1)
                    nc.scalar.activation(hi[:, :], t_flat[:, k, :], ACT.Copy).then_inc(cT_hi_ready, 1)

            def tokens_hi(g):
                for k in range(KD):
                    act.wait_ge(x_full, KD * g + k + 1)
                    nc.scalar.activation(xT_hi[:, k, :], t_flat[:, k, :], ACT.Copy).then_inc(xT_hi_ready, 1)

            def steps(g, ms):
                gate = not is_first(g)
                for m in ms:
                    if gate and m == Z_STEP:
                        routed_tokens_out(g)
                    if m >= 2:
                        outputs_hi(g, m - 2)
                    exponentials(g, m, 0)
                    if m >= 1:
                        probs_out(g, m - 1)
                    exponentials(g, m, 1)
                    if m < NM - 2:
                        queries_keys(g, m + 2)
                    if gate and m == LOGITS_STEP + 1:
                        routing_odds(g)

            def exponentials(g, m, a):
                act.wait_ge(shifted, g * (2 * NM) + 2 * m + a + 1)
                nc.scalar.activation(probs[:, m % 2, a, :, :], probs[:, m % 2, a, :, :], ACT.Exp).then_inc(expd, 1)

            def end(g):
                outputs_hi(g, NM - 2)
                probs_out(g, NM - 1)
                outputs_hi(g, NM - 1)

            def probs_out(g, m):
                for a in range(2):
                    act.wait_ge(t_full, g * (2 * NM) + 2 * m + a + 1)
                    nc.scalar.activation(probsT[:, m % 2, a, :, :], t_ps[:, a, :, :], ACT.Copy).then_inc(pT_ready, 1)

            def outputs_hi(g, m):
                b = filled(act, f"o{m}", g)
                if m == 0 and not is_first(g):
                    act.wait_ge(x2_ready, GB * g)
                nc.scalar.activation(oT_hi[:, m, :], pair[:, b, :], ACT.Copy).then_inc(oT_hi_ready, 1)

            def routed_tokens_out(g):
                for k in range(KD):
                    b = filled(act, f"z{k}", g)
                    nc.scalar.activation(zT[:, k, :], pair[:, b, :], ACT.Copy).then_inc(free[b], 1)

            def routing_odds(g):
                act.wait_ge(gap_ready, g)
                nc.scalar.activation(odds[:, :], gap[:, :], ACT.Exp).then_inc(odds_ready, 1)

            inputs_hi(0)
            group(0)
            steps(0, EARLY)
            with act.Fori(1, NG) as g:
                last = act.snap(g - 1)
                steps(last, LATE)
                end(last)
                inputs_hi(g)
                group(g)
                steps(g, EARLY)
            steps(NG - 1, LATE)
            end(NG - 1)
            routed_tokens_out(NG)
            routing_odds(NG)

        @block.vector
        def _(dve):
            for n, (lo, hi, end) in enumerate(((wv_lo, wv_hi, wv_end), (wk_lo, wk_hi, wk_end))):
                dve.wait_ge(w_hi, 2 * n + 2)
                nc.vector.tensor_tensor(lo[:, :], stage[:, n, 0:INNER], hi[:, :].bitcast(F32), ALU.subtract)
                nc.vector.tensor_tensor(end[DH:P, :], stage[DH:P, n, INNER:], end[DH:P, :].bitcast(F32), ALU.subtract).then_inc(w_ready, 1)

            def late_weights():
                dve.wait_ge(w_hi, 5)
                nc.vector.tensor_tensor(wq_lo[:, :, :].rearrange("p k n -> p (k n)"), stage[:, 0, :],
                                        wq_hi[:, :, :].rearrange("p k n -> p (k n)").bitcast(F32), ALU.subtract).then_inc(w_ready, 1)
                dve.wait_ge(w_hi, 6)
                nc.vector.tensor_tensor(wo_lo[:, :, :].rearrange("p k n -> p (k n)"), stage[:, 1, :],
                                        wo_hi[:, :, :].rearrange("p k n -> p (k n)").bitcast(F32), ALU.subtract).then_inc(w_ready, 1)

            def statistics(link, src):
                for b in range(GB):
                    i = nc.vector.bn_stats(stats[:, b, :], src[:, b, :])
                link(i)
                carry(nc.vector, cells[:, 3, :])
                for b in range(GB):
                    i = nc.vector.bn_aggr(mv[:, b, :], stats[:, b, :])
                link(i)

            def norm1(g, link):
                dve.wait_ge(x_in, g * 16 + 16)
                if not is_first(g):
                    dve.wait_ge(xn_ready, g)
                statistics(link, xin)
                rsqrt_and_shift(nc, link, mv, tmp, rstd1[:, :], shift1[:, :]).then_inc(norm1_ready, 1)

            def norm2(g, link):
                dve.wait_ge(x2_ready, GB * g)
                if not (isinstance(g, int) and g == 1):
                    dve.wait_ge(z_ready, g - 1)
                statistics(link, x2)
                rsqrt_and_shift(nc, link, mv, tmp, rstd2[:, :], shift2[:, :]).then_inc(norm2_ready, 1)

            def outputs_lo(g, m):
                b = pair_bank(f"o{m}", g)[0]
                dve.wait_ge(oT_hi_ready, g * NM + m + 1)
                i = nc.vector.tensor_tensor(oT_lo[:, m, :], pair[:, b, :], oT_hi[:, m, :].bitcast(F32), ALU.subtract)
                i.then_inc(free[b], 1)

            def inputs_lo(g):
                for k, (lo, hi, rows) in enumerate(((cT_lo, cT_hi, P), (cT_end_lo, cT_end_hi, DH))):
                    dve.wait_ge(cT_hi_ready, 2 * g + k + 1)
                    nc.vector.tensor_tensor(lo[0:rows, :], t_flat[0:rows, k, :], hi[0:rows, :].bitcast(F32), ALU.subtract).then_inc(cT_ready, 1)

            def tokens_lo(g):
                for k in range(KD):
                    dve.wait_ge(xT_hi_ready, KD * g + k + 1)
                    nc.vector.tensor_tensor(xT_lo[:, k, :], t_flat[:, k, :], xT_hi[:, k, :].bitcast(F32), ALU.subtract).then_inc(xT_ready, 1)

            def steps(g, link, ms):
                gate = not is_first(g)
                for m in ms:
                    n = g * (2 * NM) + 2 * m
                    if gate and m == LOGITS_STEP:
                        routing_in(g, m)
                    dve.wait_ge(s_full, g * NM + m + 1)
                    if not (is_first(g) and m < 2):
                        dve.wait_ge(t_full, n - 2)
                    for a in range(2):
                        link(nc.vector.tensor_reduce(row_max[:, a, :], s_ps[:, m % 2, a, :, :], AX_X, ALU.max))
                        nc.vector.tensor_tensor(probs[:, m % 2, a, :, :], s_ps[:, m % 2, a, :, :],
                                                row_max[:, a, :].unsqueeze(2).to_broadcast([P, GB, P]), ALU.subtract).then_inc(shifted, 1)
                        if a == 0 and m >= 2:
                            outputs_lo(g, m - 2)
                    if gate and m == RANK_STEP:
                        routing_in(g, m)
                    for a in range(2):
                        dve.wait_ge(expd, n + a + 1)
                        if not (is_first(g) and m == 0):
                            dve.wait_ge(p_ready, n + a - 1)
                        link(nc.vector.tensor_reduce(row_sum[:, a, :], probs[:, m % 2, a, :, :], AX_X, ALU.add))
                        nc.vector.reciprocal(row_rec[:, a, :], row_sum[:, a, :]).then_inc(rec_ready, 1)
                    if gate:
                        routing(g, m, link)

            def end(g):
                outputs_lo(g, NM - 2)
                outputs_lo(g, NM - 1)

            def tokens_out(g):
                if not is_first(g):
                    dve.wait_ge(x2_stored, 16 * g)
                dve.wait_ge(x_used, g + 1)
                for b in range(GB):
                    dve.wait_ge(y_full, GB * g + b + 1)
                    nc.vector.tensor_tensor(x2[:, b, :], y_ps[:, b, 0:D], x_bo[:, b, :], ALU.add).then_inc(x2_ready, 1)

            def routing_in(g, m):
                for step, name, to, add in ((LOGITS_STEP, "logits", logits, bg_all), (RANK_STEP, "rank", place, region_at)):
                    if m == step:
                        b = filled(dve, name, g)
                        i = nc.vector.tensor_tensor(to[:, :, :], pair[:, b, 0:GB * E].rearrange("p (t e) -> p t e", e=E),
                                                    add[:, :].unsqueeze(1).to_broadcast([P, GB, E]), ALU.add)
                        i.then_inc(free[b], 1)

            def routing(g, m, link):
                if m == LOGITS_STEP:
                    drained(dve, "logits", g)
                    carry(nc.vector, cells[:, 4, :])
                    for t in range(GB):
                        i = nc.vector.max(best[:, t, :], logits[:, t, :])
                    link(i)
                    nc.vector.tensor_tensor(gap[:, :], best[:, :, 1], best[:, :, 0], ALU.subtract).then_inc(gap_ready, 1)
                    for t in range(GB):
                        i = nc.vector.max_index(best_at[:, t, :], best[:, t, :], logits[:, t, :])
                    link(i)
                    link(nc.vector.tensor_copy(best_f[:, :, :], best_at[:, :, 0:2]))
                    link(nc.vector.tensor_tensor(picks[:, :, :, :], expert_no[:, :].unsqueeze(1).unsqueeze(1).to_broadcast([P, GB, 2, E]),
                                                 best_f[:, :, :].unsqueeze(3).to_broadcast([P, GB, 2, E]), ALU.is_equal))
                    link(nc.vector.tensor_tensor(chosen[:, :, :], picks[:, :, 0, :], picks[:, :, 1, :], ALU.add))
                    link(nc.vector.tensor_copy(sums[:, 0, :], chosen_sum[:, :]))
                    for t in range(1, GB):
                        link(nc.vector.tensor_tensor(sums[:, t, :], sums[:, t - 1, :], chosen[:, t - 1, :], ALU.add))
                    i = nc.vector.tensor_tensor(chosen_sum[:, :], sums[:, GB - 1, :], chosen[:, GB - 1, :], ALU.add)
                    i.then_inc(chosen_ready, 1)
                if m == RANK_STEP:
                    drained(dve, "rank", g)
                    link(nc.vector.tensor_tensor(place2[:, :, :, :], picks[:, :, :, :],
                                                 place[:, :, :].unsqueeze(2).to_broadcast([P, GB, 2, E]), ALU.mult))
                    link(nc.vector.tensor_reduce(place_f[:, :, :], place2[:, :, :, :], AX_X, ALU.add))
                    if not (isinstance(g, int) and g == 1):
                        dve.wait_ge(scattered, (16 * 2 * GB) * g - 16 * 2 * GB)
                    i = nc.vector.tensor_copy(places[:, :, :], place_f[:, :, :])
                    i.then_inc(places_ready, 1)
                    nc.vector.tensor_copy(places_all[:, bass.ds(g - 1, 1), :, :].rearrange("p g t k -> p (g t) k"), place_f[:, :, :])
                    dve.wait_ge(odds_ready, g)
                    link(nc.vector.tensor_scalar(gap[:, :], odds[:, :], 1.0, None, ALU.add))
                    link(nc.vector.reciprocal(p_best[:, :, 0], gap[:, :]))
                    link(nc.vector.tensor_tensor(p_best[:, :, 1], p_best[:, :, 0], odds[:, :], ALU.mult))
                    link(nc.vector.tensor_copy(weights_all[:, bass.ds(g - 1, 1), :, :].rearrange("p g t k -> p (g t) k"), p_best[:, :, :]))

            def turn(g, last, link):
                steps(last, link, LATE)
                end(last)
                inputs_lo(g)
                norm1(g, link)
                tokens_out(last)
                tokens_lo(g)
                norm2(g, link)
                steps(g, link, EARLY)

            link = Links(dve, chain)
            dve.wait_ge(const_ready, 7)
            norm1(0, link)
            inputs_lo(0)
            tokens_lo(0)
            late_weights()
            steps(0, link, EARLY)
            turn(1, 0, link)
            first_links = link.n
            with dve.Fori(2, NG) as g:
                link = Links(dve, chain, g * LINKS_PER_GROUP + (first_links - 2 * LINKS_PER_GROUP))
                turn(g, dve.snap(g - 1), link)
                assert link.n == LINKS_PER_GROUP, link.n
            link = Links(dve, chain, first_links + (NG - 2) * LINKS_PER_GROUP)
            steps(NG - 1, link, LATE)
            end(NG - 1)
            tokens_out(NG - 1)
            norm2(NG, link)
            for m in (LOGITS_STEP, RANK_STEP):
                routing_in(NG, m)
                routing(NG, m, link)

        @block.tensor
        def _(pe):
            mm, tr = nc.tensor.matmul, nc.tensor.transpose

            def three(out, a_hi, a_lo, b_hi, b_lo, start, stop):
                mm(out, a_hi, b_hi, start=start, stop=False)
                mm(out, a_hi, b_lo, start=False, stop=False)
                return mm(out, a_lo, b_hi, start=False, stop=stop)

            def project_queries_keys(g, m):
                cols = slice(m * P, m * P + P)
                b = take(pe, f"q{m}", g)
                if m == 0:
                    pe.wait_ge(xT_ready, KD * g + KD)
                for k in range(KD):
                    i = three(pair[:, b, :], wq_hi[:, k, cols], wq_lo[:, k, cols], xT_hi[:, k, :], xT_lo[:, k, :], k == 0, k == KD - 1)
                i.then_inc(full[b], 1)
                b = take(pe, f"k{m}", g)
                three(pair[:, b, :], wk_hi[:, cols], wk_lo[:, cols], cT_hi[:, :], cT_lo[:, :], True, False)
                mm(pair[:, b, :], wk_end[:, cols], cT_end_hi[:, :], start=False, stop=False)
                i = mm(pair[:, b, :], wk_end[0:DH, cols], cT_end_lo[0:DH, :], start=False, stop=True)
                i.then_inc(full[b], 1)

            def scores(g, m):
                n = g * NM + m
                drained(pe, f"q{m}", g)
                drained(pe, f"k{m}", g)
                if not (is_first(g) and m < 2):
                    pe.wait_ge(shifted, 2 * n - 2)
                if m < 2 and not is_first(g):
                    pe.wait_ge(x2_ready, GB * g - GB + 2 * m + 2)
                for b in range(GB):
                    for a in range(2):
                        rows, cols = slice(DH * a, DH * a + DH), slice(b * P, b * P + P)
                        i = mm(s_ps[:, m % 2, a, b, :], qT[rows, m % 2, cols], kT[rows, m % 2, cols], start=True, stop=True)
                i.then_inc(s_full, 1)

            def transpose_probs(g, m):
                n = g * (2 * NM) + 2 * m
                for a in range(2):
                    pe.wait_ge(p_ready, n + a + 1)
                    if not (is_first(g) and m == 0):
                        pe.wait_ge(pT_ready, n + a - 1)
                    for b in range(GB):
                        i = tr(t_ps[:, a, b, :], probs[:, m % 2, a, b, :], ident[:, :])
                    i.then_inc(t_full, 1)

            def weigh_values(g, m):
                pe.wait_ge(pT_ready, g * (2 * NM) + 2 * m + 2)
                bank = take(pe, f"o{m}", g)
                for b in range(GB):
                    for a in range(2):
                        cols = slice((2 * m + a) * DH, (2 * m + a + 1) * DH)
                        i = mm(pair[DH * a:DH * a + DH, bank, b * P:b * P + P], v[:, b, cols], probsT[:, m % 2, a, b, :],
                               start=True, stop=True)
                i.then_inc(full[bank], 1)

            def project_out(g, t, ms):
                rows = slice(t * P, t * P + P)
                if 0 in ms:
                    pe.wait_ge(shifted, g * (2 * NM) + (2 * NM - 2 if t < 2 else 2 * NM))
                for m in ms:
                    if t == 0 and m >= NM - 4:
                        drained(pe, f"o{m}", g)
                    i = three(y_ps[:, t, 0:D], oT_hi[:, m, rows], oT_lo[:, m, rows], wo_hi[:, m, :], wo_lo[:, m, :],
                              m == 0, m == NM - 1)
                if NM - 1 in ms:
                    i.then_inc(y_full, 1)

            def transpose_context(g):
                pe.wait_ge(c_in, g * 32 + 32)
                for k in range(2):
                    for t in range(GB):
                        i = tr(t_ps[:, k, t, :], cin[:, t, k * P:k * P + P], ident[:, :])
                    i.then_inc(c_full, 1)

            def transpose_tokens(g):
                pe.wait_ge(xn_ready, g + 1)
                for k in range(KD):
                    for t in range(GB):
                        i = tr(t_ps[:, k, t, :], xn[:, t, k * P:k * P + P], ident[:, :])
                    i.then_inc(x_full, 1)

            def group(g):
                pe.wait_ge(cT_ready, 2 * g + 2)
                for j in range(2 * GB):
                    if j == X_AT:
                        transpose_tokens(g)
                    b = take(pe, f"v{j}", g)
                    t, cols = slice(j // 2 * P, j // 2 * P + P), slice(j % 2 * 512, j % 2 * 512 + 512)
                    three(pair[:, b, :], cT_hi[:, t], cT_lo[:, t], wv_hi[:, cols], wv_lo[:, cols], True, False)
                    mm(pair[:, b, :], cT_end_hi[:, t], wv_end[:, cols], start=False, stop=False)
                    mm(pair[:, b, :], cT_end_lo[0:DH, t], wv_end[0:DH, cols], start=False, stop=True).then_inc(full[b], 1)
                if is_first(g):
                    pe.wait_ge(w_ready, 3)
                project_queries_keys(g, 0)
                drained(pe, f"v{2 * GB - 2}", g)
                drained(pe, f"v{2 * GB - 1}", g)
                project_queries_keys(g, 1)

            def steps(g, ms):
                for m in ms:
                    gate = not is_first(g) and m in EARLY
                    if gate and m == LOGITS_STEP:
                        routing(g, m)
                    scores(g, m)
                    if m >= 2:
                        weigh_values(g, m - 2)
                    if gate and m == Z_STEP:
                        routing(g, m)
                    if 1 <= m < NM - 1:
                        transpose_probs(g, m - 1)
                    if gate and m == RANK_STEP:
                        routing(g, m)
                    if m < NM - 2:
                        project_queries_keys(g, m + 2)

            def end(g, following=None):
                most = range(NM - 3)
                project_out(g, 0, most)
                project_out(g, 1, most)
                transpose_probs(g, NM - 2)
                project_out(g, 2, most)
                weigh_values(g, NM - 2)
                project_out(g, 3, most)
                for t in range(2):
                    project_out(g, t, [NM - 3])
                transpose_probs(g, NM - 1)
                for t in range(2, GB):
                    project_out(g, t, [NM - 3])
                weigh_values(g, NM - 1)
                if following is not None:
                    transpose_context(following)
                for t in range(GB):
                    project_out(g, t, [NM - 2])
                for t in range(GB):
                    project_out(g, t, [NM - 1])

            def routing(g, m):
                if m == Z_STEP:
                    pe.wait_ge(z_ready, g)
                    for k in range(KD):
                        b = take(pe, f"z{k}", g)
                        for t in range(GB):
                            i = tr(pair[:, b, t * P:t * P + P], z[:, t, k * P:k * P + P], ident[:, :])
                        i.then_inc(full[b], 1)
                if m == LOGITS_STEP:
                    b = take(pe, "logits", g)
                    drained(pe, "z0", g, b)
                    drained(pe, "z1", g, b)
                    for t in range(GB):
                        for k in range(KD):
                            i = mm(pair[:, b, t * E:t * E + E], zT[:, k, t * P:t * P + P], wg[:, k, :], start=(k == 0), stop=(k == KD - 1))
                    i.then_inc(full[b], 1)
                if m == RANK_STEP:
                    pe.wait_ge(chosen_ready, g)
                    b = take(pe, "rank", g)
                    for t in range(GB):
                        mm(pair[:, b, t * E:t * E + E], before[:, :], chosen[:, t, :], start=True, stop=False)
                        i = mm(pair[:, b, t * E:t * E + E], ones_b[:, :], sums[:, t, :], start=False, stop=True)
                    i.then_inc(full[b], 1)

            pe.wait_ge(const_ready, 7)
            pe.wait_ge(small_in, 48)
            transpose_context(0)
            pe.wait_ge(w_ready, 2)
            group(0)
            steps(0, EARLY)
            pe.wait_ge(w_ready, 4)
            with pe.Fori(1, NG) as g:
                last = pe.snap(g - 1)
                steps(last, LATE)
                end(last, g)
                group(g)
                steps(g, EARLY)
            steps(NG - 1, LATE)
            end(NG - 1)
            routing(NG, Z_STEP)
            routing(NG, LOGITS_STEP)
            routing(NG, RANK_STEP)


LINKS_PER_GROUP = 75


def experts(nc, W1, b1, W2, b2, routed_in, routed_out, ident, places_all, chosen_sum, ones_b, cells):
    with ExitStack() as ctx:
        def sb(name, shape, dt=F32):
            return ctx.enter_context(nc.sbuf_tensor(name, shape, dt))

        def psum(name, shape):
            return ctx.enter_context(nc.psum_tensor(name, shape, F32))

        def sem(name):
            return ctx.enter_context(nc.semaphore(name))

        w1_hi, w1_lo = sb("w1_hi", [P, RING * WIDE], F32R), sb("w1_lo", [P, RING * WIDE], F32R)
        w2_hi, w2_lo = sb("w2_hi", [P, RING * WIDE], F32R), sb("w2_lo", [P, RING * WIDE], F32R)
        w1_stage, w2_stage = sb("w1_stage", [P, WIDE]), sb("w2_stage", [P, WIDE])
        w1_first, w2_first = sb("w1_first", [P, WIDE]), sb("w2_first", [P, WIDE])
        b1_all, b2_all = sb("b1_all", [P, RING * H]), sb("b2_all", [P, RING * D])
        zeros = sb("zeros", [P, D])

        counts, tiles, ends = sb("counts", [P, E]), sb("tiles", [P, E]), sb("ends", [P, E])
        tiles_i = sb("tiles_i", [P, E], I32)
        slot_no, regions = sb("slot_no", [P, SLOTS]), sb("regions", [P, E])
        passed, passed_tiles = sb("passed", [P, SLOTS, E]), sb("passed_tiles", [P, SLOTS, E])
        slot_expert, tile_no = sb("slot_expert", [P, SLOTS]), sb("tile_no", [P, SLOTS])
        move, move_step = sb("move", [P, E]), sb("move_step", [P, E])
        place_in, moved, beyond = sb("place_in", [P, 2 * B]), sb("moved", [P, 2 * B]), sb("beyond", [P, 2 * B, E])
        slot_row, half = sb("slot_row", [P, SLOTS]), sb("half", [P, SLOTS], I32)
        x_row = sb("x_row", [P, SLOTS], I32)
        owner = sb("owner", [P, SLOTS], I32)
        need = sb("need", [P, SLOTS], I32)
        w_at = sb("w_at", [P, SLOTS], I32)
        b1_at, b2_at = sb("b1_at", [P, SLOTS], I32), sb("b2_at", [P, SLOTS], I32)
        end_slot = sb("end_slot", [P, E], I32)
        pad_row = sb("pad_row", [P, E], I32)

        tile = sb("tile", [P, 2, D])
        rT_hi, rT_lo = sb("rT_hi", [P, KD, P], F32R), sb("rT_lo", [P, KD, P], F32R)
        hid = sb("hid", [P, H])
        hT_hi, hT_lo = sb("hT_hi", [P, KH, P], F32R), sb("hT_lo", [P, KH, P], F32R)
        y = sb("y", [P, 2, D])

        h_ps, ht_ps = psum("h_ps", [P, 2, 512]), psum("ht_ps", [P, 2, 4, P])
        rt_ps, yo_ps, n_ps = psum("rt_ps", [P, 4, P]), psum("yo_ps", [P, 512]), psum("n_ps", [P, 512])

        no_ready, counted, chain = sem("no_ready"), sem("counted"), sem("table_chain")
        pads_ready, slots_ready = sem("pads_ready"), sem("slots_ready")
        padded, zeros_ready = sem("padded"), sem("zeros_ready")
        first_in, first_hi = [sem("first1_in"), sem("first2_in")], sem("first_hi")
        w1_in, w2_in, b_in, w_hi_done = sem("w1_in"), sem("w2_in"), sem("b_in"), sem("w_hi_done")
        w1_ready, weights_ready = sem("w1_ready"), sem("weights_ready")
        tile_in = [sem("tile0_in"), sem("tile1_in")]
        rt_full, rT_hi_ready, rT_ready = sem("rt_full"), sem("rT_hi_ready"), sem("rT_ready")
        h_full, h_biased, h_ready = sem("h_full"), sem("h_biased"), sem("h_ready")
        ht_full, hT_hi_ready, hT_ready = sem("ht_full"), sem("hT_hi_ready"), sem("hT_ready")
        yo_full, y_ready = sem("yo_full"), sem("y_ready")
        y_stored = [sem("y0_stored"), sem("y1_stored")]

        block = ctx.enter_context(nc.Block())

        def from_table(eng, table, s, top, least=0):
            return eng.value_load(table[0:1, bass.ds(s, 1)], min_val=least, max_val=top)

        @block.sync
        def _(sp):
            sp.dma_start(w1_first[:, :].rearrange("p (k h) -> p k h", k=KD), W1[0].rearrange("(k p) h -> p k h", p=P)).then_inc(first_in[0], 16)
            sp.dma_start(w2_first[:, :].rearrange("p (k d) -> p k d", k=KH), W2[0].rearrange("(k p) d -> p k d", p=P)).then_inc(first_in[1], 16)
            sp.wait_ge(zeros_ready, 1)
            sp.dma_start(routed_in[E * REGION:E * REGION + P, :], zeros[:, :]).then_inc(padded, 16)
            sp.wait_ge(pads_ready, 1)
            with sp.Fori(0, E) as e:
                row = from_table(sp, pad_row, e, E * REGION - P)
                sp.dma_start(routed_in[bass.ds(row, P), :], zeros[:, :]).then_inc(padded, 16)
            sp.wait_ge(slots_ready, 1)
            sp.wait_ge(padded, 16 * (E + 1))
            for s in range(2):
                row = from_table(sp, x_row, s, E * REGION)
                sp.dma_start(tile[:, s, :], routed_in[bass.ds(row, P), :]).then_inc(tile_in[s], 16)

            def load(s, j):
                row = from_table(sp, x_row, sp.snap(s + 2), E * REGION)
                sp.wait_ge(rt_full, s + 1)
                sp.dma_start(tile[:, j, :], routed_in[bass.ds(row, P), :]).then_inc(tile_in[j], 16)

            def store(s, j):
                row = s * P if isinstance(s, int) else sp.snap(s * P)
                sp.wait_ge(y_ready, s + 2)
                sp.dma_start(routed_out[bass.ds(row, P), :], y[:, j, :]).then_inc(y_stored[j], 16)

            load(0, 0)
            load(1, 1)
            with sp.Fori(0, SLOTS // 2 - 2) as i:
                for j in range(2):
                    s = sp.snap(i * 2 + j)
                    load(sp.snap(s + 2), j)
                    store(s, j)
            for s in range(SLOTS - 4, SLOTS):
                store(s, s % 2)
            sp.wait_ge(y_stored[0], 16 * (SLOTS // 2))
            sp.wait_ge(y_stored[1], 16 * (SLOTS // 2))

        @block.gpsimd
        def _(pool):
            def load_weights(e):
                one = bass.ds(e, 1)
                pool.dma_start(w1_stage[:, :].rearrange("p (k h) -> p k h", k=KD), W1[one, :, :].rearrange("a (k p) h -> p (a k) h", p=P)).then_inc(w1_in, 16)
                pool.dma_start(w2_stage[:, :].rearrange("p (k d) -> p k d", k=KH), W2[one, :, :].rearrange("a (k p) d -> p (a k) d", p=P)).then_inc(w2_in, 16)

            def load_biases(e, r):
                one = bass.ds(e, 1)
                pool.dma_start(b1_all[:, r * H:r * H + H], b1[one, :].to_broadcast([P, H])).then_inc(b_in, 16)
                pool.dma_start(b2_all[:, r * D:r * D + D], b2[one, :].to_broadcast([P, D])).then_inc(b_in, 16)

            load_weights(1)
            pool.memset(zeros[:, :], 0.0).then_inc(zeros_ready, 1)
            pool.iota(slot_no[:, :], [[1, SLOTS]], base=0, channel_multiplier=0,
                      allow_small_or_imprecise_dtypes=True).then_inc(no_ready, 1)
            pool.iota(regions[:, :], [[REGION, E]], base=0, channel_multiplier=0,
                      allow_small_or_imprecise_dtypes=True).then_inc(no_ready, 1)
            load_biases(0, 0)
            pool.wait_ge(b_in, 32)
            load_biases(1, 1)

            def split(e, r):
                at = slice(r * WIDE, r * WIDE + WIDE)
                for n, (hi, lo, stage, came, ready) in enumerate(((w1_hi, w1_lo, w1_stage, w1_in, w1_ready),
                                                                  (w2_hi, w2_lo, w2_stage, w2_in, weights_ready))):
                    pool.wait_ge(came, 16 * e)
                    carry(pool, cells[:, 5 + n, :])
                    pool.tensor_scalar(hi[:, at], stage[:, :], 1.0, 0.0, ALU.mult, ALU.add).then_inc(w_hi_done, 1)
                    pool.wait_ge(b_in, 32 * e + 32)
                    if isinstance(e, int) and e == 1 and n:
                        pool.wait_ge(ready, 1)
                    pool.wait_ge(w_hi_done, 2 * e - 1 + n)
                    pool.tensor_tensor(lo[:, at], stage[:, :], hi[:, at].bitcast(F32), ALU.subtract).then_inc(ready, 1)

            def weights(e, r, more):
                done = from_table(pool, end_slot, pool.snap(e - RING) if not isinstance(e, int) else e - RING, SLOTS + 1, 1)
                pool.wait_ge(y_ready, done)
                carry(pool, cells[:, 7, :])
                load_biases(e, r)
                split(e, r)
                if more:
                    after(e)

            def after(e):
                pool.wait_ge(weights_ready, e + 1)
                load_weights(e + 1 if isinstance(e, int) else pool.snap(e + 1))

            split(1, 1)
            after(1)
            pool.wait_ge(slots_ready, 1)
            with pool.Fori(1, E // 2 - 1) as i:
                weights(pool.snap(i * 2), 0, True)
                weights(pool.snap(i * 2 + 1), 1, True)
            weights(E - 2, 0, True)
            weights(E - 1, 1, False)

        @block.scalar
        def _(act):
            for n, (hi, stage) in enumerate(((w1_hi, w1_first), (w2_hi, w2_first))):
                act.wait_ge(first_in[n], 16)
                nc.scalar.activation(hi[:, 0:WIDE], stage[:, :], ACT.Identity).then_inc(first_hi, 1)

            def high_inputs(s):
                act.wait_ge(rt_full, s + 1)
                nc.scalar.activation(rT_hi[:, :, :], rt_ps[:, 0:KD, :], ACT.Identity).then_inc(rT_hi_ready, 1)

            def high_hidden(s):
                for a in range(2):
                    act.wait_ge(ht_full, 2 * s + a + 1)
                    nc.scalar.activation(hT_hi[:, 4 * a:4 * a + 4, :], ht_ps[:, a, :, :], ACT.Identity).then_inc(hT_hi_ready, 1)

            def gelu(s):
                for a in range(2):
                    act.wait_ge(h_biased, 2 * s + a + 1)
                    nc.scalar.activation(hid[:, 512 * a:512 * a + 512], hid[:, 512 * a:512 * a + 512], ACT.Gelu).then_inc(h_ready, 1)

            high_inputs(0)
            gelu(0)
            high_inputs(1)
            high_hidden(0)
            with act.Fori(1, SLOTS - 1) as s:
                gelu(s)
                high_inputs(act.snap(s + 1))
                high_hidden(s)
            gelu(SLOTS - 1)
            high_hidden(SLOTS - 1)

        @block.vector
        def _(dve):
            link = Links(dve, chain)
            dve.wait_ge(counted, 1)
            link(nc.vector.tensor_copy(counts[:, :], n_ps[:, 0:E]))
            dve.wait_ge(no_ready, 2)
            nc.vector.tensor_tensor(pad_row[:, :], counts[:, :], regions[:, :], ALU.add).then_inc(pads_ready, 1)
            link(nc.vector.tensor_scalar(tiles_i[:, :], counts[:, :], float(P - 1), None, ALU.add))
            link(nc.vector.tensor_scalar(tiles_i[:, :], tiles_i[:, :], TILE_BITS, None, ALU.logical_shift_right))
            link(nc.vector.tensor_copy(tiles[:, :], tiles_i[:, :]))
            link(nc.vector.tensor_copy(ends[:, 0:1], tiles[:, 0:1]))
            for e in range(1, E):
                link(nc.vector.tensor_tensor(ends[:, e:e + 1], ends[:, e - 1:e], tiles[:, e:e + 1], ALU.add))
            nc.vector.tensor_scalar(end_slot[:, :], ends[:, :], 1.0, None, ALU.add).then_inc(y_ready, 1)
            link(nc.vector.tensor_tensor(passed[:, :, :], slot_no[:, :].unsqueeze(2).to_broadcast([P, SLOTS, E]),
                                         ends[:, :].unsqueeze(1).to_broadcast([P, SLOTS, E]), ALU.is_ge))
            nc.vector.tensor_reduce(slot_expert[:, :], passed[:, :, :], AX_X, ALU.add)
            link(nc.vector.tensor_tensor(passed_tiles[:, :, :], passed[:, :, :],
                                         tiles[:, :].unsqueeze(1).to_broadcast([P, SLOTS, E]), ALU.mult))
            link(nc.vector.tensor_reduce(tile_no[:, :], passed_tiles[:, :, :], AX_X, ALU.add))
            link(nc.vector.tensor_tensor(tile_no[:, :], slot_no[:, :], tile_no[:, :], ALU.subtract))
            link(nc.vector.tensor_scalar(tile_no[:, :], tile_no[:, :], float(P), None, ALU.mult))
            link(nc.vector.scalar_tensor_tensor(out=slot_row[:, :], in0=slot_expert[:, :], scalar=float(REGION),
                                                in1=tile_no[:, :], op0=ALU.mult, op1=ALU.add))
            nc.vector.tensor_scalar(x_row[:, :], slot_row[:, :], float(E * REGION), None, ALU.min)
            link(nc.vector.tensor_scalar(owner[:, :], slot_expert[:, :], float(E - 1), None, ALU.min))
            nc.vector.tensor_scalar(need[:, :], owner[:, :], 1.0, None, ALU.add)
            link(nc.vector.tensor_scalar(half[:, :], owner[:, :], RING - 1, None, ALU.bitwise_and))
            nc.vector.tensor_scalar(w_at[:, :], half[:, :], float(WIDE), None, ALU.mult)
            nc.vector.tensor_scalar(b1_at[:, :], half[:, :], float(H), None, ALU.mult)
            nc.vector.tensor_scalar(b2_at[:, :], half[:, :], float(D), None, ALU.mult).then_inc(slots_ready, 1)
            for n, (lo, hi, stage) in enumerate(((w1_lo, w1_hi, w1_first), (w2_lo, w2_hi, w2_first))):
                dve.wait_ge(first_hi, n + 1)
                nc.vector.tensor_tensor(lo[:, 0:WIDE], stage[:, :], hi[:, 0:WIDE].bitcast(F32), ALU.subtract).then_inc((w1_ready, weights_ready)[n], 1)
            dve.wait_ge(b_in, 64)
            dve.wait_ge(slots_ready, 1)

            def low_inputs(s):
                dve.wait_ge(rT_hi_ready, s + 1)
                nc.vector.tensor_tensor(rT_lo[:, :, :], rt_ps[:, 0:KD, :], rT_hi[:, :, :].bitcast(F32), ALU.subtract).then_inc(rT_ready, 1)

            def low_hidden(s):
                for a in range(2):
                    dve.wait_ge(hT_hi_ready, 2 * s + a + 1)
                    nc.vector.tensor_tensor(hT_lo[:, 4 * a:4 * a + 4, :], ht_ps[:, a, :, :],
                                            hT_hi[:, 4 * a:4 * a + 4, :].bitcast(F32), ALU.subtract).then_inc(hT_ready, 1)

            def bias_hidden(s):
                at = from_table(dve, b1_at, s, (RING - 1) * H)
                ats = [at + 512 * a for a in range(2)]
                for a in range(2):
                    dve.wait_ge(h_full, 2 * s + a + 1)
                    nc.vector.tensor_tensor(hid[:, 512 * a:512 * a + 512], h_ps[:, a, :], b1_all[:, bass.ds(ats[a], 512)], ALU.add).then_inc(h_biased, 1)

            def outputs(s, j):
                at = from_table(dve, b2_at, s, (RING - 1) * D)
                if not (isinstance(s, int) and s < 2):
                    dve.wait_ge(y_stored[j], (s // 2) * 16 if isinstance(s, int) else s * 8 - 8 * j)
                dve.wait_ge(yo_full, s + 1)
                nc.vector.tensor_tensor(y[:, j, :], yo_ps[:, 0:D], b2_all[:, bass.ds(at, D)], ALU.add).then_inc(y_ready, 1)

            def step(s, j, more=True):
                bias_hidden(s)
                if more:
                    low_inputs(s + 1 if isinstance(s, int) else dve.snap(s + 1))
                if not (isinstance(s, int) and s == 0):
                    outputs(s - 1 if isinstance(s, int) else dve.snap(s - 1), 1 - j)
                low_hidden(s)

            def places_out():
                link(nc.vector.tensor_tensor(move[:, :], ends[:, :], tiles[:, :], ALU.subtract))
                link(nc.vector.scalar_tensor_tensor(out=move[:, :], in0=move[:, :], scalar=float(P), in1=regions[:, :],
                                                    op0=ALU.mult, op1=ALU.subtract))
                link(nc.vector.tensor_copy(move_step[:, 0:1], move[:, 0:1]))
                link(nc.vector.tensor_tensor(move_step[:, 1:E], move[:, 1:E], move[:, 0:E - 1], ALU.subtract))
                flat = places_all[:, :, :, :].rearrange("p g t k -> p (g t k)")
                link(nc.vector.tensor_copy(place_in[:, :], flat))
                link(nc.vector.tensor_tensor(beyond[:, :, :], place_in[:, :].unsqueeze(2).to_broadcast([P, 2 * B, E]),
                                             regions[:, :].unsqueeze(1).to_broadcast([P, 2 * B, E]), ALU.is_ge))
                link(nc.vector.tensor_tensor(beyond[:, :, :], beyond[:, :, :],
                                             move_step[:, :].unsqueeze(1).to_broadcast([P, 2 * B, E]), ALU.mult))
                link(nc.vector.tensor_reduce(moved[:, :], beyond[:, :, :], AX_X, ALU.add))
                nc.vector.tensor_tensor(flat, place_in[:, :], moved[:, :], ALU.add)

            low_inputs(0)
            step(0, 0)
            step(1, 1)
            places_out()
            step(2, 0)
            with dve.Fori(1, SLOTS // 2 - 1) as i:
                step(dve.snap(i * 2 + 1), 1)
                step(dve.snap(i * 2 + 2), 0)
            step(SLOTS - 1, 1, False)
            outputs(SLOTS - 1, 1)

        @block.tensor
        def _(pe):
            mm, tr = nc.tensor.matmul, nc.tensor.transpose
            mm(n_ps[:, 0:E], ones_b[:, :], chosen_sum[:, :], start=True, stop=True).then_inc(counted, 1)

            def three(out, a_hi, a_lo, b_hi, b_lo, start, stop):
                mm(out, a_hi, b_hi, start=start, stop=False)
                mm(out, a_hi, b_lo, start=False, stop=False)
                return mm(out, a_lo, b_hi, start=False, stop=stop)

            def transpose_inputs(s, j):
                pe.wait_ge(tile_in[j], (s // 2 + 1) * 16 if isinstance(s, int) else s * 8 + (16 - 8 * j))
                for k in range(KD):
                    i = tr(rt_ps[:, k, :], tile[:, j, k * P:k * P + P], ident[:, :])
                i.then_inc(rt_full, 1)

            def hidden_registers(s):
                needed = from_table(pe, need, s, E, 1)
                at = pe.snap((needed + 1) % RING * WIDE)
                return [at + 512 * n for n in range(4)], needed

            def hidden(s, ats, needed):
                pe.wait_ge(weights_ready, needed)
                pe.wait_ge(rT_ready, s + 1)
                for a in range(2):
                    if not (isinstance(s, int) and s == 0):
                        pe.wait_ge(h_biased, 2 * s + a - 1)
                    for k in range(KD):
                        cols = bass.ds(ats[2 * k + a], 512)
                        i = three(h_ps[:, a, :], rT_hi[:, k, :], rT_lo[:, k, :], w1_hi[:, cols], w1_lo[:, cols], k == 0, k == KD - 1)
                    i.then_inc(h_full, 1)

            def transpose_hidden(s):
                for a in range(2):
                    pe.wait_ge(h_ready, 2 * s + a + 1)
                    for k in range(4):
                        i = tr(ht_ps[:, a, k, :], hid[:, (4 * a + k) * P:(4 * a + k) * P + P], ident[:, :])
                    i.then_inc(ht_full, 1)

            def output_registers(s):
                at = from_table(pe, w_at, s, (RING - 1) * WIDE)
                return [at + D * k for k in range(KH)]

            def outputs(s, ats):
                if not (isinstance(s, int) and s == 0):
                    pe.wait_ge(y_ready, s + 1)
                for k in range(KH):
                    if k % 4 == 0:
                        pe.wait_ge(hT_ready, 2 * s + 1 + k // 4)
                    cols = bass.ds(ats[k], D)
                    i = three(yo_ps[:, 0:D], hT_hi[:, k, :], hT_lo[:, k, :], w2_hi[:, cols], w2_lo[:, cols], k == 0, k == KH - 1)
                i.then_inc(yo_full, 1)

            def step(s, j):
                fixed = isinstance(s, int)
                after = s + 1 if fixed else pe.snap(s + 1)
                last = s - 1 if fixed else pe.snap(s - 1)
                hidden_at = hidden_registers(after)
                transpose_inputs(after, 1 - j)
                if not (fixed and s == 0):
                    outputs(last, output_registers(last))
                transpose_hidden(s)
                hidden(after, *hidden_at)

            transpose_inputs(0, 0)
            pe.wait_ge(slots_ready, 1)
            hidden(0, *hidden_registers(0))
            step(0, 0)
            with pe.Fori(0, SLOTS // 2 - 1) as i:
                step(pe.snap(i * 2 + 1), 1)
                step(pe.snap(i * 2 + 2), 0)
            last = SLOTS - 1
            outputs(last - 1, output_registers(last - 1))
            transpose_hidden(last)
            outputs(last, output_registers(last))


def combine(nc, x2_dram, z_dram, routed_out, gamma, beta, places_all, weights_all, cells, out):
    with ExitStack() as ctx:
        def sb(name, shape, dt=F32):
            return ctx.enter_context(nc.sbuf_tensor(name, shape, dt))

        def sem(name):
            return ctx.enter_context(nc.semaphore(name))

        gamma_all, beta_all = sb("gamma_all", [P, D]), sb("beta_all", [P, D])
        rows = sb("rows", [P, 2, GB, 2], U32)
        y = sb("y_rows", [P, 2, GB, 2, D])
        z, x2 = sb("z_rows", [P, 2, GB, D]), sb("x2_rows", [P, 2, GB, D])
        r = sb("r", [P, 2, GB, D])
        normed, result = sb("normed", [P, 2, GB, D]), sb("result", [P, 2, GB, D])
        stats, mv = sb("stats2", [P, GB, 6]), sb("mv2", [P, GB, 2])
        tmp = sb("tmp2", [P, 2 * GB])
        rstd, shift = sb("rstd", [P, 2, GB]), sb("shift", [P, 2, GB])

        params_in, chain = sem("params_in"), sem("combine_chain")
        z_in, x2_in, y_in = [sem("z0_in"), sem("z1_in")], [sem("x20_in"), sem("x21_in")], [sem("y0_in"), sem("y1_in")]
        rows_ready, summed = sem("rows_ready"), sem("summed")
        norm_ready, normed_ready, result_ready = sem("norm_ready"), sem("normed_ready"), sem("result_ready")
        x2_beta_ready = sem("x2_beta_ready")
        out_stored = [sem("out0_stored"), sem("out1_stored")]

        block = ctx.enter_context(nc.Block())

        @block.sync
        def _(sp):
            sp.dma_start(gamma_all[:, :], gamma.rearrange("(a n) -> a n", a=1).to_broadcast([P, D])).then_inc(params_in, 16)
            sp.dma_start(beta_all[:, :], beta.rearrange("(a n) -> a n", a=1).to_broadcast([P, D])).then_inc(params_in, 16)

            def load(g, j):
                row = g * GT if isinstance(g, int) else sp.snap(g * GT)
                if not isinstance(g, int):
                    sp.wait_ge(result_ready, g - 1)
                sp.dma_start(z[:, j, :, :], z_dram[bass.ds(row, GT), :].rearrange("(b p) d -> p b d", p=P)).then_inc(z_in[j], 16)
                sp.dma_start(x2[:, j, :, :], x2_dram[bass.ds(row, GT), :].rearrange("(b p) d -> p b d", p=P)).then_inc(x2_in[j], 16)

            def store(g, j):
                at = g * GB if isinstance(g, int) else sp.snap(g * GB)
                sp.wait_ge(result_ready, g + 1)
                sp.dma_start(out[bass.ds(at, GB), :, :].rearrange("b p d -> p b d"), result[:, j, :, :]).then_inc(out_stored[j], 16)

            load(0, 0)
            load(1, 1)
            with sp.Fori(1, NG // 2) as i:
                for j in range(2):
                    g = sp.snap(i * 2 + j)
                    before = sp.snap(g - 2)
                    load(g, j)
                    store(before, j)
            store(NG - 2, 0)
            store(NG - 1, 1)
            sp.wait_ge(out_stored[0], 16 * (NG // 2))
            sp.wait_ge(out_stored[1], 16 * (NG // 2))

        @block.gpsimd
        def _(pool):
            def gather(g, j):
                pool.wait_ge(rows_ready, g + 1)
                if not isinstance(g, int):
                    pool.wait_ge(summed, g - 1)
                    carry(pool, cells[:, 8 + j, :])
                for b in range(GB):
                    for k in range(2):
                        pool.indirect_dma_start(
                            out=y[:, j, b, k, :], out_offset=None, in_=routed_out,
                            in_offset=bass.IndirectOffsetOnAxis(ap=rows[:, j, b, k:k + 1], axis=0)).then_inc(y_in[j], 16)

            def add_beta(g, j):
                pool.wait_ge(params_in, 32)
                pool.wait_ge(x2_in[j], (g // 2 + 1) * 16 if isinstance(g, int) else g * 8 + (16 - 8 * j))
                pool.tensor_tensor(x2[:, j, :, :], x2[:, j, :, :], beta_all[:, :].unsqueeze(1).to_broadcast([P, GB, D]), ALU.add).then_inc(x2_beta_ready, 1)

            gather(0, 0)
            gather(1, 1)
            with pool.Fori(1, NG // 2) as i:
                gather(pool.snap(i * 2), 0)
                add_beta(pool.snap(i * 2 - 2), 0)
                gather(pool.snap(i * 2 + 1), 1)
                add_beta(pool.snap(i * 2 - 1), 1)
            add_beta(NG - 2, 0)
            add_beta(NG - 1, 1)

        @block.scalar
        def _(act):
            def group(g, j):
                act.wait_ge(norm_ready, g + 1)
                if not (isinstance(g, int) and g < 2):
                    act.wait_ge(result_ready, g - 1)
                for b in range(GB):
                    i = nc.scalar.activation(normed[:, j, b, :], r[:, j, b, :], ACT.Identity, scale=rstd[:, j, b:b + 1], bias=shift[:, j, b:b + 1])
                i.then_inc(normed_ready, 1)

            group(0, 0)
            group(1, 1)
            with act.Fori(1, NG // 2) as i:
                group(act.snap(i * 2), 0)
                group(act.snap(i * 2 + 1), 1)

        @block.vector
        def _(dve):
            def take_rows(g, j):
                at = g if isinstance(g, int) else dve.snap(g)
                nc.vector.tensor_copy(rows[:, j, :, :], places_all[:, bass.ds(at, 1), :, :].rearrange("p g t k -> p (g t) k")).then_inc(rows_ready, 1)

            def add_up(g, j, link):
                fixed = isinstance(g, int)
                if not (fixed and g < 2):
                    dve.wait_ge(normed_ready, g - 1)
                dve.wait_ge(z_in[j], (g // 2 + 1) * 16 if fixed else g * 8 + (16 - 8 * j))
                dve.wait_ge(y_in[j], (g // 2 + 1) * (32 * GB) if fixed else g * (16 * GB) + (32 - 16 * j) * GB)
                for k in range(2):
                    for b in range(GB):
                        w = weights_all[:, bass.ds(g, 1), b:b + 1, k:k + 1].rearrange("p g t k -> p (g t k)")
                        i = nc.vector.scalar_tensor_tensor(out=r[:, j, b, :], in0=y[:, j, b, k, :], scalar=w,
                                                           in1=(z if k == 0 else r)[:, j, b, :], op0=ALU.mult, op1=ALU.add)
                    link(i)
                for b in range(GB):
                    i = nc.vector.bn_stats(stats[:, b, :], r[:, j, b, :])
                i.then_inc(summed, 1)
                dve.wait_ge(summed, g + 1)
                carry(nc.vector, cells[:, 10, :])
                for b in range(GB):
                    i = nc.vector.bn_aggr(mv[:, b, :], stats[:, b, :])
                link(i)

            def scale(g, j, link):
                rsqrt_and_shift(nc, link, mv, tmp, rstd[:, j, :], shift[:, j, :]).then_inc(norm_ready, 1)

            def finish(g, j, link):
                if not (isinstance(g, int) and g < 2):
                    dve.wait_ge(out_stored[j], g * 8 - 8 * j)
                dve.wait_ge(x2_beta_ready, g + 1)
                dve.wait_ge(normed_ready, g + 1)
                link(nc.vector.tensor_tensor(normed[:, j, :, :], normed[:, j, :, :], gamma_all[:, :].unsqueeze(1).to_broadcast([P, GB, D]), ALU.mult))
                nc.vector.tensor_tensor(result[:, j, :, :], normed[:, j, :, :], x2[:, j, :, :], ALU.add).then_inc(result_ready, 1)

            def step(g, j, link, ahead=True):
                add_up(g, j, link)
                if ahead:
                    take_rows(g + 2, j)
                if not (isinstance(g, int) and g == 0):
                    finish(g - 1 if isinstance(g, int) else dve.snap(g - 1), 1 - j, link)
                scale(g, j, link)

            take_rows(0, 0)
            take_rows(1, 1)
            dve.wait_ge(params_in, 32)
            link = Links(dve, chain)
            step(0, 0, link)
            step(1, 1, link)
            step(2, 0, link)
            with dve.Fori(1, NG // 2 - 2) as i:
                link = Links(dve, chain, i * (2 * STEP_LINKS) + (STEP_LINKS - 1))
                step(dve.snap(i * 2 + 1), 1, link)
                step(dve.snap(i * 2 + 2), 0, link)
                assert link.n == 2 * STEP_LINKS
            link = Links(dve, chain, (NG - 3) * STEP_LINKS - 1)
            step(NG - 3, 1, link)
            step(NG - 2, 0, link, False)
            step(NG - 1, 1, link, False)
            finish(NG - 1, 1, link)


STEP_LINKS = 16


_INS = ["x", "ctx_768", "L0_xattn_Wq", "L0_xattn_Wk", "L0_xattn_Wv", "L0_xattn_Wo", "L0_xattn_bo", "L0_ffn_Wg",
        "L0_ffn_bg", "L0_ffn_W1", "L0_ffn_b1", "L0_ffn_W2", "L0_ffn_b2", "L0_ffn_gamma", "L0_ffn_beta"]


def kernel(**inputs):
    import numpy as _np
    import concourse.bacc as _bacc
    from concourse.bass_utils import run_bass_kernel_spmd as _run

    nc = _bacc.Bacc("TRN2", target_bir_lowering=False, num_devices=1)
    arrays, args = {}, []
    for name in _INS:
        a = _np.ascontiguousarray(inputs[name])
        arrays[f"in_{name}"] = a
        args.append(nc.dram_tensor(f"in_{name}", a.shape, mybir.dt.from_np(a.dtype), kind="ExternalInput").ap())
    args.append(nc.dram_tensor("out_0", (B, P, D), F32, kind="ExternalOutput").ap())
    build(nc, *args)
    r = _run(nc, [arrays], core_ids=[0])
    return r.results[0]["out_0"]
```

```python
from contextlib import ExitStack

import concourse.bass as bass
from concourse import mybir

F32 = mybir.dt.float32
F32R = mybir.dt.float32r
BF16 = mybir.dt.bfloat16
I32 = mybir.dt.int32
U32 = mybir.dt.uint32
ALU = mybir.AluOpType
ACT = mybir.ActivationFunctionType
AX_X = mybir.AxisListType.X

P = 128
B, D, DC = 32, 256, 192
HEADS, DH = 16, 64
INNER = HEADS * DH
GB = 4
GT = GB * P
NG = B // GB
NM = INNER // P
KD = D // P
E, H = 8, 1024
KH = H // P
REGION = B * P + P
SLOTS = (2 * B * P + E * (P - 1)) // P + 1
RING = 2
WIDE = KD * H
TILE_BITS = 7
assert KD * H == KH * D and 1 << TILE_BITS == P
EPS = 1e-5
CELLS = 16
RSQRT_SEED = 0x5F3759DF


def pair_bank_order(gate):
    order = [f"v{j}" for j in range(2 * GB)] + ["q0", "k0", "q1", "k1"]
    for m in range(NM):
        if gate and m != RANK_STEP:
            order += ROUTING_STEPS.get(m, [])
        if m >= 2:
            order.append(f"o{m - 2}")
        if gate and m == RANK_STEP:
            order += ROUTING_STEPS[m]
        if m < NM - 2:
            order += [f"q{m + 2}", f"k{m + 2}"]
    return order + [f"o{NM - 2}", f"o{NM - 1}"]


Z_STEP, LOGITS_STEP, RANK_STEP = 1, 3, 5
ROUTING_STEPS = {Z_STEP: ["z0", "z1"], LOGITS_STEP: ["logits"], RANK_STEP: ["rank"]}
EARLY = range(6)
LATE = range(6, NM)
X_AT = 6
SCATTER_STEPS = {5: [(0, 0), (0, 1)], 6: [(1, 0), (1, 1), (2, 0)], 7: [(2, 1), (3, 0), (3, 1)]}
FIRST, LATER, LAST = pair_bank_order(False), pair_bank_order(True), ["z0", "z1", "logits", "rank"]
assert len(FIRST) % 2 == 0 and len(LATER) % 2 == 0


def pair_bank(name, g):
    if isinstance(g, int) and g == 0:
        at, before = FIRST.index(name), 0
    elif isinstance(g, int) and g == NG:
        at, before = LAST.index(name), len(FIRST) // 2 + (NG - 1) * (len(LATER) // 2)
    else:
        at, before = LATER.index(name), g * (len(LATER) // 2) + (len(FIRST) - len(LATER)) // 2
    return at % 2, before + at // 2


def is_first(g):
    return isinstance(g, int) and g == 0


def build(nc, x, ctx_in, Wq, Wk, Wv, Wo, bo, Wg, bg, W1, b1, W2, b2, gamma, beta, out):
    x2_dram = nc.dram_tensor("x2_dram", (B * P, D), F32).ap()
    z_dram = nc.dram_tensor("z_dram", (B * P, D), F32).ap()
    routed_in = nc.dram_tensor("routed_in", (E * REGION + P, D), F32).ap()
    routed_out = nc.dram_tensor("routed_out", (SLOTS * P, D), F32).ap()

    with ExitStack() as whole:
        def keep(name, shape, dt):
            return whole.enter_context(nc.sbuf_tensor(name, shape, dt))

        ident = keep("ident", [P, P], F32)
        places_all = keep("places_all", [P, NG, GB, 2], U32)
        cells = keep("cells", [P, CELLS, 2], F32)
        weights_all = keep("weights_all", [P, NG, GB, 2], F32)
        chosen_sum = keep("chosen_sum", [P, E], BF16)
        ones_b = keep("ones_b", [P, P], BF16)
        stage = keep("stage", [P, 2, WIDE], F32)
        zeros = keep("zeros", [P, D], F32)
        tables = Tables(keep)

        attention(nc, x, ctx_in, Wq, Wk, Wv, Wo, bo, Wg, bg, x2_dram, z_dram, routed_in,
                  W1, W2, ident, places_all, weights_all, chosen_sum, ones_b, cells, stage, zeros, tables)
        z_all, x2_all = keep("z_all", [P, B, D], F32), keep("x2_all", [P, B, D], F32)
        gamma_all = keep("gamma_all", [P, D], F32)
        experts(nc, W1, b1, W2, b2, routed_in, routed_out, ident, places_all, cells, stage, tables,
                x2_dram, z_dram, gamma, beta, z_all, x2_all, gamma_all)
        combine(nc, routed_out, places_all, weights_all, cells, z_all, x2_all, gamma_all, out)


def carry(eng, cell):
    return eng.tensor_tensor(cell[:, 0:1], cell[:, 1:2], cell[:, 1:2], ALU.add)


class Tables:

    def __init__(self, keep):
        self.x_row = keep("x_row", [P, SLOTS], I32)
        self.need = keep("need", [P, SLOTS], I32)
        self.w_at = keep("w_at", [P, SLOTS], I32)
        self.b1_at = keep("b1_at", [P, SLOTS], I32)
        self.b2_at = keep("b2_at", [P, SLOTS], I32)
        self.end_slot = keep("end_slot", [P, E], I32)
        self.pad_row = keep("pad_row", [P, E], I32)
        self.move = keep("move", [P, E], F32)


class Links:

    def __init__(self, eng, sem, before=0):
        self.eng, self.sem, self.before, self.n = eng, sem, before, 0

    def __call__(self, ins):
        self.n += 1
        ins.then_inc(self.sem, 1)
        self.eng.wait_ge(self.sem, self.before + self.n)


def rsqrt_and_shift(nc, link, mv, t, rstd, shift):
    n = mv.shape[1]
    v, a = t[:, 0:n], t[:, n:2 * n]
    link(nc.vector.tensor_scalar(v, mv[:, :, 1], EPS, None, ALU.add))
    link(nc.vector.tensor_scalar(a.bitcast(I32), v.bitcast(I32), 1, None, ALU.logical_shift_right))
    link(nc.vector.tensor_scalar(rstd.bitcast(I32), a.bitcast(I32), -1.0, float(RSQRT_SEED),
                                 ALU.mult, ALU.add))
    for _ in range(3):
        link(nc.vector.scalar_tensor_tensor(out=a, in0=rstd, scalar=-0.5, in1=rstd,
                                            op0=ALU.mult, op1=ALU.mult))
        link(nc.vector.tensor_tensor(a, a, v, ALU.mult))
        link(nc.vector.scalar_tensor_tensor(out=rstd, in0=a, scalar=1.5, in1=rstd,
                                            op0=ALU.add, op1=ALU.mult))
    return nc.vector.scalar_tensor_tensor(out=shift, in0=mv[:, :, 0], scalar=-1.0, in1=rstd,
                                          op0=ALU.mult, op1=ALU.mult)


def attention(nc, x, ctx_in, Wq, Wk, Wv, Wo, bo, Wg, bg, x2_dram, z_dram, routed_in,
              W1, W2, ident, places_all, weights_all, chosen_sum, ones_b, cells, stage, zeros, tables):
    with ExitStack() as ctx:
        def sb(name, shape, dt=F32):
            return ctx.enter_context(nc.sbuf_tensor(name, shape, dt))

        def psum(name, shape):
            return ctx.enter_context(nc.psum_tensor(name, shape, F32))

        def sem(name):
            return ctx.enter_context(nc.semaphore(name))

        wq_hi, wq_lo = sb("wq_hi", [P, KD, INNER], F32R), sb("wq_lo", [P, KD, INNER], F32R)
        wk_hi, wk_lo = sb("wk_hi", [P, INNER], F32R), sb("wk_lo", [P, INNER], F32R)
        wv_hi, wv_lo = sb("wv_hi", [P, INNER], F32R), sb("wv_lo", [P, INNER], F32R)
        wk_end, wv_end = sb("wk_end", [P, INNER], F32R), sb("wv_end", [P, INNER], F32R)
        wo_hi, wo_lo = sb("wo_hi", [P, NM, D], F32R), sb("wo_lo", [P, NM, D], F32R)
        wg = sb("wg", [P, KD, E])
        bo_all, bg_all = sb("bo_all", [P, D]), sb("bg_all", [P, E])
        before = sb("before", [P, P], BF16)
        expert_no = sb("expert_no", [P, E])
        region_at = sb("region_at", [P, E])

        xin, xn = sb("xin", [P, GB, D]), sb("xn", [P, GB, D])
        x_bo = sb("x_bo", [P, GB, D])
        cin = sb("cin", [P, GB, 2 * P])
        xT_hi, xT_lo = sb("xT_hi", [P, KD, GT], F32R), sb("xT_lo", [P, KD, GT], F32R)
        cT_hi, cT_lo = sb("cT_hi", [P, GT], F32R), sb("cT_lo", [P, GT], F32R)
        cT_end_hi, cT_end_lo = sb("cT_end_hi", [P, GT], F32R), sb("cT_end_lo", [P, GT], F32R)
        qT, kT = sb("qT", [P, 2, GT]), sb("kT", [P, 2, GT])
        v = sb("v", [P, GB, INNER])
        probs = sb("probs", [P, 2, 2, GB, P])
        probsT = sb("probsT", [P, 2, 2, GB, P])
        oT_hi, oT_lo = sb("oT_hi", [P, NM, GT], F32R), sb("oT_lo", [P, NM, GT], F32R)
        x2, z, zT = sb("x2", [P, GB, D]), sb("z", [P, GB, D]), sb("zT", [P, KD, GT])

        stats, mv = sb("stats", [P, GB, 6]), sb("mv", [P, GB, 2])
        tmp = sb("tmp", [P, 2 * GB])
        rstd1, shift1 = sb("rstd1", [P, GB]), sb("shift1", [P, GB])
        rstd2, shift2 = sb("rstd2", [P, GB]), sb("shift2", [P, GB])
        row_max = sb("row_max", [P, 2, GB])
        row_sum, row_rec = sb("row_sum", [P, 2, GB]), sb("row_rec", [P, 2, GB])
        logits = sb("logits", [P, GB, E])
        best, best_at = sb("best", [P, GB, 8]), sb("best_at", [P, GB, 8], U32)
        best_f = sb("best_f", [P, GB, 2])
        picks = sb("picks", [P, GB, 2, E])
        chosen = sb("chosen", [P, GB, E], BF16)
        sums = sb("sums", [P, GB, E], BF16)
        place = sb("place", [P, GB, E])
        place2 = sb("place2", [P, GB, 2, E])
        place_f = sb("place_f", [P, GB, 2])
        places = sb("places", [P, GB, 2], U32)
        gap, odds, p_best = sb("gap", [P, GB]), sb("odds", [P, GB]), sb("p_best", [P, GB, 2])

        counts, tiles, ends = sb("counts", [P, E]), sb("tiles", [P, E]), sb("ends", [P, E])
        tiles_i, slot_no = sb("tiles_i", [P, E], I32), sb("slot_no", [P, SLOTS])
        passed, passed_tiles = sb("passed", [P, SLOTS, E]), sb("passed_tiles", [P, SLOTS, E])
        slot_expert, tile_no = sb("slot_expert", [P, SLOTS]), sb("tile_no", [P, SLOTS])
        owner, half = sb("owner", [P, SLOTS], I32), sb("half", [P, SLOTS], I32)

        s_ps = psum("s_ps", [P, 2, 2, GB, P])
        t_ps = psum("t_ps", [P, 2, GB, P])
        t_flat = t_ps[:, :, :, :].rearrange("p a b k -> p a (b k)")
        pair = psum("pair", [P, 2, 512])
        y_ps = s_ps[:, :, :, :, :].rearrange("p u a b k -> p (u a) (b k)")
        n_ps = y_ps[:, 0, 0:E]

        w_in = [sem(f"w_in{n}") for n in range(4)]
        w_hi, w_ready = sem("w_hi"), sem("w_ready")
        small_in, first_in = sem("small_in"), sem("first_in")
        counted, pads_ready, padded = sem("counted"), sem("pads_ready"), sem("padded")
        x_in, c_in, x_used = sem("x_in"), sem("c_in"), sem("x_used")
        const_step, const_ready = sem("const_step"), sem("const_ready")
        chain = sem("chain")
        norm1_ready, xn_ready, norm2_ready, z_ready = sem("norm1_ready"), sem("xn_ready"), sem("norm2_ready"), sem("z_ready")
        full = [sem("pair0_full"), sem("pair1_full")]
        free = [sem("pair0_free"), sem("pair1_free")]
        c_full, x_full, cT_ready, xT_ready = sem("c_full"), sem("x_full"), sem("cT_ready"), sem("xT_ready")
        cT_hi_ready, xT_hi_ready, oT_hi_ready = sem("cT_hi_ready"), sem("xT_hi_ready"), sem("oT_hi_ready")
        s_full, shifted, p_ready = sem("s_full"), sem("shifted"), sem("p_ready")
        expd, rec_ready, t_full, pT_ready = sem("expd"), sem("rec_ready"), sem("t_full"), sem("pT_ready")
        y_full, x2_ready = sem("y_full"), sem("x2_ready")
        x2_stored, z_stored, scattered = sem("x2_stored"), sem("z_stored"), sem("scattered")
        chosen_ready, places_ready, gap_ready, odds_ready = sem("chosen_ready"), sem("places_ready"), sem("gap_ready"), sem("odds_ready")

        block = ctx.enter_context(nc.Block())

        def take(eng, name, g):
            b, n = pair_bank(name, g)
            if not (isinstance(n, int) and n == 0):
                eng.wait_ge(free[b], n)
            return b

        def filled(eng, name, g):
            b, n = pair_bank(name, g)
            eng.wait_ge(full[b], n + 1)
            return b

        def drained(eng, name, g, taken=None):
            b, n = pair_bank(name, g)
            if b != taken:
                eng.wait_ge(free[b], n + 1)

        def pad(eng, first, end):
            eng.wait_ge(pads_ready, 1)
            with eng.Fori(first, end) as e:
                row = eng.value_load(tables.pad_row[0:1, bass.ds(e, 1)], min_val=0, max_val=E * REGION - P)
                eng.dma_start(routed_in[bass.ds(row, P), :], zeros[:, :]).then_inc(padded, 16)

        @block.sync
        def _(sp):
            def load_x(g):
                sp.dma_start(xin[:, :, :], x[bass.ds(g * GB, GB), :, :].rearrange("b p d -> p b d")).then_inc(x_in, 16)

            def load_c(g):
                src = ctx_in[bass.ds(g * GB, GB), :, :]
                sp.dma_start(cin[:, :, 0:DC], src.rearrange("b p d -> p b d")).then_inc(c_in, 16)
                sp.dma_start(cin[:, :, DC:2 * P], src[:, :, P:DC].rearrange("b p d -> p b d")).then_inc(c_in, 16)

            load_c(0)
            load_x(0)
            sp.wait_ge(w_ready, 4)
            sp.dma_start(stage[:, 0, :].rearrange("p (k h) -> p k h", k=KD), W1[0].rearrange("(k p) h -> p k h", p=P)).then_inc(first_in, 16)
            sp.dma_start(stage[:, 1, :].rearrange("p (k d) -> p k d", k=KH), W2[0].rearrange("(k p) d -> p k d", p=P)).then_inc(first_in, 16)
            sp.dma_start(routed_in[E * REGION:E * REGION + P, :], zeros[:, :]).then_inc(padded, 16)
            with sp.Fori(1, NG) as g:
                row = sp.snap(g * (GB * P) - GB * P)
                sp.wait_ge(cT_hi_ready, 2 * g)
                load_c(g)
                sp.wait_ge(x_used, g)
                load_x(g)
                sp.wait_ge(x2_ready, GB * g)
                sp.dma_start(x2_dram[bass.ds(row, GT), :].rearrange("(b p) d -> p b d", p=P), x2[:, :, :]).then_inc(x2_stored, 16)
                sp.wait_ge(z_ready, g)
                sp.dma_start(z_dram[bass.ds(row, GT), :].rearrange("(b p) d -> p b d", p=P), z[:, :, :]).then_inc(z_stored, 16)
            sp.wait_ge(x2_ready, GB * NG)
            last = (NG - 1) * GT
            sp.dma_start(x2_dram[last:last + GT, :].rearrange("(b p) d -> p b d", p=P), x2[:, :, :]).then_inc(x2_stored, 16)
            sp.wait_ge(z_ready, NG)
            sp.dma_start(z_dram[last:last + GT, :].rearrange("(b p) d -> p b d", p=P), z[:, :, :]).then_inc(z_stored, 16)
            pad(sp, 0, E // 2)
            sp.wait_ge(x2_stored, 16 * NG)
            sp.wait_ge(z_stored, 16 * NG)
            sp.wait_ge(padded, 16 * (E + 1))
            sp.wait_ge(first_in, 32)

        @block.gpsimd
        def _(pool):
            pool.memset(ident[:, :], 0.0).then_inc(const_step, 1)
            pool.memset(before[:, :], 1.0).then_inc(const_step, 1)
            pool.memset(cells[:, :, :], 0.0).then_inc(const_ready, 1)
            pool.memset(zeros[:, :], 0.0).then_inc(const_ready, 1)
            pool.iota(slot_no[:, :], [[1, SLOTS]], base=0, channel_multiplier=0,
                      allow_small_or_imprecise_dtypes=True).then_inc(const_ready, 1)
            pool.memset(ones_b[:, :], 1.0).then_inc(const_ready, 1)
            pool.iota(expert_no[:, :], [[1, E]], base=0, channel_multiplier=0,
                      allow_small_or_imprecise_dtypes=True).then_inc(const_ready, 1)
            pool.iota(region_at[:, :], [[REGION, E]], base=0, channel_multiplier=0,
                      allow_small_or_imprecise_dtypes=True).then_inc(const_ready, 1)
            pool.memset(chosen_sum[:, :], 0.0).then_inc(const_ready, 1)
            pool.wait_ge(const_step, 2)
            pool.affine_select(out=ident[:, :], in_=ident[:, :], compare_op=ALU.not_equal, fill=1.0,
                               base=0, pattern=[[-1, P]], channel_multiplier=1).then_inc(const_ready, 1)
            pool.affine_select(out=before[:, :], in_=before[:, :], compare_op=ALU.is_gt, fill=0.0,
                               base=0, pattern=[[1, P]], channel_multiplier=-1).then_inc(const_ready, 1)
            pool.wait_ge(small_in, 16 * 3)
            pool.wait_ge(const_ready, 9)

            def group(g):
                pool.wait_ge(norm1_ready, g + 1)
                if not is_first(g):
                    pool.wait_ge(xT_hi_ready, g * 2)
                    carry(pool, cells[:, 0, :])
                for b in range(GB):
                    last = pool.tensor_scalar(xn[:, b, :], xin[:, b, :], rstd1[:, b:b + 1], shift1[:, b:b + 1], ALU.mult, ALU.add)
                last.then_inc(xn_ready, 1)

            def residual(g):
                if not is_first(g):
                    pool.wait_ge(x2_ready, GB * g)
                pool.tensor_tensor(x_bo[:, :, :], xin[:, :, :], bo_all[:, :].unsqueeze(1).to_broadcast([P, GB, D]),
                                   ALU.add).then_inc(x_used, 1)

            def normalise_out(g):
                pool.wait_ge(norm2_ready, g)
                if not (isinstance(g, int) and g == 1):
                    pool.wait_ge(z_stored, 16 * g - 16)
                    pool.wait_ge(scattered, (16 * 2 * GB) * g - 16 * 2 * GB)
                    carry(pool, cells[:, 1, :])
                for b in range(GB):
                    last = pool.tensor_scalar(z[:, b, :], x2[:, b, :], rstd2[:, b:b + 1], shift2[:, b:b + 1], ALU.mult, ALU.add)
                last.then_inc(z_ready, 1)

            def scatter(g, picks):
                if picks[0] == (0, 0):
                    pool.wait_ge(places_ready, g)
                    carry(pool, cells[:, 2, :])
                for b, k in picks:
                    pool.indirect_dma_start(
                        out=routed_in, out_offset=bass.IndirectOffsetOnAxis(ap=places[:, b, k:k + 1], axis=0),
                        in_=z[:, b, :], in_offset=None).then_inc(scattered, 16)

            def steps(g, ms):
                for m in ms:
                    for a in range(2):
                        pool.wait_ge(rec_ready, g * (2 * NM) + 2 * m + a + 1)
                        pool.tensor_tensor(probs[:, m % 2, a, :, :], probs[:, m % 2, a, :, :],
                                           row_rec[:, a, :].unsqueeze(2).to_broadcast([P, GB, P]), ALU.mult).then_inc(p_ready, 1)
                    if m in SCATTER_STEPS and not is_first(g):
                        scatter(g, SCATTER_STEPS[m])

            def turn(g):
                steps(g - 1 if isinstance(g, int) else pool.snap(g - 1), LATE)
                group(g)
                normalise_out(g)
                residual(g)
                steps(g, EARLY)

            group(0)
            residual(0)
            steps(0, EARLY)
            turn(1)
            with pool.Fori(2, NG) as g:
                turn(g)
            steps(NG - 1, LATE)
            normalise_out(NG)
            scatter(NG, [(b, k) for b in range(GB) for k in range(2)])
            pool.wait_ge(scattered, 16 * 2 * GB * NG)

        @block.scalar
        def _(act):
            def halves(n):
                return stage[:, n % 2, 0:INNER], stage[:, n % 2, INNER:2 * INNER]

            act.dma_start(stage[:, 0, 0:INNER], Wv[0:P, :]).then_inc(w_in[0], 16)
            act.dma_start(stage[0:DH, 0, INNER:], Wv[P:DC, :]).then_inc(w_in[0], 16)
            act.dma_start(stage[DH:P, 0, INNER:], Wv[P:DC, :]).then_inc(w_in[0], 16)
            act.dma_start(stage[:, 1, 0:INNER], Wk[0:P, :]).then_inc(w_in[1], 16)
            act.dma_start(stage[0:DH, 1, INNER:], Wk[P:DC, :]).then_inc(w_in[1], 16)
            act.dma_start(stage[DH:P, 1, INNER:], Wk[P:DC, :]).then_inc(w_in[1], 16)
            act.dma_start(bo_all[:, :], bo.rearrange("(a n) -> a n", a=1).to_broadcast([P, D])).then_inc(small_in, 16)
            act.dma_start(bg_all[:, :], bg.rearrange("(a n) -> a n", a=1).to_broadcast([P, E])).then_inc(small_in, 16)
            act.dma_start(wg[:, :, :], Wg.rearrange("(k p) e -> p k e", p=P)).then_inc(small_in, 16)
            for n, (hi, end) in enumerate(((wv_hi, wv_end), (wk_hi, wk_end))):
                act.wait_ge(w_in[n], 48)
                nc.scalar.activation(hi[:, :], halves(n)[0], ACT.Copy).then_inc(w_hi, 1)
                nc.scalar.activation(end[:, :], halves(n)[1], ACT.Copy).then_inc(w_hi, 1)
            act.wait_ge(w_ready, 1)
            act.dma_start(stage[:, 0, :].rearrange("p (k n) -> p k n", k=KD), Wq.rearrange("(k p) n -> p k n", p=P)).then_inc(w_in[2], 16)
            act.wait_ge(w_ready, 2)
            act.dma_start(stage[:, 1, :].rearrange("p (k n) -> p k n", k=NM), Wo.rearrange("(k p) n -> p k n", p=P)).then_inc(w_in[3], 16)
            act.wait_ge(w_in[2], 16)
            nc.scalar.activation(wq_hi[:, :, :].rearrange("p k n -> p (k n)"), stage[:, 0, :], ACT.Copy).then_inc(w_hi, 1)
            act.wait_ge(w_in[3], 16)
            nc.scalar.activation(wo_hi[:, :, :].rearrange("p k n -> p (k n)"), stage[:, 1, :], ACT.Copy).then_inc(w_hi, 1)

            def queries_keys(g, m):
                if not (is_first(g) and m < 2):
                    act.wait_ge(s_full, g * NM + m - 1)
                b = filled(act, f"q{m}", g)
                nc.scalar.activation(qT[:, m % 2, :], pair[:, b, :], ACT.Copy, scale=DH ** -0.5).then_inc(free[b], 1)
                b = filled(act, f"k{m}", g)
                nc.scalar.activation(kT[:, m % 2, :], pair[:, b, :], ACT.Copy).then_inc(free[b], 1)

            def group(g):
                for j in range(2 * GB):
                    if j == X_AT:
                        tokens_hi(g)
                    b = filled(act, f"v{j}", g)
                    nc.scalar.activation(v[:, j // 2, 512 * (j % 2):512 * (j % 2) + 512], pair[:, b, :], ACT.Copy).then_inc(free[b], 1)
                queries_keys(g, 0)
                queries_keys(g, 1)

            def inputs_hi(g):
                for k, hi in enumerate((cT_hi, cT_end_hi)):
                    act.wait_ge(c_full, 2 * g + k + 1)
                    nc.scalar.activation(hi[:, :], t_flat[:, k, :], ACT.Copy).then_inc(cT_hi_ready, 1)

            def tokens_hi(g):
                for k in range(KD):
                    act.wait_ge(x_full, KD * g + k + 1)
                    nc.scalar.activation(xT_hi[:, k, :], t_flat[:, k, :], ACT.Copy).then_inc(xT_hi_ready, 1)

            def steps(g, ms):
                gate = not is_first(g)
                for m in ms:
                    if gate and m == Z_STEP:
                        routed_tokens_out(g)
                    if m >= 2:
                        outputs_hi(g, m - 2)
                    exponentials(g, m, 0)
                    if m >= 1:
                        probs_out(g, m - 1)
                    exponentials(g, m, 1)
                    if m < NM - 2:
                        queries_keys(g, m + 2)
                    if gate and m == LOGITS_STEP + 1:
                        routing_odds(g)

            def exponentials(g, m, a):
                act.wait_ge(shifted, g * (2 * NM) + 2 * m + a + 1)
                nc.scalar.activation(probs[:, m % 2, a, :, :], probs[:, m % 2, a, :, :], ACT.Exp).then_inc(expd, 1)

            def end(g):
                outputs_hi(g, NM - 2)
                probs_out(g, NM - 1)
                outputs_hi(g, NM - 1)

            def probs_out(g, m):
                for a in range(2):
                    act.wait_ge(t_full, g * (2 * NM) + 2 * m + a + 1)
                    nc.scalar.activation(probsT[:, m % 2, a, :, :], t_ps[:, a, :, :], ACT.Copy).then_inc(pT_ready, 1)

            def outputs_hi(g, m):
                b = filled(act, f"o{m}", g)
                if m == 0 and not is_first(g):
                    act.wait_ge(x2_ready, GB * g)
                nc.scalar.activation(oT_hi[:, m, :], pair[:, b, :], ACT.Copy).then_inc(oT_hi_ready, 1)

            def routed_tokens_out(g):
                for k in range(KD):
                    b = filled(act, f"z{k}", g)
                    nc.scalar.activation(zT[:, k, :], pair[:, b, :], ACT.Copy).then_inc(free[b], 1)

            def routing_odds(g):
                act.wait_ge(gap_ready, g)
                nc.scalar.activation(odds[:, :], gap[:, :], ACT.Exp).then_inc(odds_ready, 1)

            inputs_hi(0)
            group(0)
            steps(0, EARLY)
            with act.Fori(1, NG) as g:
                last = act.snap(g - 1)
                steps(last, LATE)
                end(last)
                inputs_hi(g)
                group(g)
                steps(g, EARLY)
            steps(NG - 1, LATE)
            end(NG - 1)
            routed_tokens_out(NG)
            routing_odds(NG)
            pad(act, E // 2, E)

        @block.vector
        def _(dve):
            for n, (lo, hi, end) in enumerate(((wv_lo, wv_hi, wv_end), (wk_lo, wk_hi, wk_end))):
                dve.wait_ge(w_hi, 2 * n + 2)
                nc.vector.tensor_tensor(lo[:, :], stage[:, n, 0:INNER], hi[:, :].bitcast(F32), ALU.subtract)
                nc.vector.tensor_tensor(end[DH:P, :], stage[DH:P, n, INNER:], end[DH:P, :].bitcast(F32), ALU.subtract).then_inc(w_ready, 1)

            def late_weights():
                dve.wait_ge(w_hi, 5)
                nc.vector.tensor_tensor(wq_lo[:, :, :].rearrange("p k n -> p (k n)"), stage[:, 0, :],
                                        wq_hi[:, :, :].rearrange("p k n -> p (k n)").bitcast(F32), ALU.subtract).then_inc(w_ready, 1)
                dve.wait_ge(w_hi, 6)
                nc.vector.tensor_tensor(wo_lo[:, :, :].rearrange("p k n -> p (k n)"), stage[:, 1, :],
                                        wo_hi[:, :, :].rearrange("p k n -> p (k n)").bitcast(F32), ALU.subtract).then_inc(w_ready, 1)

            def statistics(link, src):
                for b in range(GB):
                    i = nc.vector.bn_stats(stats[:, b, :], src[:, b, :])
                link(i)
                carry(nc.vector, cells[:, 3, :])
                for b in range(GB):
                    i = nc.vector.bn_aggr(mv[:, b, :], stats[:, b, :])
                link(i)

            def norm1(g, link):
                dve.wait_ge(x_in, g * 16 + 16)
                if not is_first(g):
                    dve.wait_ge(xn_ready, g)
                statistics(link, xin)
                rsqrt_and_shift(nc, link, mv, tmp, rstd1[:, :], shift1[:, :]).then_inc(norm1_ready, 1)

            def norm2(g, link):
                dve.wait_ge(x2_ready, GB * g)
                if not (isinstance(g, int) and g == 1):
                    dve.wait_ge(z_ready, g - 1)
                statistics(link, x2)
                rsqrt_and_shift(nc, link, mv, tmp, rstd2[:, :], shift2[:, :]).then_inc(norm2_ready, 1)

            def outputs_lo(g, m):
                b = pair_bank(f"o{m}", g)[0]
                dve.wait_ge(oT_hi_ready, g * NM + m + 1)
                i = nc.vector.tensor_tensor(oT_lo[:, m, :], pair[:, b, :], oT_hi[:, m, :].bitcast(F32), ALU.subtract)
                i.then_inc(free[b], 1)

            def inputs_lo(g):
                for k, (lo, hi, rows) in enumerate(((cT_lo, cT_hi, P), (cT_end_lo, cT_end_hi, DH))):
                    dve.wait_ge(cT_hi_ready, 2 * g + k + 1)
                    nc.vector.tensor_tensor(lo[0:rows, :], t_flat[0:rows, k, :], hi[0:rows, :].bitcast(F32), ALU.subtract).then_inc(cT_ready, 1)

            def tokens_lo(g):
                for k in range(KD):
                    dve.wait_ge(xT_hi_ready, KD * g + k + 1)
                    nc.vector.tensor_tensor(xT_lo[:, k, :], t_flat[:, k, :], xT_hi[:, k, :].bitcast(F32), ALU.subtract).then_inc(xT_ready, 1)

            def steps(g, link, ms):
                gate = not is_first(g)
                for m in ms:
                    n = g * (2 * NM) + 2 * m
                    if gate and m == LOGITS_STEP:
                        routing_in(g, m)
                    dve.wait_ge(s_full, g * NM + m + 1)
                    if not (is_first(g) and m < 2):
                        dve.wait_ge(t_full, n - 2)
                    for a in range(2):
                        link(nc.vector.tensor_reduce(row_max[:, a, :], s_ps[:, m % 2, a, :, :], AX_X, ALU.max))
                        nc.vector.tensor_tensor(probs[:, m % 2, a, :, :], s_ps[:, m % 2, a, :, :],
                                                row_max[:, a, :].unsqueeze(2).to_broadcast([P, GB, P]), ALU.subtract).then_inc(shifted, 1)
                        if a == 0 and m >= 2:
                            outputs_lo(g, m - 2)
                    if gate and m == RANK_STEP:
                        routing_in(g, m)
                    for a in range(2):
                        dve.wait_ge(expd, n + a + 1)
                        if not (is_first(g) and m == 0):
                            dve.wait_ge(p_ready, n + a - 1)
                        link(nc.vector.tensor_reduce(row_sum[:, a, :], probs[:, m % 2, a, :, :], AX_X, ALU.add))
                        nc.vector.reciprocal(row_rec[:, a, :], row_sum[:, a, :]).then_inc(rec_ready, 1)
                    if gate:
                        routing(g, m, link)

            def end(g):
                outputs_lo(g, NM - 2)
                outputs_lo(g, NM - 1)

            def tokens_out(g):
                if not is_first(g):
                    dve.wait_ge(x2_stored, 16 * g)
                dve.wait_ge(x_used, g + 1)
                for b in range(GB):
                    dve.wait_ge(y_full, GB * g + b + 1)
                    nc.vector.tensor_tensor(x2[:, b, :], y_ps[:, b, 0:D], x_bo[:, b, :], ALU.add).then_inc(x2_ready, 1)

            def routing_in(g, m):
                for step, name, to, add in ((LOGITS_STEP, "logits", logits, bg_all), (RANK_STEP, "rank", place, region_at)):
                    if m == step:
                        b = filled(dve, name, g)
                        i = nc.vector.tensor_tensor(to[:, :, :], pair[:, b, 0:GB * E].rearrange("p (t e) -> p t e", e=E),
                                                    add[:, :].unsqueeze(1).to_broadcast([P, GB, E]), ALU.add)
                        i.then_inc(free[b], 1)

            def routing(g, m, link):
                if m == LOGITS_STEP:
                    drained(dve, "logits", g)
                    carry(nc.vector, cells[:, 4, :])
                    for t in range(GB):
                        i = nc.vector.max(best[:, t, :], logits[:, t, :])
                    link(i)
                    nc.vector.tensor_tensor(gap[:, :], best[:, :, 1], best[:, :, 0], ALU.subtract).then_inc(gap_ready, 1)
                    for t in range(GB):
                        i = nc.vector.max_index(best_at[:, t, :], best[:, t, :], logits[:, t, :])
                    link(i)
                    link(nc.vector.tensor_copy(best_f[:, :, :], best_at[:, :, 0:2]))
                    link(nc.vector.tensor_tensor(picks[:, :, :, :], expert_no[:, :].unsqueeze(1).unsqueeze(1).to_broadcast([P, GB, 2, E]),
                                                 best_f[:, :, :].unsqueeze(3).to_broadcast([P, GB, 2, E]), ALU.is_equal))
                    link(nc.vector.tensor_tensor(chosen[:, :, :], picks[:, :, 0, :], picks[:, :, 1, :], ALU.add))
                    link(nc.vector.tensor_copy(sums[:, 0, :], chosen_sum[:, :]))
                    for t in range(1, GB):
                        link(nc.vector.tensor_tensor(sums[:, t, :], sums[:, t - 1, :], chosen[:, t - 1, :], ALU.add))
                    i = nc.vector.tensor_tensor(chosen_sum[:, :], sums[:, GB - 1, :], chosen[:, GB - 1, :], ALU.add)
                    i.then_inc(chosen_ready, 1)
                if m == RANK_STEP:
                    drained(dve, "rank", g)
                    link(nc.vector.tensor_tensor(place2[:, :, :, :], picks[:, :, :, :],
                                                 place[:, :, :].unsqueeze(2).to_broadcast([P, GB, 2, E]), ALU.mult))
                    link(nc.vector.tensor_reduce(place_f[:, :, :], place2[:, :, :, :], AX_X, ALU.add))
                    if not (isinstance(g, int) and g == 1):
                        dve.wait_ge(scattered, (16 * 2 * GB) * g - 16 * 2 * GB)
                    i = nc.vector.tensor_copy(places[:, :, :], place_f[:, :, :])
                    i.then_inc(places_ready, 1)
                    nc.vector.tensor_copy(places_all[:, bass.ds(g - 1, 1), :, :].rearrange("p g t k -> p (g t) k"), place_f[:, :, :])
                    dve.wait_ge(odds_ready, g)
                    link(nc.vector.tensor_scalar(gap[:, :], odds[:, :], 1.0, None, ALU.add))
                    link(nc.vector.reciprocal(p_best[:, :, 0], gap[:, :]))
                    link(nc.vector.tensor_tensor(p_best[:, :, 1], p_best[:, :, 0], odds[:, :], ALU.mult))
                    link(nc.vector.tensor_copy(weights_all[:, bass.ds(g - 1, 1), :, :].rearrange("p g t k -> p (g t) k"), p_best[:, :, :]))

            def turn(g, last, link):
                steps(last, link, LATE)
                end(last)
                inputs_lo(g)
                norm1(g, link)
                tokens_out(last)
                tokens_lo(g)
                norm2(g, link)
                steps(g, link, EARLY)

            link = Links(dve, chain)
            dve.wait_ge(const_ready, 9)
            norm1(0, link)
            inputs_lo(0)
            tokens_lo(0)
            late_weights()
            steps(0, link, EARLY)
            turn(1, 0, link)
            first_links = link.n
            with dve.Fori(2, NG) as g:
                link = Links(dve, chain, g * LINKS_PER_GROUP + (first_links - 2 * LINKS_PER_GROUP))
                turn(g, dve.snap(g - 1), link)
                assert link.n == LINKS_PER_GROUP, link.n
            link = Links(dve, chain, first_links + (NG - 2) * LINKS_PER_GROUP)
            steps(NG - 1, link, LATE)
            end(NG - 1)
            tokens_out(NG - 1)
            norm2(NG, link)
            for m in (LOGITS_STEP, RANK_STEP):
                routing_in(NG, m)
                routing(NG, m, link)

            dve.wait_ge(counted, 1)
            link(nc.vector.tensor_copy(counts[:, :], n_ps))
            nc.vector.tensor_tensor(tables.pad_row[:, :], counts[:, :], region_at[:, :], ALU.add).then_inc(pads_ready, 1)
            link(nc.vector.tensor_scalar(tiles_i[:, :], counts[:, :], float(P - 1), None, ALU.add))
            link(nc.vector.tensor_scalar(tiles_i[:, :], tiles_i[:, :], TILE_BITS, None, ALU.logical_shift_right))
            link(nc.vector.tensor_copy(tiles[:, :], tiles_i[:, :]))
            link(nc.vector.tensor_copy(ends[:, 0:1], tiles[:, 0:1]))
            for e in range(1, E):
                link(nc.vector.tensor_tensor(ends[:, e:e + 1], ends[:, e - 1:e], tiles[:, e:e + 1], ALU.add))
            nc.vector.tensor_scalar(tables.end_slot[:, :], ends[:, :], 1.0, None, ALU.add)
            link(nc.vector.tensor_tensor(tables.move[:, :], ends[:, :], tiles[:, :], ALU.subtract))
            link(nc.vector.scalar_tensor_tensor(out=tables.move[:, :], in0=tables.move[:, :], scalar=float(P), in1=region_at[:, :],
                                                op0=ALU.mult, op1=ALU.subtract))
            link(nc.vector.tensor_tensor(passed[:, :, :], slot_no[:, :].unsqueeze(2).to_broadcast([P, SLOTS, E]),
                                         ends[:, :].unsqueeze(1).to_broadcast([P, SLOTS, E]), ALU.is_ge))
            nc.vector.tensor_reduce(slot_expert[:, :], passed[:, :, :], AX_X, ALU.add)
            link(nc.vector.tensor_tensor(passed_tiles[:, :, :], passed[:, :, :],
                                         tiles[:, :].unsqueeze(1).to_broadcast([P, SLOTS, E]), ALU.mult))
            link(nc.vector.tensor_reduce(tile_no[:, :], passed_tiles[:, :, :], AX_X, ALU.add))
            link(nc.vector.tensor_tensor(tile_no[:, :], slot_no[:, :], tile_no[:, :], ALU.subtract))
            link(nc.vector.tensor_scalar(tile_no[:, :], tile_no[:, :], float(P), None, ALU.mult))
            link(nc.vector.scalar_tensor_tensor(out=tile_no[:, :], in0=slot_expert[:, :], scalar=float(REGION),
                                                in1=tile_no[:, :], op0=ALU.mult, op1=ALU.add))
            nc.vector.tensor_scalar(tables.x_row[:, :], tile_no[:, :], float(E * REGION), None, ALU.min)
            link(nc.vector.tensor_scalar(owner[:, :], slot_expert[:, :], float(E - 1), None, ALU.min))
            nc.vector.tensor_scalar(tables.need[:, :], owner[:, :], 1.0, None, ALU.add)
            link(nc.vector.tensor_scalar(half[:, :], owner[:, :], RING - 1, None, ALU.bitwise_and))
            nc.vector.tensor_scalar(tables.w_at[:, :], half[:, :], float(WIDE), None, ALU.mult)
            nc.vector.tensor_scalar(tables.b1_at[:, :], half[:, :], float(H), None, ALU.mult)
            link(nc.vector.tensor_scalar(tables.b2_at[:, :], half[:, :], float(D), None, ALU.mult))

        @block.tensor
        def _(pe):
            mm, tr = nc.tensor.matmul, nc.tensor.transpose

            def three(out, a_hi, a_lo, b_hi, b_lo, start, stop):
                mm(out, a_hi, b_hi, start=start, stop=False)
                mm(out, a_hi, b_lo, start=False, stop=False)
                return mm(out, a_lo, b_hi, start=False, stop=stop)

            def project_queries_keys(g, m):
                cols = slice(m * P, m * P + P)
                b = take(pe, f"q{m}", g)
                if m == 0:
                    pe.wait_ge(xT_ready, KD * g + KD)
                for k in range(KD):
                    i = three(pair[:, b, :], wq_hi[:, k, cols], wq_lo[:, k, cols], xT_hi[:, k, :], xT_lo[:, k, :], k == 0, k == KD - 1)
                i.then_inc(full[b], 1)
                b = take(pe, f"k{m}", g)
                three(pair[:, b, :], wk_hi[:, cols], wk_lo[:, cols], cT_hi[:, :], cT_lo[:, :], True, False)
                mm(pair[:, b, :], wk_end[:, cols], cT_end_hi[:, :], start=False, stop=False)
                i = mm(pair[:, b, :], wk_end[0:DH, cols], cT_end_lo[0:DH, :], start=False, stop=True)
                i.then_inc(full[b], 1)

            def scores(g, m):
                n = g * NM + m
                drained(pe, f"q{m}", g)
                drained(pe, f"k{m}", g)
                if not (is_first(g) and m < 2):
                    pe.wait_ge(shifted, 2 * n - 2)
                if m < 2 and not is_first(g):
                    pe.wait_ge(x2_ready, GB * g - GB + 2 * m + 2)
                for b in range(GB):
                    for a in range(2):
                        rows, cols = slice(DH * a, DH * a + DH), slice(b * P, b * P + P)
                        i = mm(s_ps[:, m % 2, a, b, :], qT[rows, m % 2, cols], kT[rows, m % 2, cols], start=True, stop=True)
                i.then_inc(s_full, 1)

            def transpose_probs(g, m):
                n = g * (2 * NM) + 2 * m
                for a in range(2):
                    pe.wait_ge(p_ready, n + a + 1)
                    if not (is_first(g) and m == 0):
                        pe.wait_ge(pT_ready, n + a - 1)
                    for b in range(GB):
                        i = tr(t_ps[:, a, b, :], probs[:, m % 2, a, b, :], ident[:, :])
                    i.then_inc(t_full, 1)

            def weigh_values(g, m):
                pe.wait_ge(pT_ready, g * (2 * NM) + 2 * m + 2)
                bank = take(pe, f"o{m}", g)
                for b in range(GB):
                    for a in range(2):
                        cols = slice((2 * m + a) * DH, (2 * m + a + 1) * DH)
                        i = mm(pair[DH * a:DH * a + DH, bank, b * P:b * P + P], v[:, b, cols], probsT[:, m % 2, a, b, :],
                               start=True, stop=True)
                i.then_inc(full[bank], 1)

            def project_out(g, t, ms):
                rows = slice(t * P, t * P + P)
                if 0 in ms:
                    pe.wait_ge(shifted, g * (2 * NM) + (2 * NM - 2 if t < 2 else 2 * NM))
                for m in ms:
                    if t == 0 and m >= NM - 4:
                        drained(pe, f"o{m}", g)
                    i = three(y_ps[:, t, 0:D], oT_hi[:, m, rows], oT_lo[:, m, rows], wo_hi[:, m, :], wo_lo[:, m, :],
                              m == 0, m == NM - 1)
                if NM - 1 in ms:
                    i.then_inc(y_full, 1)

            def transpose_context(g):
                pe.wait_ge(c_in, g * 32 + 32)
                for k in range(2):
                    for t in range(GB):
                        i = tr(t_ps[:, k, t, :], cin[:, t, k * P:k * P + P], ident[:, :])
                    i.then_inc(c_full, 1)

            def transpose_tokens(g):
                pe.wait_ge(xn_ready, g + 1)
                for k in range(KD):
                    for t in range(GB):
                        i = tr(t_ps[:, k, t, :], xn[:, t, k * P:k * P + P], ident[:, :])
                    i.then_inc(x_full, 1)

            def group(g):
                pe.wait_ge(cT_ready, 2 * g + 2)
                for j in range(2 * GB):
                    if j == X_AT:
                        transpose_tokens(g)
                    b = take(pe, f"v{j}", g)
                    t, cols = slice(j // 2 * P, j // 2 * P + P), slice(j % 2 * 512, j % 2 * 512 + 512)
                    three(pair[:, b, :], cT_hi[:, t], cT_lo[:, t], wv_hi[:, cols], wv_lo[:, cols], True, False)
                    mm(pair[:, b, :], cT_end_hi[:, t], wv_end[:, cols], start=False, stop=False)
                    mm(pair[:, b, :], cT_end_lo[0:DH, t], wv_end[0:DH, cols], start=False, stop=True).then_inc(full[b], 1)
                if is_first(g):
                    pe.wait_ge(w_ready, 3)
                project_queries_keys(g, 0)
                drained(pe, f"v{2 * GB - 2}", g)
                drained(pe, f"v{2 * GB - 1}", g)
                project_queries_keys(g, 1)

            def steps(g, ms):
                for m in ms:
                    gate = not is_first(g) and m in EARLY
                    if gate and m == LOGITS_STEP:
                        routing(g, m)
                    scores(g, m)
                    if m >= 2:
                        weigh_values(g, m - 2)
                    if gate and m == Z_STEP:
                        routing(g, m)
                    if 1 <= m < NM - 1:
                        transpose_probs(g, m - 1)
                    if gate and m == RANK_STEP:
                        routing(g, m)
                    if m < NM - 2:
                        project_queries_keys(g, m + 2)

            def end(g, following=None):
                most = range(NM - 3)
                project_out(g, 0, most)
                project_out(g, 1, most)
                transpose_probs(g, NM - 2)
                project_out(g, 2, most)
                weigh_values(g, NM - 2)
                project_out(g, 3, most)
                for t in range(2):
                    project_out(g, t, [NM - 3])
                transpose_probs(g, NM - 1)
                for t in range(2, GB):
                    project_out(g, t, [NM - 3])
                weigh_values(g, NM - 1)
                if following is not None:
                    transpose_context(following)
                for t in range(GB):
                    project_out(g, t, [NM - 2])
                for t in range(GB):
                    project_out(g, t, [NM - 1])

            def routing(g, m):
                if m == Z_STEP:
                    pe.wait_ge(z_ready, g)
                    for k in range(KD):
                        b = take(pe, f"z{k}", g)
                        for t in range(GB):
                            i = tr(pair[:, b, t * P:t * P + P], z[:, t, k * P:k * P + P], ident[:, :])
                        i.then_inc(full[b], 1)
                if m == LOGITS_STEP:
                    b = take(pe, "logits", g)
                    drained(pe, "z0", g, b)
                    drained(pe, "z1", g, b)
                    for t in range(GB):
                        for k in range(KD):
                            i = mm(pair[:, b, t * E:t * E + E], zT[:, k, t * P:t * P + P], wg[:, k, :], start=(k == 0), stop=(k == KD - 1))
                    i.then_inc(full[b], 1)
                if m == RANK_STEP:
                    pe.wait_ge(chosen_ready, g)
                    b = take(pe, "rank", g)
                    for t in range(GB):
                        mm(pair[:, b, t * E:t * E + E], before[:, :], chosen[:, t, :], start=True, stop=False)
                        i = mm(pair[:, b, t * E:t * E + E], ones_b[:, :], sums[:, t, :], start=False, stop=True)
                    i.then_inc(full[b], 1)

            pe.wait_ge(const_ready, 9)
            pe.wait_ge(small_in, 48)
            transpose_context(0)
            pe.wait_ge(w_ready, 2)
            group(0)
            steps(0, EARLY)
            pe.wait_ge(w_ready, 4)
            with pe.Fori(1, NG) as g:
                last = pe.snap(g - 1)
                steps(last, LATE)
                end(last, g)
                group(g)
                steps(g, EARLY)
            steps(NG - 1, LATE)
            end(NG - 1)
            routing(NG, Z_STEP)
            routing(NG, LOGITS_STEP)
            routing(NG, RANK_STEP)
            pe.wait_ge(x2_ready, GB * NG)
            mm(n_ps, ones_b[:, :], chosen_sum[:, :], start=True, stop=True).then_inc(counted, 1)


LINKS_PER_GROUP = 75


def experts(nc, W1, b1, W2, b2, routed_in, routed_out, ident, places_all, cells, stage, tables,
            x2_dram, z_dram, gamma, beta, z_all, x2_all, gamma_all):
    with ExitStack() as ctx:
        def sb(name, shape, dt=F32):
            return ctx.enter_context(nc.sbuf_tensor(name, shape, dt))

        def psum(name, shape):
            return ctx.enter_context(nc.psum_tensor(name, shape, F32))

        def sem(name):
            return ctx.enter_context(nc.semaphore(name))

        w1_hi, w1_lo = sb("w1_hi", [P, RING * WIDE], F32R), sb("w1_lo", [P, RING * WIDE], F32R)
        w2_hi, w2_lo = sb("w2_hi", [P, RING * WIDE], F32R), sb("w2_lo", [P, RING * WIDE], F32R)
        w1_stage, w2_stage = sb("w1_stage", [P, WIDE]), sb("w2_stage", [P, WIDE])
        b1_all, b2_all = sb("b1_all", [P, RING * H]), sb("b2_all", [P, RING * D])
        beta_all = sb("beta_all", [P, D])
        regions, move_step = sb("regions", [P, E]), sb("move_step", [P, E])
        place_in, moved, beyond = sb("place_in", [P, 2 * B]), sb("moved", [P, 2 * B]), sb("beyond", [P, 2 * B, E])

        tile = sb("tile", [P, 2, D])
        rT_hi, rT_lo = sb("rT_hi", [P, KD, P], F32R), sb("rT_lo", [P, KD, P], F32R)
        hid = sb("hid", [P, H])
        hT_hi, hT_lo = sb("hT_hi", [P, KH, P], F32R), sb("hT_lo", [P, KH, P], F32R)
        y = sb("y", [P, 2, D])

        h_ps, ht_ps = psum("h_ps", [P, 2, 512]), psum("ht_ps", [P, 2, 4, P])
        rt_ps, yo_ps = psum("rt_ps", [P, 4, P]), psum("yo_ps", [P, 512])

        rows_in, params_in, sums_ready = sem("rows_in"), sem("params_in"), sem("sums_ready")
        regions_ready, chain, first_hi = sem("regions_ready"), sem("place_chain"), sem("first_hi")
        w1_in, w2_in, b_in, w_hi_done = sem("w1_in"), sem("w2_in"), sem("b_in"), sem("w_hi_done")
        w1_ready, weights_ready = sem("w1_ready"), sem("weights_ready")
        tile_in = [sem("tile0_in"), sem("tile1_in")]
        rt_full, rT_hi_ready, rT_ready = sem("rt_full"), sem("rT_hi_ready"), sem("rT_ready")
        h_full, h_biased, h_ready = sem("h_full"), sem("h_biased"), sem("h_ready")
        ht_full, hT_hi_ready, hT_ready = sem("ht_full"), sem("hT_hi_ready"), sem("hT_ready")
        yo_full, y_ready = sem("yo_full"), sem("y_ready")
        y_stored = [sem("y0_stored"), sem("y1_stored")]

        block = ctx.enter_context(nc.Block())

        def from_table(eng, table, s, top, least=0):
            return eng.value_load(table[0:1, bass.ds(s, 1)], min_val=least, max_val=top)

        @block.sync
        def _(sp):
            for s in range(2):
                row = from_table(sp, tables.x_row, s, E * REGION)
                sp.dma_start(tile[:, s, :], routed_in[bass.ds(row, P), :]).then_inc(tile_in[s], 16)

            def load(s, j):
                row = from_table(sp, tables.x_row, sp.snap(s + 2), E * REGION)
                sp.wait_ge(rt_full, s + 1)
                sp.dma_start(tile[:, j, :], routed_in[bass.ds(row, P), :]).then_inc(tile_in[j], 16)

            def store(s, j):
                row = s * P if isinstance(s, int) else sp.snap(s * P)
                sp.wait_ge(y_ready, s + 2)
                sp.dma_start(routed_out[bass.ds(row, P), :], y[:, j, :]).then_inc(y_stored[j], 16)

            load(0, 0)
            load(1, 1)
            with sp.Fori(0, SLOTS // 2 - 2) as i:
                for j in range(2):
                    s = sp.snap(i * 2 + j)
                    load(sp.snap(s + 2), j)
                    store(s, j)
            for s in range(SLOTS - 4, SLOTS):
                store(s, s % 2)
            sp.wait_ge(y_stored[0], 16 * (SLOTS // 2))
            sp.wait_ge(y_stored[1], 16 * (SLOTS // 2))

        @block.gpsimd
        def _(pool):
            def load_weights(e):
                one = bass.ds(e, 1)
                pool.dma_start(w1_stage[:, :].rearrange("p (k h) -> p k h", k=KD), W1[one, :, :].rearrange("a (k p) h -> p (a k) h", p=P)).then_inc(w1_in, 16)
                pool.dma_start(w2_stage[:, :].rearrange("p (k d) -> p k d", k=KH), W2[one, :, :].rearrange("a (k p) d -> p (a k) d", p=P)).then_inc(w2_in, 16)

            def load_biases(e, r):
                one = bass.ds(e, 1)
                pool.dma_start(b1_all[:, r * H:r * H + H], b1[one, :].to_broadcast([P, H])).then_inc(b_in, 16)
                pool.dma_start(b2_all[:, r * D:r * D + D], b2[one, :].to_broadcast([P, D])).then_inc(b_in, 16)

            load_biases(0, 0)
            pool.iota(regions[:, :], [[REGION, E]], base=0, channel_multiplier=0,
                      allow_small_or_imprecise_dtypes=True).then_inc(regions_ready, 1)
            pool.wait_ge(tile_in[0], 16)
            pool.wait_ge(tile_in[1], 16)
            pool.wait_ge(b_in, 32)
            load_weights(1)
            load_biases(1, 1)

            def split(e, r):
                at = slice(r * WIDE, r * WIDE + WIDE)
                for n, (hi, lo, stage, came, ready) in enumerate(((w1_hi, w1_lo, w1_stage, w1_in, w1_ready),
                                                                  (w2_hi, w2_lo, w2_stage, w2_in, weights_ready))):
                    pool.wait_ge(came, 16 * e)
                    carry(pool, cells[:, 5 + n, :])
                    pool.tensor_scalar(hi[:, at], stage[:, :], 1.0, 0.0, ALU.mult, ALU.add).then_inc(w_hi_done, 1)
                    pool.wait_ge(b_in, 32 * e + 32)
                    if isinstance(e, int) and e == 1 and n:
                        pool.wait_ge(ready, 1)
                    pool.wait_ge(w_hi_done, 2 * e - 1 + n)
                    pool.tensor_tensor(lo[:, at], stage[:, :], hi[:, at].bitcast(F32), ALU.subtract).then_inc(ready, 1)

            def weights(e, r, more):
                done = from_table(pool, tables.end_slot, pool.snap(e - RING) if not isinstance(e, int) else e - RING, SLOTS + 1, 1)
                pool.wait_ge(y_ready, done)
                carry(pool, cells[:, 7, :])
                load_biases(e, r)
                split(e, r)
                if more:
                    after(e)

            def after(e):
                pool.wait_ge(weights_ready, e + 1)
                load_weights(e + 1 if isinstance(e, int) else pool.snap(e + 1))

            split(1, 1)
            after(1)
            with pool.Fori(1, E // 2 - 1) as i:
                weights(pool.snap(i * 2), 0, True)
                weights(pool.snap(i * 2 + 1), 1, True)
            weights(E - 2, 0, True)
            weights(E - 1, 1, False)
            pool.dma_start(gamma_all[:, :], gamma.rearrange("(a n) -> a n", a=1).to_broadcast([P, D])).then_inc(params_in, 16)
            pool.dma_start(beta_all[:, :], beta.rearrange("(a n) -> a n", a=1).to_broadcast([P, D])).then_inc(params_in, 16)
            with pool.Fori(0, NG) as g:
                row, at = pool.snap(g * GT), pool.snap(g * GB)
                for src, to in ((z_dram, z_all), (x2_dram, x2_all)):
                    pool.dma_start(to[:, bass.ds(at, GB), :], src[bass.ds(row, GT), :].rearrange("(b p) d -> p b d", p=P)).then_inc(rows_in, 16)
            pool.wait_ge(params_in, 32)
            pool.wait_ge(rows_in, 32 * NG)
            with pool.Fori(0, NG) as g:
                some = x2_all[:, bass.ds(pool.snap(g * GB), GB), :]
                pool.tensor_tensor(some, some, beta_all[:, :].unsqueeze(1).to_broadcast([P, GB, D]), ALU.add).then_inc(sums_ready, 1)

        @block.scalar
        def _(act):
            for n, hi in enumerate((w1_hi, w2_hi)):
                nc.scalar.activation(hi[:, 0:WIDE], stage[:, n, :], ACT.Identity).then_inc(first_hi, 1)

            def high_inputs(s):
                act.wait_ge(rt_full, s + 1)
                nc.scalar.activation(rT_hi[:, :, :], rt_ps[:, 0:KD, :], ACT.Identity).then_inc(rT_hi_ready, 1)

            def high_hidden(s):
                for a in range(2):
                    act.wait_ge(ht_full, 2 * s + a + 1)
                    nc.scalar.activation(hT_hi[:, 4 * a:4 * a + 4, :], ht_ps[:, a, :, :], ACT.Identity).then_inc(hT_hi_ready, 1)

            def gelu(s):
                for a in range(2):
                    act.wait_ge(h_biased, 2 * s + a + 1)
                    nc.scalar.activation(hid[:, 512 * a:512 * a + 512], hid[:, 512 * a:512 * a + 512], ACT.Gelu).then_inc(h_ready, 1)

            high_inputs(0)
            gelu(0)
            high_inputs(1)
            high_hidden(0)
            with act.Fori(1, SLOTS - 1) as s:
                gelu(s)
                high_inputs(act.snap(s + 1))
                high_hidden(s)
            gelu(SLOTS - 1)
            high_hidden(SLOTS - 1)

        @block.vector
        def _(dve):
            link = Links(dve, chain)
            for n, (lo, hi) in enumerate(((w1_lo, w1_hi), (w2_lo, w2_hi))):
                dve.wait_ge(first_hi, n + 1)
                nc.vector.tensor_tensor(lo[:, 0:WIDE], stage[:, n, :], hi[:, 0:WIDE].bitcast(F32), ALU.subtract).then_inc((w1_ready, weights_ready)[n], 1)
            carry(nc.vector, cells[:, 10, :]).then_inc(y_ready, 1)

            def low_inputs(s):
                dve.wait_ge(rT_hi_ready, s + 1)
                nc.vector.tensor_tensor(rT_lo[:, :, :], rt_ps[:, 0:KD, :], rT_hi[:, :, :].bitcast(F32), ALU.subtract).then_inc(rT_ready, 1)

            def low_hidden(s):
                for a in range(2):
                    dve.wait_ge(hT_hi_ready, 2 * s + a + 1)
                    nc.vector.tensor_tensor(hT_lo[:, 4 * a:4 * a + 4, :], ht_ps[:, a, :, :],
                                            hT_hi[:, 4 * a:4 * a + 4, :].bitcast(F32), ALU.subtract).then_inc(hT_ready, 1)

            def bias_hidden(s):
                at = from_table(dve, tables.b1_at, s, (RING - 1) * H)
                ats = [at + 512 * a for a in range(2)]
                for a in range(2):
                    dve.wait_ge(h_full, 2 * s + a + 1)
                    nc.vector.tensor_tensor(hid[:, 512 * a:512 * a + 512], h_ps[:, a, :], b1_all[:, bass.ds(ats[a], 512)], ALU.add).then_inc(h_biased, 1)

            def outputs(s, j):
                at = from_table(dve, tables.b2_at, s, (RING - 1) * D)
                if not (isinstance(s, int) and s < 2):
                    dve.wait_ge(y_stored[j], (s // 2) * 16 if isinstance(s, int) else s * 8 - 8 * j)
                dve.wait_ge(yo_full, s + 1)
                nc.vector.tensor_tensor(y[:, j, :], yo_ps[:, 0:D], b2_all[:, bass.ds(at, D)], ALU.add).then_inc(y_ready, 1)

            def step(s, j, more=True):
                bias_hidden(s)
                if more:
                    low_inputs(s + 1 if isinstance(s, int) else dve.snap(s + 1))
                if not (isinstance(s, int) and s == 0):
                    outputs(s - 1 if isinstance(s, int) else dve.snap(s - 1), 1 - j)
                low_hidden(s)

            def places_out():
                move = tables.move
                dve.wait_ge(regions_ready, 1)
                link(nc.vector.tensor_copy(move_step[:, 0:1], move[:, 0:1]))
                link(nc.vector.tensor_tensor(move_step[:, 1:E], move[:, 1:E], move[:, 0:E - 1], ALU.subtract))
                flat = places_all[:, :, :, :].rearrange("p g t k -> p (g t k)")
                link(nc.vector.tensor_copy(place_in[:, :], flat))
                link(nc.vector.tensor_tensor(beyond[:, :, :], place_in[:, :].unsqueeze(2).to_broadcast([P, 2 * B, E]),
                                             regions[:, :].unsqueeze(1).to_broadcast([P, 2 * B, E]), ALU.is_ge))
                link(nc.vector.tensor_tensor(beyond[:, :, :], beyond[:, :, :],
                                             move_step[:, :].unsqueeze(1).to_broadcast([P, 2 * B, E]), ALU.mult))
                link(nc.vector.tensor_reduce(moved[:, :], beyond[:, :, :], AX_X, ALU.add))
                nc.vector.tensor_tensor(flat, place_in[:, :], moved[:, :], ALU.add)

            low_inputs(0)
            dve.wait_ge(b_in, 32)
            step(0, 0)
            step(1, 1)
            places_out()
            step(2, 0)
            with dve.Fori(1, SLOTS // 2 - 1) as i:
                step(dve.snap(i * 2 + 1), 1)
                step(dve.snap(i * 2 + 2), 0)
            step(SLOTS - 1, 1, False)
            outputs(SLOTS - 1, 1)

        @block.tensor
        def _(pe):
            mm, tr = nc.tensor.matmul, nc.tensor.transpose
            def three(out, a_hi, a_lo, b_hi, b_lo, start, stop):
                mm(out, a_hi, b_hi, start=start, stop=False)
                mm(out, a_hi, b_lo, start=False, stop=False)
                return mm(out, a_lo, b_hi, start=False, stop=stop)

            def transpose_inputs(s, j):
                pe.wait_ge(tile_in[j], (s // 2 + 1) * 16 if isinstance(s, int) else s * 8 + (16 - 8 * j))
                for k in range(KD):
                    i = tr(rt_ps[:, k, :], tile[:, j, k * P:k * P + P], ident[:, :])
                i.then_inc(rt_full, 1)

            def hidden_registers(s):
                needed = from_table(pe, tables.need, s, E, 1)
                at = pe.snap((needed + 1) % RING * WIDE)
                return [at + 512 * n for n in range(4)], needed

            def hidden(s, ats, needed):
                pe.wait_ge(weights_ready, needed)
                pe.wait_ge(rT_ready, s + 1)
                for a in range(2):
                    if not (isinstance(s, int) and s == 0):
                        pe.wait_ge(h_biased, 2 * s + a - 1)
                    for k in range(KD):
                        cols = bass.ds(ats[2 * k + a], 512)
                        i = three(h_ps[:, a, :], rT_hi[:, k, :], rT_lo[:, k, :], w1_hi[:, cols], w1_lo[:, cols], k == 0, k == KD - 1)
                    i.then_inc(h_full, 1)

            def transpose_hidden(s):
                for a in range(2):
                    pe.wait_ge(h_ready, 2 * s + a + 1)
                    for k in range(4):
                        i = tr(ht_ps[:, a, k, :], hid[:, (4 * a + k) * P:(4 * a + k) * P + P], ident[:, :])
                    i.then_inc(ht_full, 1)

            def output_registers(s):
                at = from_table(pe, tables.w_at, s, (RING - 1) * WIDE)
                return [at + D * k for k in range(KH)]

            def outputs(s, ats):
                if not (isinstance(s, int) and s == 0):
                    pe.wait_ge(y_ready, s + 1)
                for k in range(KH):
                    if k % 4 == 0:
                        pe.wait_ge(hT_ready, 2 * s + 1 + k // 4)
                    cols = bass.ds(ats[k], D)
                    i = three(yo_ps[:, 0:D], hT_hi[:, k, :], hT_lo[:, k, :], w2_hi[:, cols], w2_lo[:, cols], k == 0, k == KH - 1)
                i.then_inc(yo_full, 1)

            def step(s, j):
                fixed = isinstance(s, int)
                after = s + 1 if fixed else pe.snap(s + 1)
                last = s - 1 if fixed else pe.snap(s - 1)
                hidden_at = hidden_registers(after)
                transpose_inputs(after, 1 - j)
                if not (fixed and s == 0):
                    outputs(last, output_registers(last))
                transpose_hidden(s)
                hidden(after, *hidden_at)

            transpose_inputs(0, 0)
            hidden(0, *hidden_registers(0))
            step(0, 0)
            with pe.Fori(0, SLOTS // 2 - 1) as i:
                step(pe.snap(i * 2 + 1), 1)
                step(pe.snap(i * 2 + 2), 0)
            last = SLOTS - 1
            outputs(last - 1, output_registers(last - 1))
            transpose_hidden(last)
            outputs(last, output_registers(last))


def combine(nc, routed_out, places_all, weights_all, cells, z_all, x2_all, gamma_all, out):
    with ExitStack() as ctx:
        def sb(name, shape, dt=F32):
            return ctx.enter_context(nc.sbuf_tensor(name, shape, dt))

        def sem(name):
            return ctx.enter_context(nc.semaphore(name))

        rows = sb("rows", [P, 2, GB, 2], U32)
        y = sb("y_rows", [P, 2, GB, 2, D])
        stats, mv = sb("stats2", [P, 2 * GB, 6]), sb("mv2", [P, 2 * GB, 2])
        tmp = sb("tmp2", [P, 4 * GB])
        rstd, shift = sb("rstd", [P, 2 * GB]), sb("shift", [P, 2 * GB])

        chain = sem("combine_chain")
        y_in = [sem("y0_in"), sem("y1_in")]
        rows_ready, summed, went_on = sem("rows_ready"), sem("summed"), sem("went_on")
        norm_ready, normed_ready, result_ready = sem("norm_ready"), sem("normed_ready"), sem("result_ready")
        out_stored = sem("out_stored")

        block = ctx.enter_context(nc.Block())

        def group_of(eng, g):
            return bass.ds(g * GB if isinstance(g, int) else eng.snap(g * GB), GB)

        @block.sync
        def _(sp):
            with sp.Fori(0, NG) as g:
                tiles = group_of(sp, g)
                sp.wait_ge(result_ready, g + 1)
                sp.dma_start(out[tiles, :, :].rearrange("b p d -> p b d"), x2_all[:, tiles, :]).then_inc(out_stored, 16)
            sp.wait_ge(out_stored, 16 * NG)

        @block.gpsimd
        def _(pool):
            def gather(g, j):
                pool.wait_ge(rows_ready, g + 1)
                if not isinstance(g, int):
                    pool.wait_ge(summed, g - 1)
                    carry(pool, cells[:, 8 + j, :]).then_inc(went_on, 1)
                for b in range(GB):
                    for k in range(2):
                        pool.indirect_dma_start(
                            out=y[:, j, b, k, :], out_offset=None, in_=routed_out,
                            in_offset=bass.IndirectOffsetOnAxis(ap=rows[:, j, b, k:k + 1], axis=0)).then_inc(y_in[j], 16)

            gather(0, 0)
            gather(1, 1)
            with pool.Fori(1, NG // 2) as i:
                gather(pool.snap(i * 2), 0)
                gather(pool.snap(i * 2 + 1), 1)

        @block.scalar
        def _(act):
            with act.Fori(0, NG // 2) as i:
                act.wait_ge(norm_ready, i + 1)
                for b in range(2 * GB):
                    tile = z_all[:, bass.ds(act.snap(i * (2 * GB) + b), 1), :].rearrange("p b d -> p (b d)")
                    n = nc.scalar.activation(tile, tile, ACT.Identity, scale=rstd[:, b:b + 1], bias=shift[:, b:b + 1])
                    if b % GB == GB - 1:
                        n.then_inc(normed_ready, 1)

        @block.vector
        def _(dve):
            def take_rows(g, j):
                at = g if isinstance(g, int) else dve.snap(g)
                nc.vector.tensor_copy(rows[:, j, :, :], places_all[:, bass.ds(at, 1), :, :].rearrange("p g t k -> p (g t) k")).then_inc(rows_ready, 1)

            def add_up(i, j, link):
                g = 2 * i + j if isinstance(i, int) else dve.snap(i * 2 + j)
                tiles = [bass.ds(g * GB + b if isinstance(g, int) else dve.snap(g * GB + b), 1) for b in range(GB)]
                if not (isinstance(i, int) and i == 0):
                    dve.wait_ge(went_on, g - 1)
                dve.wait_ge(y_in[j], (i + 1) * (32 * GB))
                for k in range(2):
                    for b in range(GB):
                        w = weights_all[:, bass.ds(g, 1), b:b + 1, k:k + 1].rearrange("p g t k -> p (g t k)")
                        sums = z_all[:, tiles[b], :].rearrange("p b d -> p (b d)")
                        last = nc.vector.scalar_tensor_tensor(out=sums, in0=y[:, j, b, k, :], scalar=w,
                                                              in1=sums, op0=ALU.mult, op1=ALU.add)
                    link(last)
                carry(nc.vector, cells[:, 11, :])
                for b in range(GB):
                    last = nc.vector.bn_stats(stats[:, j * GB + b, :], z_all[:, tiles[b], :].rearrange("p b d -> p (b d)"))
                last.then_inc(summed, 1)

            def scale(i, link):
                if not (isinstance(i, int) and i == 0):
                    dve.wait_ge(normed_ready, 2 * i)
                dve.wait_ge(summed, 2 * i + 2)
                carry(nc.vector, cells[:, 10, :])
                for b in range(2 * GB):
                    last = nc.vector.bn_aggr(mv[:, b, :], stats[:, b, :])
                link(last)
                rsqrt_and_shift(nc, link, mv, tmp, rstd[:, :], shift[:, :]).then_inc(norm_ready, 1)

            def finish(i, j, link):
                g = 2 * i + j if isinstance(i, int) else dve.snap(i * 2 + j)
                tiles = group_of(dve, g)
                dve.wait_ge(normed_ready, g + 1)
                link(nc.vector.tensor_tensor(z_all[:, tiles, :], z_all[:, tiles, :], gamma_all[:, :].unsqueeze(1).to_broadcast([P, GB, D]), ALU.mult))
                nc.vector.tensor_tensor(x2_all[:, tiles, :], z_all[:, tiles, :], x2_all[:, tiles, :], ALU.add).then_inc(result_ready, 1)

            def pair(i, link, ahead=True):
                for j in range(2):
                    add_up(i, j, link)
                    if ahead:
                        take_rows(2 * i + 2 + j, j)
                    if not (isinstance(i, int) and i == 0):
                        finish(i - 1, j, link)
                scale(i, link)

            take_rows(0, 0)
            take_rows(1, 1)
            link = Links(dve, chain)
            pair(0, link)
            first_links = link.n
            with dve.Fori(1, NG // 2 - 1) as i:
                link = Links(dve, chain, i * PAIR_LINKS + (first_links - PAIR_LINKS))
                pair(i, link)
                assert link.n == PAIR_LINKS, link.n
            link = Links(dve, chain, first_links + (NG // 2 - 2) * PAIR_LINKS)
            pair(NG // 2 - 1, link, False)
            finish(NG // 2 - 1, 0, link)
            finish(NG // 2 - 1, 1, link)


PAIR_LINKS = 19


_INS = ["x", "ctx_768", "L0_xattn_Wq", "L0_xattn_Wk", "L0_xattn_Wv", "L0_xattn_Wo", "L0_xattn_bo", "L0_ffn_Wg",
        "L0_ffn_bg", "L0_ffn_W1", "L0_ffn_b1", "L0_ffn_W2", "L0_ffn_b2", "L0_ffn_gamma", "L0_ffn_beta"]


def kernel(**inputs):
    import numpy as _np
    import concourse.bacc as _bacc
    from concourse.bass_utils import run_bass_kernel_spmd as _run

    nc = _bacc.Bacc("TRN2", target_bir_lowering=False, num_devices=1)
    arrays, args = {}, []
    for name in _INS:
        a = _np.ascontiguousarray(inputs[name])
        arrays[f"in_{name}"] = a
        args.append(nc.dram_tensor(f"in_{name}", a.shape, mybir.dt.from_np(a.dtype), kind="ExternalInput").ap())
    args.append(nc.dram_tensor("out_0", (B, P, D), F32, kind="ExternalOutput").ap())
    build(nc, *args)
    r = _run(nc, [arrays], core_ids=[0])
    return r.results[0]["out_0"]
```
